# Optimizing a Trainium2 kernel written in Bass

```python
import numpy as np
import jax
import jax.numpy as jnp

def _softmax(x, axis=-1):
    return jax.nn.softmax(x, axis=axis)

def _gelu(x):
    return jax.nn.gelu(x, approximate=True)

def _silu(x):
    return jax.nn.silu(x)

def _sigmoid(x):
    return jax.nn.sigmoid(x)

def _layernorm(x, axis=-1, eps=1e-05):
    m = jnp.mean(x, axis=axis, keepdims=True)
    v = jnp.var(x, axis=axis, keepdims=True)
    return (x - m) / jnp.sqrt(v + eps)

def _scatter_add(tgt, idx, src, axis=0):
    return tgt.at[idx].add(src)

def _segment_sum(src, seg, n):
    return jax.ops.segment_sum(src, seg, n)
kernel_name = 'mk_decoder_preln_d2_seqx_r4_066f32'

def setup_inputs(seed: int=0):
    np.random.seed(seed)
    _w = jnp.asarray

    def _rec_inputs():
        import jax
        import jax.numpy as jnp
        _rk = jax.random.key(seed)
        x = 7.22e-05 + 1 * jax.random.normal(jax.random.fold_in(_rk, 1), (2, 512, 256), jnp.float32)
        _lenS = 512 - jax.random.randint(jax.random.fold_in(_rk, 7), (2,), 0, max(1, 512 // 4) + 1, jnp.int32)
        _lenS2 = 1024 - jax.random.randint(jax.random.fold_in(_rk, 8), (2,), 0, max(1, 1024 // 4) + 1, jnp.int32)
        _ctx_1024P = jax.random.normal(jax.random.fold_in(_rk, 11), (2, 16, 256), jnp.float32)
        _ctx_1024c = jax.random.dirichlet(jax.random.fold_in(_rk, 511), 0.3 * jnp.ones((16,), jnp.float32), (2, 1024))
        _ctx_1024t = jnp.einsum('bsk,bkd->bsd', _ctx_1024c, _ctx_1024P)
        _ctx_1024t = _ctx_1024t * jax.lax.rsqrt(jnp.mean(jnp.square(_ctx_1024t)) + 1e-12) * 0.953939
        ctx_1024 = 4.13588e-05 + 0.999923 * (_ctx_1024t + 0.3 * jax.random.normal(jax.random.fold_in(_rk, 611), (2, 1024, 256), jnp.float32))
        _validS = jnp.arange(512)[None, :] < _lenS[:, None]
        _validS2 = jnp.arange(1024)[None, :] < _lenS2[:, None]
        _causal = jnp.tril(jnp.ones((512, 512), dtype=bool))
        mask_Bx1x1xS2_if1 = jnp.where(jnp.ones((2, 1, 1, 1024), dtype=bool), 1, 0).astype(jnp.int32)
        return (x, ctx_1024, mask_Bx1x1xS2_if1)
    x, ctx_1024, mask_Bx1x1xS2_if1 = _rec_inputs()

    def _L0_attn_setup():
        import jax, jax.numpy as jnp
        import numpy as np
        import math
        D_MODEL = 256
        EXPAND = 2
        HEADDIM = 64
        D_STATE = 64
        D_CONV = 4
        NGROUPS = 1
        D_INNER = EXPAND * D_MODEL
        NHEADS = D_INNER // HEADDIM
        CONV_DIM = D_INNER + 2 * NGROUPS * D_STATE
        D_IN_PROJ = 2 * D_INNER + 2 * NGROUPS * D_STATE + NHEADS
        BATCH, SEQLEN = (4, 512)
        RMS_EPS = 1.1920929e-07
        GNORM_EPS = 1e-05

        def _rmsnorm(x, w, eps):
            return x * jax.lax.rsqrt(jnp.mean(x * x, axis=-1, keepdims=True) + eps) * w

        def _forward(x, norm_w, r_w1, r_b1, r_w2, r_b2, in_proj_w, conv_w, conv_b, dt_bias, A_log, D_param, gnorm_w, out_proj_w):
            B, S, Dm = x.shape
            x_norm = _rmsnorm(x, norm_w, RMS_EPS)
            h = jax.nn.silu(x_norm.mean(axis=1) @ r_w1.T + r_b1)
            probs = jax.nn.softmax(h @ r_w2.T + r_b2, axis=-1)
            p_fast = probs[:, 0][:, None, None]
            p_mamba = (probs[:, 1] + probs[:, 2])[:, None, None]
            zxbcdt = x_norm @ in_proj_w.T
            z, xBC, dt = jnp.split(zxbcdt, [D_INNER, D_INNER + CONV_DIM], axis=-1)
            conv = jax.lax.conv_general_dilated(xBC.transpose(0, 2, 1), conv_w[:, None, :], (1,), [(D_CONV - 1, 0)], feature_group_count=CONV_DIM)
            xBC = jax.nn.silu(conv.transpose(0, 2, 1) + conv_b)
            xh, Bmat, Cmat = jnp.split(xBC, [D_INNER, D_INNER + NGROUPS * D_STATE], axis=-1)
            xh = xh.reshape(B, S, NHEADS, HEADDIM)
            dt = jax.nn.softplus(dt + dt_bias)
            A = -jnp.exp(A_log)
            dA = jnp.exp(dt * A)

            def step(hstate, inp):
                dA_t, dt_t, x_t, B_t, C_t = inp
                hstate = hstate * dA_t[..., None, None] + (dt_t[..., None] * x_t)[..., None] * B_t[:, None, None, :]
                y_t = jnp.einsum('bhpn,bn->bhp', hstate, C_t)
                return (hstate, y_t)
            h0 = jnp.zeros((B, NHEADS, HEADDIM, D_STATE), x.dtype)
            xs = (dA.transpose(1, 0, 2), dt.transpose(1, 0, 2), xh.transpose(1, 0, 2, 3), Bmat.transpose(1, 0, 2), Cmat.transpose(1, 0, 2))
            _, ys = jax.lax.scan(step, h0, xs)
            y = ys.transpose(1, 0, 2, 3) + D_param[:, None] * xh
            y = y.reshape(B, S, D_INNER)
            yg = y * jax.nn.silu(z)
            yg = _rmsnorm(yg, gnorm_w, GNORM_EPS)
            mamba_out = yg @ out_proj_w.T
            out = p_fast * x_norm + p_mamba * mamba_out
            return x + out
        key = jax.random.key(seed)
        ks = jax.random.split(key, 8)
        x = jax.random.normal(ks[0], (BATCH, SEQLEN, D_MODEL), jnp.float32)
        r_w1 = jax.random.normal(ks[1], (32, D_MODEL), jnp.float32) / math.sqrt(D_MODEL)
        r_b1 = jnp.zeros((32,), jnp.float32)
        r_w2 = jax.random.normal(ks[2], (3, 32), jnp.float32) / math.sqrt(32)
        r_b2 = jnp.zeros((3,), jnp.float32)
        in_proj_w = jax.random.normal(ks[3], (D_IN_PROJ, D_MODEL), jnp.float32) / math.sqrt(D_MODEL)
        conv_w = jax.random.normal(ks[4], (CONV_DIM, D_CONV), jnp.float32) * 0.2
        conv_b = jnp.zeros((CONV_DIM,), jnp.float32)
        dt_bias = jax.random.normal(ks[5], (NHEADS,), jnp.float32) * 0.1
        A_log = jnp.log(0.001 * 2.0 ** jnp.arange(NHEADS, dtype=jnp.float32))
        D_param = jnp.ones((NHEADS,), jnp.float32)
        gnorm_w = jnp.ones((D_INNER,), jnp.float32)
        out_proj_w = jax.random.normal(ks[6], (D_MODEL, D_INNER), jnp.float32) / math.sqrt(D_INNER)
        norm_w = jnp.ones((D_MODEL,), jnp.float32)
        return {'x': x, 'norm_w': norm_w, 'r_w1': r_w1, 'r_b1': r_b1, 'r_w2': r_w2, 'r_b2': r_b2, 'in_proj_w': in_proj_w, 'conv_w': conv_w, 'conv_b': conv_b, 'dt_bias': dt_bias, 'A_log': A_log, 'D_param': D_param, 'gnorm_w': gnorm_w, 'out_proj_w': out_proj_w}
    _L0_attn_all = _L0_attn_setup()
    _L0_attn_in = {k: v for k, v in _L0_attn_all.items() if k in ('norm_w', 'r_w1', 'r_b1', 'r_w2', 'r_b2', 'in_proj_w', 'conv_w', 'conv_b', 'dt_bias', 'A_log', 'D_param', 'gnorm_w', 'out_proj_w')}
    del _L0_attn_all

    def _L0_xattn_setup():
        import jax, jax.numpy as jnp
        import numpy as np
        import math
        D_MODEL = 256
        H = 16
        D_K = D_MODEL // H

        def _split_heads(x, B):
            return x.reshape(B, -1, H, D_K).transpose(0, 2, 1, 3)
        key = jax.random.key(seed)
        ks = jax.random.split(key, 12)
        B, S = (4, 512)
        scale = 1.0 / math.sqrt(D_MODEL)
        inp = {'q': jax.random.normal(ks[0], (B, S, D_MODEL), jnp.float32), 'k': jax.random.normal(ks[1], (B, S, D_MODEL), jnp.float32), 'v': jax.random.normal(ks[2], (B, S, D_MODEL), jnp.float32), 'mask': jnp.ones((B, 1, 1, S), jnp.int32), 'wq': jax.random.normal(ks[3], (D_MODEL, D_MODEL), jnp.float32) * scale, 'bq': jax.random.normal(ks[4], (D_MODEL,), jnp.float32) * scale, 'wk': jax.random.normal(ks[5], (D_MODEL, D_MODEL), jnp.float32) * scale, 'bk': jax.random.normal(ks[6], (D_MODEL,), jnp.float32) * scale, 'wv': jax.random.normal(ks[7], (D_MODEL, D_MODEL), jnp.float32) * scale, 'bv': jax.random.normal(ks[8], (D_MODEL,), jnp.float32) * scale, 'wo': jax.random.normal(ks[9], (D_MODEL, D_MODEL), jnp.float32) * scale, 'bo': jax.random.normal(ks[10], (D_MODEL,), jnp.float32) * scale}
        return inp
    _L0_xattn_all = _L0_xattn_setup()
    _L0_xattn_in = {k: v for k, v in _L0_xattn_all.items() if k in ('wq', 'bq', 'wk', 'bk', 'wv', 'bv', 'wo', 'bo')}
    del _L0_xattn_all

    def _L0_ffn_setup():
        import jax, jax.numpy as jnp
        import numpy as np
        B, S, D, E = (4, 512, 256, 8)
        H = 2 * D
        key = jax.random.key(seed)
        ks = jax.random.split(key, 7)
        s_d = 1.0 / np.sqrt(D)
        s_h = 1.0 / np.sqrt(H)
        return {'x': jax.random.normal(ks[0], (B, S, D), dtype=jnp.float32), 'w_router': jax.random.normal(ks[1], (D, E), dtype=jnp.float32) * s_d, 'b_router': jnp.zeros((E,), dtype=jnp.float32), 'w1': jax.random.normal(ks[2], (E, D, H), dtype=jnp.float32) * s_d, 'b1': jnp.zeros((E, H), dtype=jnp.float32), 'w2': jax.random.normal(ks[3], (E, H, D), dtype=jnp.float32) * s_h, 'b2': jnp.zeros((E, D), dtype=jnp.float32)}
    _L0_ffn_all = _L0_ffn_setup()
    _L0_ffn_in = {k: v for k, v in _L0_ffn_all.items() if k in ('w_router', 'b_router', 'w1', 'b1', 'w2', 'b2')}
    del _L0_ffn_all

    def _L1_attn_setup():
        import jax, jax.numpy as jnp
        import numpy as np
        DIM_IN, DIM_K, DIM_V, N_QUERY = (256, 128, 128, 8)

        def _kaiming_uniform(key, shape):
            fan_in = shape[-2] if len(shape) > 1 else shape[-1]
            gain = 1.0 / np.sqrt(3.0)
            bound = gain * np.sqrt(3.0 / fan_in)
            return jax.random.uniform(key, shape, jnp.float32, -bound, bound)
        key = jax.random.key(seed)
        kx, kq, kk, kv, ko = jax.random.split(key, 5)
        x = jax.random.normal(kx, (4, 512, DIM_IN), dtype=jnp.float32)
        proj_q = _kaiming_uniform(kq, (N_QUERY, DIM_IN, DIM_K))
        proj_k = _kaiming_uniform(kk, (DIM_IN, DIM_K))
        proj_v = _kaiming_uniform(kv, (DIM_IN, DIM_V))
        proj_o = _kaiming_uniform(ko, (N_QUERY, DIM_IN, DIM_V))
        return {'x': x, 'proj_q': proj_q, 'proj_k': proj_k, 'proj_v': proj_v, 'proj_o': proj_o}
    _L1_attn_all = _L1_attn_setup()
    _L1_attn_in = {k: v for k, v in _L1_attn_all.items() if k in ('proj_q', 'proj_k', 'proj_v', 'proj_o')}
    del _L1_attn_all

    def _L1_xattn_setup():
        import jax, jax.numpy as jnp
        import numpy as np
        N_HEAD = 16
        key = jax.random.key(seed)
        ks = jax.random.split(key, 5)
        b, l, d = (4, 512, 256)
        dh = d // N_HEAD
        return {'q': jax.random.normal(ks[0], (b, l, d), dtype=jnp.float32), 'kv': jax.random.normal(ks[1], (b, l, d), dtype=jnp.float32), 'Wq': jax.random.normal(ks[2], (d, d), dtype=jnp.float32) * 0.02, 'Wkv': jax.random.normal(ks[3], (2 * dh, d), dtype=jnp.float32) * 0.02, 'Wc': jax.random.normal(ks[4], (d, d), dtype=jnp.float32) * 0.02}
    _L1_xattn_all = _L1_xattn_setup()
    _L1_xattn_in = {k: v for k, v in _L1_xattn_all.items() if k in ('Wq', 'Wkv', 'Wc')}
    del _L1_xattn_all

    def _L1_ffn_setup():
        import jax, jax.numpy as jnp
        import numpy as np
        LN_EPS = 1e-12
        key = jax.random.key(seed)
        ks = jax.random.split(key, 8)
        B, S, H, I, E = (4, 512, 256, 1024, 8)
        sH = 1.0 / np.sqrt(H)
        sI = 1.0 / np.sqrt(I)
        return {'hidden_states': jax.random.normal(ks[0], (B, S, H), dtype=jnp.float32), 'Wr': jax.random.uniform(ks[1], (E, H), jnp.float32, -sH, sH), 'W1': jax.random.uniform(ks[2], (E, H, I), jnp.float32, -sH, sH), 'b1': jax.random.uniform(ks[3], (E, I), jnp.float32, -sH, sH), 'Wo': jax.random.uniform(ks[4], (I, H), jnp.float32, -sI, sI), 'bo': jax.random.uniform(ks[5], (H,), jnp.float32, -sI, sI), 'gamma': jnp.ones((H,), jnp.float32), 'beta': jnp.zeros((H,), jnp.float32)}
    _L1_ffn_all = _L1_ffn_setup()
    _L1_ffn_in = {k: v for k, v in _L1_ffn_all.items() if k in ('Wr', 'W1', 'b1', 'Wo', 'bo', 'gamma', 'beta')}
    del _L1_ffn_all
    return {'x': x, 'ctx_1024': ctx_1024, 'mask_Bx1x1xS2_if1': mask_Bx1x1xS2_if1, 'L0_attn_norm_w': _L0_attn_in['norm_w'], 'L0_attn_r_w1': _L0_attn_in['r_w1'], 'L0_attn_r_b1': _L0_attn_in['r_b1'], 'L0_attn_r_w2': _L0_attn_in['r_w2'], 'L0_attn_r_b2': _L0_attn_in['r_b2'], 'L0_attn_in_proj_w': _L0_attn_in['in_proj_w'], 'L0_attn_conv_w': _L0_attn_in['conv_w'], 'L0_attn_conv_b': _L0_attn_in['conv_b'], 'L0_attn_dt_bias': _L0_attn_in['dt_bias'], 'L0_attn_A_log': _L0_attn_in['A_log'], 'L0_attn_D_param': _L0_attn_in['D_param'], 'L0_attn_gnorm_w': _L0_attn_in['gnorm_w'], 'L0_attn_out_proj_w': _L0_attn_in['out_proj_w'], 'L0_xattn_wq': _L0_xattn_in['wq'], 'L0_xattn_bq': _L0_xattn_in['bq'], 'L0_xattn_wk': _L0_xattn_in['wk'], 'L0_xattn_bk': _L0_xattn_in['bk'], 'L0_xattn_wv': _L0_xattn_in['wv'], 'L0_xattn_bv': _L0_xattn_in['bv'], 'L0_xattn_wo': _L0_xattn_in['wo'], 'L0_xattn_bo': _L0_xattn_in['bo'], 'L0_ffn_w_router': _L0_ffn_in['w_router'], 'L0_ffn_b_router': _L0_ffn_in['b_router'], 'L0_ffn_w1': _L0_ffn_in['w1'], 'L0_ffn_b1': _L0_ffn_in['b1'], 'L0_ffn_w2': _L0_ffn_in['w2'], 'L0_ffn_b2': _L0_ffn_in['b2'], 'L1_attn_proj_q': _L1_attn_in['proj_q'], 'L1_attn_proj_k': _L1_attn_in['proj_k'], 'L1_attn_proj_v': _L1_attn_in['proj_v'], 'L1_attn_proj_o': _L1_attn_in['proj_o'], 'L1_xattn_Wq': _L1_xattn_in['Wq'], 'L1_xattn_Wkv': _L1_xattn_in['Wkv'], 'L1_xattn_Wc': _L1_xattn_in['Wc'], 'L1_ffn_Wr': _L1_ffn_in['Wr'], 'L1_ffn_W1': _L1_ffn_in['W1'], 'L1_ffn_b1': _L1_ffn_in['b1'], 'L1_ffn_Wo': _L1_ffn_in['Wo'], 'L1_ffn_bo': _L1_ffn_in['bo'], 'L1_ffn_gamma': _L1_ffn_in['gamma'], 'L1_ffn_beta': _L1_ffn_in['beta']}

def reference(x, ctx_1024, mask_Bx1x1xS2_if1, L0_attn_norm_w, L0_attn_r_w1, L0_attn_r_b1, L0_attn_r_w2, L0_attn_r_b2, L0_attn_in_proj_w, L0_attn_conv_w, L0_attn_conv_b, L0_attn_dt_bias, L0_attn_A_log, L0_attn_D_param, L0_attn_gnorm_w, L0_attn_out_proj_w, L0_xattn_wq, L0_xattn_bq, L0_xattn_wk, L0_xattn_bk, L0_xattn_wv, L0_xattn_bv, L0_xattn_wo, L0_xattn_bo, L0_ffn_w_router, L0_ffn_b_router, L0_ffn_w1, L0_ffn_b1, L0_ffn_w2, L0_ffn_b2, L1_attn_proj_q, L1_attn_proj_k, L1_attn_proj_v, L1_attn_proj_o, L1_xattn_Wq, L1_xattn_Wkv, L1_xattn_Wc, L1_ffn_Wr, L1_ffn_W1, L1_ffn_b1, L1_ffn_Wo, L1_ffn_bo, L1_ffn_gamma, L1_ffn_beta):
    import jax
    import jax.numpy as jnp

    def _L0_attn_ref(x, norm_w, r_w1, r_b1, r_w2, r_b2, in_proj_w, conv_w, conv_b, dt_bias, A_log, D_param, gnorm_w, out_proj_w):
        import jax, jax.numpy as jnp
        import numpy as np
        import math
        D_MODEL = 256
        EXPAND = 2
        HEADDIM = 64
        D_STATE = 64
        D_CONV = 4
        NGROUPS = 1
        D_INNER = EXPAND * D_MODEL
        NHEADS = D_INNER // HEADDIM
        CONV_DIM = D_INNER + 2 * NGROUPS * D_STATE
        D_IN_PROJ = 2 * D_INNER + 2 * NGROUPS * D_STATE + NHEADS
        BATCH, SEQLEN = (4, 512)
        RMS_EPS = 1.1920929e-07
        GNORM_EPS = 1e-05

        def _rmsnorm(x, w, eps):
            return x * jax.lax.rsqrt(jnp.mean(x * x, axis=-1, keepdims=True) + eps) * w

        def _forward(x, norm_w, r_w1, r_b1, r_w2, r_b2, in_proj_w, conv_w, conv_b, dt_bias, A_log, D_param, gnorm_w, out_proj_w):
            B, S, Dm = x.shape
            x_norm = _rmsnorm(x, norm_w, RMS_EPS)
            h = jax.nn.silu(x_norm.mean(axis=1) @ r_w1.T + r_b1)
            probs = jax.nn.softmax(h @ r_w2.T + r_b2, axis=-1)
            p_fast = probs[:, 0][:, None, None]
            p_mamba = (probs[:, 1] + probs[:, 2])[:, None, None]
            zxbcdt = x_norm @ in_proj_w.T
            z, xBC, dt = jnp.split(zxbcdt, [D_INNER, D_INNER + CONV_DIM], axis=-1)
            conv = jax.lax.conv_general_dilated(xBC.transpose(0, 2, 1), conv_w[:, None, :], (1,), [(D_CONV - 1, 0)], feature_group_count=CONV_DIM)
            xBC = jax.nn.silu(conv.transpose(0, 2, 1) + conv_b)
            xh, Bmat, Cmat = jnp.split(xBC, [D_INNER, D_INNER + NGROUPS * D_STATE], axis=-1)
            xh = xh.reshape(B, S, NHEADS, HEADDIM)
            dt = jax.nn.softplus(dt + dt_bias)
            A = -jnp.exp(A_log)
            dA = jnp.exp(dt * A)

            def step(hstate, inp):
                dA_t, dt_t, x_t, B_t, C_t = inp
                hstate = hstate * dA_t[..., None, None] + (dt_t[..., None] * x_t)[..., None] * B_t[:, None, None, :]
                y_t = jnp.einsum('bhpn,bn->bhp', hstate, C_t)
                return (hstate, y_t)
            h0 = jnp.zeros((B, NHEADS, HEADDIM, D_STATE), x.dtype)
            xs = (dA.transpose(1, 0, 2), dt.transpose(1, 0, 2), xh.transpose(1, 0, 2, 3), Bmat.transpose(1, 0, 2), Cmat.transpose(1, 0, 2))
            _, ys = jax.lax.scan(step, h0, xs)
            y = ys.transpose(1, 0, 2, 3) + D_param[:, None] * xh
            y = y.reshape(B, S, D_INNER)
            yg = y * jax.nn.silu(z)
            yg = _rmsnorm(yg, gnorm_w, GNORM_EPS)
            mamba_out = yg @ out_proj_w.T
            out = p_fast * x_norm + p_mamba * mamba_out
            return x + out
        return _forward(x, norm_w, r_w1, r_b1, r_w2, r_b2, in_proj_w, conv_w, conv_b, dt_bias, A_log, D_param, gnorm_w, out_proj_w)

    def _L0_xattn_ref(q, k, v, mask, wq, bq, wk, bk, wv, bv, wo, bo):
        import jax, jax.numpy as jnp
        import numpy as np
        import math
        D_MODEL = 256
        H = 16
        D_K = D_MODEL // H

        def _split_heads(x, B):
            return x.reshape(B, -1, H, D_K).transpose(0, 2, 1, 3)
        B = q.shape[0]
        qh = _split_heads(q @ wq.T + bq, B)
        kh = _split_heads(k @ wk.T + bk, B)
        vh = _split_heads(v @ wv.T + bv, B)
        scores = jnp.einsum('bhqd,bhkd->bhqk', qh, kh) / math.sqrt(D_K)
        scores = jnp.where(mask == 0, jnp.float32(-1000000000.0), scores)
        attn = jax.nn.softmax(scores, axis=-1)
        out = jnp.einsum('bhqk,bhkd->bhqd', attn, vh)
        out = out.transpose(0, 2, 1, 3).reshape(B, -1, D_MODEL)
        return out @ wo.T + bo

    def _L0_ffn_ref(x, w_router, b_router, w1, b1, w2, b2):
        import jax, jax.numpy as jnp
        import numpy as np
        B, S, D, E = (4, 512, 256, 8)
        H = 2 * D
        scores = jax.nn.softmax(x @ w_router + b_router, axis=2)
        expert_probs = jnp.max(scores, axis=2)
        expert_idx = jnp.argmax(scores, axis=2)
        h = jax.nn.relu(jnp.einsum('bsd,edh->ebsh', x, w1) + b1[:, None, None, :])
        y = jnp.einsum('ebsh,ehd->ebsd', h, w2) + b2[:, None, None, :]
        onehot = jax.nn.one_hot(expert_idx, E, dtype=x.dtype)
        out = jnp.einsum('ebsd,bse->bsd', y, onehot)
        return out * expert_probs[..., None]

    def _L1_attn_ref(x, proj_q, proj_k, proj_v, proj_o):
        import jax, jax.numpy as jnp
        import numpy as np
        DIM_IN, DIM_K, DIM_V, N_QUERY = (256, 128, 128, 8)

        def _kaiming_uniform(key, shape):
            fan_in = shape[-2] if len(shape) > 1 else shape[-1]
            gain = 1.0 / np.sqrt(3.0)
            bound = gain * np.sqrt(3.0 / fan_in)
            return jax.random.uniform(key, shape, jnp.float32, -bound, bound)
        Q = jnp.einsum('bnd,hdk->bhnk', x, proj_q)
        K = jnp.einsum('bmd,dk->bmk', x, proj_k)
        V = jnp.einsum('bmd,dv->bmv', x, proj_v)
        logits = jnp.einsum('bhnk,bmk->bhnm', Q, K)
        weights = jax.nn.softmax(logits, axis=-1)
        O = jnp.einsum('bhnm,bmv->bhnv', weights, V)
        Y = jnp.einsum('bhnv,hdv->bnd', O, proj_o)
        return Y

    def _L1_xattn_ref(q, kv, Wq, Wkv, Wc):
        import jax, jax.numpy as jnp
        import numpy as np
        N_HEAD = 16
        b, l, d = q.shape
        h = N_HEAD
        dh = d // h
        qp = jnp.einsum('bld,ed->ble', q, Wq)
        scores = jnp.einsum('bld,bmd->blm', qp, kv)
        idx = jnp.argmax(scores, axis=-1)
        mem = jnp.take_along_axis(kv, idx[..., None], axis=1)
        mkv = jnp.einsum('bld,ed->ble', mem, Wkv)
        mk, mv = jnp.split(mkv, 2, axis=-1)
        qh = qp.reshape(b, l, h, dh).transpose(0, 2, 1, 3)
        scale = 1.0 / np.sqrt(dh).astype(np.float32)
        logits = jnp.einsum('bhld,bmd->bhlm', qh, mk) * scale
        attn = jax.nn.softmax(logits, axis=-1)
        out = jnp.einsum('bhlm,bmd->bhld', attn, mv)
        out = out.transpose(0, 2, 1, 3).reshape(b, l, d)
        return jnp.einsum('bld,ed->ble', out, Wc)

    def _L1_ffn_ref(hidden_states, Wr, W1, b1, Wo, bo, gamma, beta):
        import jax, jax.numpy as jnp
        import numpy as np
        LN_EPS = 1e-12
        B, S, H = hidden_states.shape
        E = Wr.shape[0]
        x = hidden_states.reshape(-1, H)
        router_logits = x @ Wr.T
        expert_idx = jnp.argmax(jax.nn.softmax(router_logits, axis=-1), axis=-1)
        inter = jnp.zeros((x.shape[0], W1.shape[2]), dtype=x.dtype)
        for e in range(E):
            mask = (expert_idx == e)[:, None].astype(x.dtype)
            inter = inter + mask * jax.nn.gelu(x @ W1[e] + b1[e], approximate=False)
        y = inter @ Wo + bo + x
        mu = jnp.mean(y, axis=-1, keepdims=True)
        var = jnp.mean(jnp.square(y - mu), axis=-1, keepdims=True)
        out = (y - mu) * jax.lax.rsqrt(var + LN_EPS) * gamma + beta
        return out.reshape(B, S, H)
    x = x + _L0_attn_ref(_layernorm(x, axis=-1), L0_attn_norm_w, L0_attn_r_w1, L0_attn_r_b1, L0_attn_r_w2, L0_attn_r_b2, L0_attn_in_proj_w, L0_attn_conv_w, L0_attn_conv_b, L0_attn_dt_bias, L0_attn_A_log, L0_attn_D_param, L0_attn_gnorm_w, L0_attn_out_proj_w)
    x = x + _L0_xattn_ref(_layernorm(x, axis=-1), ctx_1024, ctx_1024, mask_Bx1x1xS2_if1, L0_xattn_wq, L0_xattn_bq, L0_xattn_wk, L0_xattn_bk, L0_xattn_wv, L0_xattn_bv, L0_xattn_wo, L0_xattn_bo)
    x = x + _L0_ffn_ref(_layernorm(x, axis=-1), L0_ffn_w_router, L0_ffn_b_router, L0_ffn_w1, L0_ffn_b1, L0_ffn_w2, L0_ffn_b2)
    x = x + _L1_attn_ref(_layernorm(x, axis=-1), L1_attn_proj_q, L1_attn_proj_k, L1_attn_proj_v, L1_attn_proj_o)
    x = x + _L1_xattn_ref(_layernorm(x, axis=-1), ctx_1024, L1_xattn_Wq, L1_xattn_Wkv, L1_xattn_Wc)
    x = x + _L1_ffn_ref(_layernorm(x, axis=-1), L1_ffn_Wr, L1_ffn_W1, L1_ffn_b1, L1_ffn_Wo, L1_ffn_bo, L1_ffn_gamma, L1_ffn_beta)
    return x

_drawn_inputs = setup_inputs


def setup_inputs(seed=0):
    import zlib

    import numpy as np

    out = dict(_drawn_inputs(seed))
    spreads = {'L0_attn_norm_w': (1.0, 0.2),
     'L0_attn_r_b1': (0.0, 0.8),
     'L0_attn_r_b2': (0.0, 0.1),
     'L0_attn_conv_b': (0.0, 0.1),
     'L0_attn_D_param': (1.0, 0.6),
     'L0_attn_gnorm_w': (1.0, 0.2),
     'L0_ffn_b_router': (0.0, 0.392),
     'L0_ffn_b1': (0.0, 0.626),
     'L0_ffn_b2': (0.0, 0.426),
     'L1_ffn_gamma': (1.0, 0.2),
     'L1_ffn_beta': (0.0, 0.301)}
    factors = {'L0_attn_r_w1': 5.962,
     'L0_attn_r_w2': 3.71,
     'L0_attn_dt_bias': 5.016,
     'L0_xattn_bq': 6.247,
     'L0_xattn_bk': 8.0,
     'L1_xattn_Wq': 8.0,
     'L1_xattn_Wkv': 2.76,
     'L1_ffn_b1': 8.0,
     'L1_ffn_bo': 8.0}
    for name, (base, spread) in spreads.items():
        noise = np.random.default_rng([zlib.crc32(name.encode()), seed]).standard_normal(out[name].shape)
        drawn = base * np.exp(spread * noise) if base else spread * noise
        out[name] = jnp.asarray(drawn.astype(out[name].dtype))
    for name, factor in factors.items():
        out[name] = (out[name] * factor).astype(out[name].dtype)
    return out
```

```python
from contextlib import ExitStack

import concourse.bass as bass
from concourse import mybir

ALU = mybir.AluOpType
ACT = mybir.ActivationFunctionType
AX = mybir.AxisListType
F32 = mybir.dt.float32
BF16 = mybir.dt.bfloat16
I32 = mybir.dt.int32
U32 = mybir.dt.uint32

P = 128
B, S, D = 2, 512, 256
T = B * S
NT = T // P
TB = S // P
KD = D // P
BANK = 512


class Chain:

    def __init__(self, eng, sem):
        self.eng, self.sem, self.n = eng, sem, 0

    def link(self, ins):
        self.n += 1
        ins.then_inc(self.sem, 1)
        self.eng.wait_ge(self.sem, self.n)


def layernorm_vector(dve, link, src, dst, st6, mv, rstd, var_ready, rstd_ready):
    for i in range(NT):
        last = dve.bn_stats(st6[:, i, :], src[:, i, :])
    link(last)
    for i in range(NT):
        last = dve.bn_aggr(mv[:, i, :], st6[:, i, :])
    last.then_inc(var_ready, 1)
    dve.wait_ge(var_ready, 1)
    dve.wait_ge(rstd_ready, 1)
    for i in range(NT):
        last = dve.tensor_scalar(dst[:, i, :], src[:, i, :], mv[:, i, 0:1], rstd[:, i:i + 1],
                                 ALU.subtract, ALU.mult)
    return last


def transposes_tensor(pe, PS, XN, ident, done):
    for k in range(KD):
        for b in range(B):
            for i in range(TB):
                last = pe.transpose(PS[:, 2 * k + b, i * P:(i + 1) * P],
                                    XN[:, b * TB + i, k * P:(k + 1) * P], ident[:, :])
            last.then_inc(done, 1)


class Shared:
    pass


class StageSemaphores:

    def __init__(self, nc):
        self.nc, self.held = nc, []

    def enter_context(self, semaphore):
        handle = semaphore.__enter__()
        self.held.append((semaphore, handle))
        return handle

    def clear(self):
        nums = sorted(h.num for _, h in self.held)
        starts = [n for n in nums if n - 1 not in nums]
        ends = [n + 1 for n in nums if n + 1 not in nums]
        for lo, hi in zip(starts, ends):
            self.nc.all_engine_barrier(sems_to_clear=range(lo, hi))
        for semaphore, _ in self.held:
            semaphore.__exit__(None, None, None)


def mamba_stage(nc, ctx, sh, A):
    HEADS, HD, DI, DS, TAPS = 8, 64, 512, 64, 4
    MX = DI // P
    PAD = TAPS - 1
    DT0, B0, C0, X0, Z0 = 2 * DI + 2 * DS, 2 * DI, 2 * DI + DS, DI, 0
    RMS_EPS, GN_EPS, LN_EPS = 1.1920929e-07, 1e-05, 1e-05
    PS, X, XN, XT, ident = sh.PS, sh.X, sh.XN, sh.XT, sh.ident

    stage = ExitStack()
    mhalf = sh.mhalf

    def sb(name, shape, dt=F32):
        return stage.enter_context(nc.sbuf_tensor("m_" + name, shape, dt))

    def sem(name):
        return ctx.enter_context(nc.semaphore("m_" + name))

    w_in = sb("w_in", [P, KD, 2 * DI + 2 * DS + HEADS])
    w_out = sb("w_out", [P, MX, D])
    rw1, rw2 = sb("rw1", [P, KD, 32]), sb("rw2", [32, 3])
    rb1, rb2 = sb("rb1", [32, 1]), sb("rb2", [P, 3])
    nw = sb("nw", [P, D])
    cwx, cbx = sb("cwx", [P, MX, TAPS]), sb("cbx", [P, MX])
    cwbc, cbbc = sb("cwbc", [DS, 2, TAPS]), sb("cbbc", [DS, 2])
    hp = sb("hp", [HEADS, 2])
    negA = sb("negA", [HEADS, 1])
    Dv, gw = sb("Dv", [P, MX]), sb("gw", [P, MX])
    tri = sb("tri", [P, P])
    sel = sb("sel", [HEADS, HEADS, P])
    ones = sb("ones", [P, S])
    XL = sb("XL", [P, NT, D])
    st6, mv, rstd = sb("st6", [P, NT, 6]), sb("mv", [P, NT, 2]), sb("rstd", [P, NT])
    ms = sb("ms", [P, NT])
    rr, rms = sb("rr", [P, NT]), sb("rms", [P, NT])
    xsum = sb("xsum", [P, KD, B])
    hid, hidB = sb("hid", [32, B]), sb("hidB", [32, B, P])
    lg, mxl, pr, psm = sb("lg", [P, B, 3]), sb("mxl", [P, B]), sb("pr", [P, B, 3]), sb("psm", [P, B])
    pmam = sb("pmam", [P, B])
    dtr, ab, sp, dt = (sb(n, [HEADS, T]) for n in ("dtr", "ab", "sp", "dt"))
    La = sb("La", [HEADS, T])
    TD = sb("TD", [P, 2, NT, HEADS])
    XC = [sb(f"XC{n}", [P, B, PAD + S]) for n in range(2)]
    CV = [sb(f"CV{n}", [P, B, S]) for n in range(2)]
    XH = sb("XH", [P, MX, T])
    BC = sb("BC", [DS, 2, T])
    SZ = sb("SZ", [P, MX, T])
    XD = sb("XD", [P, NT, DI])
    GT = sb("GT", [P, B, TB * BANK])
    Lm = [sb(f"Lm{n}", [P, TB, P]) for n in range(2)]
    E = [sb(f"E{n}", [P, 5 * BANK]) for n in range(2)]
    W = [sb(f"W{n}", [P, TB * BANK]) for n in range(2)]
    SQ, YG, YW = XH, SZ, SZ
    base = XL
    gr = sb("gr", [P, NT])
    yt = sb("yt", [P, S])

    small_in, w_in_in, w_out_in = sem("small_in"), sem("w_in_in"), sem("w_out_in")
    normed, squared, xn_ready = sem("normed"), sem("squared"), sem("xn_ready")
    xT_done, xT_ready = sem("xT_done"), sem("xT_ready")
    proj_done, proj_taken = sem("proj_done"), sem("proj_taken")
    hid_mm, hid_ready, hidB_ready, lg_mm, lg_ready, pr_ready = (
        sem(n) for n in ("hid_mm", "hid_ready", "hidB_ready", "lg_mm", "lg_ready", "pr_ready"))
    negA_ready, sp_ready, dt_ready, La_ready = sem("negA_ready"), sem("sp_ready"), sem("dt_ready"), sem("La_ready")
    td_mm, td_ready = sem("td_mm"), sem("td_ready")
    padded, conv_ready, silu_ready = sem("padded"), sem("conv_ready"), sem("silu_ready")
    xh_mm, xd_ready = sem("xh_mm"), sem("xd_ready")
    g_mm, g_copied, g_ready = sem("g_mm"), sem("g_copied"), sem("g_ready")
    decay_mm, diag_ready, e_ready, w_ready, y_mm, yg_ready = (
        sem(n) for n in ("decay_mm", "diag_ready", "e_ready", "w_ready", "y_mm", "yg_ready"))
    sq_ready, yw_ready, ss_mm, gr_ready, out_mm, base_ready = (
        sem(n) for n in ("sq_ready", "yw_ready", "ss_mm", "gr_ready", "out_mm", "base_ready"))
    var_ready, rstd_ready = sem("var_ready"), sem("rstd_ready")
    own_v, own_a, own_p = sem("own_v"), sem("own_a"), sem("own_p")
    out_taken = sem("out_taken")

    mtiles = ([("dt", DT0, HEADS, 0), ("bc", B0, DS, 0), ("bc", C0, DS, 1)]
              + [("x", X0 + P * m, P, m) for m in range(MX)]
              + [("z", Z0 + P * m, P, m) for m in range(MX)])
    convs = [t for t in mtiles if t[0] in ("bc", "x")]
    NSMALL = 14

    with stage, nc.Block() as block:

        @block.sync
        def _(sp_):
            for dst, name in ((nw, "m_nw"), (rw1, "m_rw1"), (rw2, "m_rw2"), (rb1, "m_rb1"),
                              (rb2, "m_rb2"), (cwx, "m_cwx"), (cbx, "m_cbx"), (cwbc, "m_cwbc"),
                              (cbbc, "m_cbbc"), (hp, "m_hp"), (Dv, "m_D"), (gw, "m_gw"),
                              (tri, "tri"), (sel, "sel")):
                src = A[name]
                sp_.dma_start(dst[tuple(slice(None) for _ in dst.shape)], src).then_inc(small_in, 16)
            sp_.dma_start(w_in[:, :, :], A["m_win"]).then_inc(w_in_in, 16)
            sp_.dma_start(w_out[:, :, :], A["m_wout"]).then_inc(w_out_in, 16)

        @block.gpsimd
        def _(pool):
            c = Chain(pool, own_p)
            for n in range(2):
                last = pool.memset(XC[n][:, :, 0:PAD], 0.0)
            pool.memset(ones[:, :], 1.0).then_inc(padded, 1)
            pool.wait_ge(var_ready, 1)
            c.link(pool.tensor_scalar(rstd[:, :], mv[:, :, 1], LN_EPS, None, ALU.add))
            pool.tensor_tensor(rstd[:, :], rstd[:, :], mhalf[:, :], ALU.pow).then_inc(rstd_ready, 1)
            pool.wait_ge(var_ready, 2)
            pool.tensor_tensor(rms[:, :], rr[:, :], mhalf[:, :], ALU.pow).then_inc(rstd_ready, 1)
            pool.wait_ge(xn_ready, NT)
            c.link(pool.tensor_tensor(base[:, :, :], X[:, :, :], XL[:, :, :], ALU.add))
            pool.wait_ge(pr_ready, 1)
            pool.wait_ge(xT_done, KD * B)
            for i in range(NT):
                b = i // TB
                last = pool.tensor_scalar(XN[:, i, :], XN[:, i, :], pr[:, b, 0:1], None, ALU.mult)
            c.link(last)
            pool.tensor_tensor(base[:, :, :], base[:, :, :], XN[:, :, :], ALU.add).then_inc(base_ready, 1)
            pool.wait_ge(var_ready, 3)
            pool.tensor_tensor(rr[:, :], gr[:, :], mhalf[:, :], ALU.pow).then_inc(rstd_ready, 1)

        @block.vector
        def _(dve):
            c = Chain(dve, own_v)
            layernorm_vector(dve, c.link, X, XL, st6, mv, rstd, var_ready, rstd_ready).then_inc(normed, 1)
            dve.wait_ge(squared, NT)
            dve.tensor_scalar(rr[:, :], ms[:, :], 1.0 / D, RMS_EPS, ALU.mult, ALU.add).then_inc(var_ready, 1)
            dve.wait_ge(rstd_ready, 2)
            dve.wait_ge(small_in, 16 * NSMALL)
            for i in range(NT):
                dve.scalar_tensor_tensor(out=XN[:, i, :], in0=XL[:, i, :], scalar=rms[:, i:i + 1],
                                         in1=nw[:, :], op0=ALU.mult, op1=ALU.mult).then_inc(xn_ready, 1)

            dve.wait_ge(hid_ready, 1)
            dve.tensor_copy(hidB[:, :, :], hid[:, :].unsqueeze(2).to_broadcast([32, B, P])).then_inc(hidB_ready, 1)

            dve.wait_ge(sp_ready, 1)
            c.link(dve.tensor_scalar(ab[:, :], dtr[:, :], 0.0, None, ALU.max))
            c.link(dve.tensor_tensor(dt[:, :], ab[:, :], sp[:, :], ALU.add))
            dve.wait_ge(negA_ready, 1)
            c.link(dve.tensor_scalar(ab[:, :], dt[:, :], negA[:, 0:1], -1.0, ALU.mult, ALU.mult))
            dve.wait_ge(padded, 1)
            for b in range(B):
                cols = slice(b * S, (b + 1) * S)
                last = dve.tensor_tensor_scan(La[:, cols], ones[0:HEADS, :], ab[:, cols], 0.0,
                                              ALU.mult, ALU.add)
            last.then_inc(La_ready, 1)

            dve.wait_ge(lg_mm, 1)
            c.link(dve.tensor_tensor(lg[:, :, :], PS[:, 1, 0:3 * B].rearrange("p (b e) -> p b e", b=B),
                                     rb2[:, :].unsqueeze(1).to_broadcast([P, B, 3]), ALU.add))
            c.link(dve.tensor_reduce(mxl[:, :], lg[:, :, :], AX.X, ALU.max))
            dve.tensor_tensor(lg[:, :, :], lg[:, :, :], mxl[:, :].unsqueeze(2).to_broadcast([P, B, 3]),
                              ALU.subtract).then_inc(lg_ready, 1)
            for n, (what, _, rows, m) in enumerate(convs):
                w = cwbc[:, m, :] if what == "bc" else cwx[:, m, :]
                xc, cv = XC[n % 2], CV[n % 2]
                dve.wait_ge(proj_taken, 2 * (n + 2))
                if n >= 2:
                    dve.wait_ge(silu_ready, n - 1)
                c.link(dve.tensor_scalar(cv[0:rows, :, :], xc[0:rows, :, 0:S], w[0:rows, 0:1], None, ALU.mult))
                for tap in range(1, TAPS):
                    last = dve.scalar_tensor_tensor(out=cv[0:rows, :, :], in0=xc[0:rows, :, tap:tap + S],
                                                    scalar=w[0:rows, tap:tap + 1], in1=cv[0:rows, :, :],
                                                    op0=ALU.mult, op1=ALU.add)
                    if tap < TAPS - 1:
                        c.link(last)
                last.then_inc(conv_ready, 1)
                if n == 1:
                    dve.wait_ge(td_mm, 1)
                    c.link(dve.tensor_copy(TD[:, 0, :, :], PS[:, 2, 0:NT * HEADS].rearrange("p (i h) -> p i h", i=NT)))
                    dve.tensor_scalar(TD[:, 1, :, :], PS[:, 2, NT * HEADS:2 * NT * HEADS].rearrange("p (i h) -> p i h", i=NT),
                                      -1.0, None, ALU.mult).then_inc(td_ready, 1)

            dve.wait_ge(lg_ready, 2)
            c.link(dve.tensor_reduce(psm[:, :], pr[:, :, :], AX.X, ALU.add))
            c.link(dve.reciprocal(mxl[:, :], psm[:, :]))
            c.link(dve.tensor_tensor(pr[:, :, :], pr[:, :, :], mxl[:, :].unsqueeze(2).to_broadcast([P, B, 3]),
                                     ALU.mult))
            dve.tensor_tensor(pmam[:, :], pr[:, :, 1], pr[:, :, 2], ALU.add).then_inc(pr_ready, 1)

            for n in range(B * TB):
                b, s = divmod(n, TB)
                dve.wait_ge(g_copied, n + 1)
                o = s * (BANK + P)
                dve.tensor_tensor(GT[:, b, o:o + P], GT[:, b, o:o + P], tri[:, :], ALU.mult).then_inc(g_ready, 1)

            for i in range(NT):
                dve.wait_ge(xh_mm, i + 1)
                dve.tensor_tensor(XD[:, i, :].rearrange("p (h c) -> p h c", h=HEADS),
                                  PS[:, 6 + i % 2, :].rearrange("p (h c) -> p h c", h=HEADS),
                                  TD[:, 0, i, :].unsqueeze(2).to_broadcast([P, HEADS, HD]),
                                  ALU.mult).then_inc(xd_ready, 1)

            def diagonal(n):
                b, h = divmod(n, HEADS)
                dve.wait_ge(decay_mm, n + 1)
                if n >= 2:
                    dve.wait_ge(e_ready, n - 1)
                for s in range(TB):
                    last = dve.tensor_scalar(Lm[n % 2][:, s, :], PS[:, n % 2, s * P:(s + 1) * P],
                                             TD[:, 1, b * TB + s, h:h + 1], 0.0, ALU.add, ALU.min)
                last.then_inc(diag_ready, 1)

            def weights(n):
                b = n // HEADS
                dve.wait_ge(e_ready, n + 1)
                if n >= 2:
                    dve.wait_ge(y_mm, n - 1)
                for s in range(TB):
                    o, m = s * BANK + s * P, S - s * P
                    last = dve.tensor_tensor(W[n % 2][:, o:o + m], E[n % 2][:, o:o + m], GT[:, b, o:o + m], ALU.mult)
                last.then_inc(w_ready, 1)

            def gate(n):
                b, h = divmod(n, HEADS)
                m = h // 2
                cols = slice(b * S, (b + 1) * S)
                dve.wait_ge(y_mm, n + 1)
                c.link(dve.scalar_tensor_tensor(out=yt[:, :], in0=XH[:, m, cols], scalar=Dv[:, m:m + 1],
                                                in1=PS[:, 2 + (n // 2) % 2, :], op0=ALU.mult, op1=ALU.add))
                dve.tensor_tensor(YG[:, m, cols], yt[:, :], SZ[:, m, cols], ALU.mult).then_inc(yg_ready, 1)

            diagonal(0)
            for n in range(B * HEADS):
                if n + 1 < B * HEADS:
                    diagonal(n + 1)
                weights(n)
                if n >= 2 and n % 2 == 0:
                    gate(n - 1)
            gate(B * HEADS - 1)

            dve.wait_ge(sq_ready, B * MX)
            for m in range(MX):
                last = dve.tensor_scalar(YW[:, m, :], YG[:, m, :], gw[:, m:m + 1], None, ALU.mult)
            last.then_inc(yw_ready, 1)
            dve.wait_ge(ss_mm, 1)
            dve.tensor_scalar(gr[:, :], PS[:, 6, 0:NT], 1.0 / DI, GN_EPS, ALU.mult, ALU.add).then_inc(var_ready, 1)
            dve.wait_ge(rstd_ready, 3)
            c.link(dve.tensor_tensor(gr[:, :].rearrange("p (b i) -> p b i", b=B),
                                     rr[:, :].rearrange("p (b i) -> p b i", b=B),
                                     pmam[:, :].unsqueeze(2).to_broadcast([P, B, TB]), ALU.mult))
            dve.wait_ge(base_ready, 1)
            for i in range(NT):
                dve.wait_ge(out_mm, i + 1)
                dve.scalar_tensor_tensor(out=X[:, i, :], in0=PS[:, i % 4, 0:D], scalar=gr[:, i:i + 1],
                                         in1=base[:, i, :], op0=ALU.mult, op1=ALU.add).then_inc(out_taken, 1)

        def silu_of(act, n):
            if n >= len(convs):
                return
            what, _, rows, m = convs[n]
            bias = cbbc[:, m:m + 1] if what == "bc" else cbx[:, m:m + 1]
            dst = BC if what == "bc" else XH
            act.wait_ge(conv_ready, n + 1)
            act.activation(dst[:, m, :], CV[n % 2][0:rows, :, :], ACT.Silu, bias=bias).then_inc(silu_ready, 1)

        @block.scalar
        def _(act):
            c = Chain(act, own_a)
            act.wait_ge(normed, 1)
            for i in range(NT):
                act.activation(XN[:, i, :], XL[:, i, :], ACT.Square, accum_out=ms[:, i:i + 1]).then_inc(squared, 1)
            for g in range(KD * B):
                act.wait_ge(xT_done, g + 1)
                k, b = divmod(g, B)
                act.activation(XT[:, k, b * S:(b + 1) * S], PS[:, g, :], ACT.Identity,
                               accum_out=xsum[:, k, b:b + 1]).then_inc(xT_ready, 1)
            act.wait_ge(small_in, 16 * NSMALL)
            act.activation(negA[:, :], hp[:, 1:2], ACT.Exp).then_inc(negA_ready, 1)
            for n, (what, _, rows, m) in enumerate(mtiles):
                for b in range(B):
                    j = 2 * n + b
                    act.wait_ge(proj_done, j + 1)
                    src = PS[0:rows, 4 + j % 4, :]
                    if what == "dt":
                        dst = dtr[:, b * S:(b + 1) * S]
                        act.activation(dst, src, ACT.Identity, bias=hp[:, 0:1]).then_inc(proj_taken, 1)
                    elif what == "z":
                        act.activation(SZ[:, m, b * S:(b + 1) * S], src, ACT.Silu).then_inc(proj_taken, 1)
                    else:
                        k = n - 1
                        if b == 0 and k >= 2:
                            act.wait_ge(conv_ready, k - 1)
                        if k == 0 and b == 0:
                            act.wait_ge(padded, 1)
                        act.activation(XC[k % 2][0:rows, b, PAD:PAD + S], src, ACT.Copy).then_inc(proj_taken, 1)
                if what == "dt":
                    act.wait_ge(proj_taken, 2)
                    c.link(act.activation(ab[:, :], dtr[:, :], ACT.Abs))
                    c.link(act.activation(dt[:, :], ab[:, :], ACT.Exp, scale=-1.0))
                    act.activation(sp[:, :], dt[:, :], ACT.Ln, bias=1.0).then_inc(sp_ready, 1)
                if n == 1:
                    act.wait_ge(hid_mm, 1)
                    act.activation(hid[:, :], PS[0:32, 0, 0:B], ACT.Silu, bias=rb1[:, 0:1],
                                   scale=1.0 / S).then_inc(hid_ready, 1)
                if n >= 2:
                    silu_of(act, n - 2)
            act.wait_ge(lg_ready, 1)
            act.activation(pr[:, :, :], lg[:, :, :], ACT.Exp).then_inc(lg_ready, 1)

            for n in range(B * TB):
                b, s = divmod(n, TB)
                act.wait_ge(g_mm, n + 1)
                o, m = s * (BANK + P), S - s * P
                act.activation(GT[:, b, o:o + m], PS[:, 4 + n % 2, s * P:S], ACT.Copy).then_inc(g_copied, 1)

            for n in range(B * HEADS):
                b, h = divmod(n, HEADS)
                e = E[n % 2]
                act.wait_ge(diag_ready, n + 1)
                if n >= 2:
                    act.wait_ge(w_ready, n - 1)
                for s in range(TB - 1):
                    o, m = s * BANK + (s + 1) * P, S - (s + 1) * P
                    act.activation(e[:, o:o + m], PS[:, n % 2, (s + 1) * P:S], ACT.Exp,
                                   bias=TD[:, 1, b * TB + s, h:h + 1])
                act.activation(e[:, :].rearrange("p (s c) -> p s c", s=TB)[:, :, 0:P], Lm[n % 2][:, :, :],
                               ACT.Exp).then_inc(e_ready, 1)
            for n in range(B * MX):
                b, m = divmod(n, MX)
                act.wait_ge(yg_ready, n + 1)
                cols = slice(b * S, (b + 1) * S)
                act.activation(SQ[:, m, cols], YG[:, m, cols], ACT.Square).then_inc(sq_ready, 1)

        @block.tensor
        def _(pe):
            pe.wait_ge(small_in, 16 * NSMALL)
            pe.wait_ge(xn_ready, NT)
            transposes_tensor(pe, PS, XN, ident, xT_done)
            pe.wait_ge(w_in_in, 16)
            for n, (what, col, rows, m) in enumerate(mtiles):
                for b in range(B):
                    j = 2 * n + b
                    pe.wait_ge(xT_ready, KD * B)
                    if j >= 4:
                        pe.wait_ge(proj_taken, j - 3)
                    for k in range(KD):
                        last = pe.matmul(PS[0:rows, 4 + j % 4, :], w_in[:, k, col:col + rows],
                                         XT[:, k, b * S:(b + 1) * S], start=(k == 0), stop=(k == KD - 1))
                    last.then_inc(proj_done, 1)
                if n == 0:
                    for k in range(KD):
                        last = pe.matmul(PS[0:32, 0, 0:B], rw1[:, k, :], xsum[:, k, :], start=(k == 0),
                                         stop=(k == KD - 1))
                    last.then_inc(hid_mm, 1)
                if n == 3:
                    pe.wait_ge(hidB_ready, 1)
                    for b in range(B):
                        last = pe.matmul(PS[:, 1, 3 * b:3 * b + 3], hidB[:, b, :], rw2[:, :], start=True, stop=True)
                    last.then_inc(lg_mm, 1)
                if n == 4:
                    pe.wait_ge(La_ready, 1)
                    for a, src in enumerate((dt, La)):
                        for i in range(NT):
                            o = (a * NT + i) * HEADS
                            last = pe.transpose(PS[:, 2, o:o + HEADS], src[:, i * P:(i + 1) * P],
                                                ident[0:HEADS, 0:HEADS])
                    last.then_inc(td_mm, 1)
            pe.wait_ge(silu_ready, 2)
            pe.wait_ge(td_ready, 1)
            pe.wait_ge(lg_ready, 1)
            pe.wait_ge(proj_taken, 2 * len(mtiles))
            for n in range(B * TB):
                b, s = divmod(n, TB)
                if n >= 2:
                    pe.wait_ge(g_copied, n - 1)
                pe.matmul(PS[:, 4 + n % 2, s * P:S], BC[:, 0, b * S + s * P:b * S + (s + 1) * P],
                          BC[:, 1, b * S + s * P:(b + 1) * S], start=True, stop=True).then_inc(g_mm, 1)
            pe.wait_ge(silu_ready, len(convs))
            for i in range(NT):
                if i >= 2:
                    pe.wait_ge(xd_ready, i - 1)
                for m in range(MX):
                    last = pe.transpose(PS[:, 6 + i % 2, m * P:(m + 1) * P], XH[:, m, i * P:(i + 1) * P], ident[:, :])
                last.then_inc(xh_mm, 1)

            def decay(n):
                b, h = divmod(n, HEADS)
                if n >= 2:
                    pe.wait_ge(e_ready, n - 1)
                pe.matmul(PS[:, n % 2, :], sel[:, h, :], La[:, b * S:(b + 1) * S], start=True,
                          stop=True).then_inc(decay_mm, 1)

            decay(0)
            decay(1)
            pe.wait_ge(xd_ready, NT)
            for n in range(B * HEADS):
                b, h = divmod(n, HEADS)
                half = slice((h % 2) * HD, (h % 2 + 1) * HD)
                pe.wait_ge(w_ready, n + 1)
                if n >= 4 and n % 2 == 0:
                    pe.wait_ge(yg_ready, n // 2 - 1)
                for s in range(TB):
                    o, m = s * BANK + s * P, S - s * P
                    last = pe.matmul(PS[half, 2 + (n // 2) % 2, s * P:S], XD[:, b * TB + s, h * HD:(h + 1) * HD],
                                     W[n % 2][:, o:o + m], start=(s == 0), stop=(s == TB - 1),
                                     skip_group_check=True)
                last.then_inc(y_mm, 1)
                if n + 2 < B * HEADS:
                    decay(n + 2)
            pe.wait_ge(sq_ready, B * MX)
            for i in range(NT):
                for m in range(MX):
                    last = pe.matmul(PS[:, 6, i:i + 1], SQ[:, m, i * P:(i + 1) * P], ones[:, 0:1],
                                     start=(m == 0), stop=(m == MX - 1))
            last.then_inc(ss_mm, 1)
            pe.wait_ge(w_out_in, 16)
            pe.wait_ge(yw_ready, 1)
            for i in range(NT):
                if i >= 4:
                    pe.wait_ge(out_taken, i - 3)
                for m in range(MX):
                    last = pe.matmul(PS[:, i % 4, 0:D], YW[:, m, i * P:(i + 1) * P], w_out[:, m, :],
                                     start=(m == 0), stop=(m == MX - 1))
                last.then_inc(out_mm, 1)


HEADS, HD = 16, 16
GH = 4
NG = HEADS // GH
UNITS = B * NG
VW = 32
Q_PARTS = (0, 0, 1, 1, 0, 2)
K_PARTS = (0, 1, 0, 1, 2, 0)
NBLK = len(Q_PARTS)
TAIL = NBLK * HD
MASKED = 2.0 ** 32


class Attention:

    def __init__(self, nc, ctx, stage, PS, name, NK, KH, loads, ident, identb):
        def sb(n, shape, dt=F32):
            return stage.enter_context(nc.sbuf_tensor(name + n, shape, dt))

        def sem(n):
            return ctx.enter_context(nc.semaphore(name + n))

        assert loads % 3 == 0
        self.PS, self.ident, self.identb = PS, ident, identb
        self.NK, self.KT, self.C, self.KH, self.loads = NK, NK // P, TB * NK // BANK, KH, loads
        self.Qs = [sb(f"Qs{n}", [P, GH, S], BF16) for n in range(3)]
        self.Ks = [sb(f"Ks{n}", [P, KH, NK], BF16) for n in range(3)]
        self.Vs = [sb(f"Vs{n}", [P, NK // P, KH, VW]) for n in range(3)]
        self.qtail = sb("qtail", [P, GH, S], BF16)
        self.E = [sb(f"E{n}", [P, GH, S]) for n in range(2)]
        self.mx = sb("mx", [P, TB, GH, 2])
        self.m = sb("m", [P, TB, GH])
        self.MT = sb("MT", [P, TB, GH, VW], BF16)
        self.Oraw = sb("Oraw", [P, S])
        self.rc = sb("rc", [P, TB, GH])
        self.Otok = sb("Otok", [P, UNITS, TB, GH * HD])
        self.loaded = [sem(f"loaded{n}") for n in range(3)]
        (self.s_done, self.max_done, self.m_ready, self.mT_done, self.q_ready,
         self.st_done, self.exp_done, self.av_done, self.o_copied, self.oT_done, self.o_normed, self.own) = (
            sem(n) for n in ("s_done", "max_done", "m_ready", "mT_done", "q_ready",
                             "st_done", "exp_done", "av_done", "o_copied", "oT_done", "o_normed", "own"))
        self.m_final, self.mt_set = sem("m_final"), sem("mt_set")

    def steps(self, eng, step):
        step(0, 0, first=True)
        with eng.Fori(0, (UNITS - 2) // 3) as i:
            for n in range(1, 4):
                step(i * 3 + n, n % 3)
        step(UNITS - 1, (UNITS - 1) % 3, last=True)

    def sync(self, sp, load):
        for u in range(2):
            load(u, u)
        with sp.Fori(0, (UNITS - 2) // 3) as i:
            for n in range(2, 5):
                u = i * 3 + n
                sp.wait_ge(self.st_done, (u - 2) * (2 * self.KT) + 1)
                load(u, n % 3)

    def tensor(self, pe):
        PS, KT, C = self.PS, self.KT, self.C

        def scores(u, buf, c, p, first=False):
            qt, half = divmod(c, C // TB)
            if c == 0 and p == 0:
                pe.wait_ge(self.loaded[buf], 16 * self.loads // 3 * (u - buf + 3))
            if not (first and c == 0 and p == 0):
                pe.wait_ge(self.max_done, u * (2 * C) + (2 * c + p))
            for j in (2 * p, 2 * p + 1):
                last = pe.matmul(PS[:, j % 2, :], self.Qs[buf][:, j, qt * P:(qt + 1) * P],
                                 self.Ks[buf][:, j % self.KH, half * BANK:(half + 1) * BANK],
                                 start=True, stop=True)
            last.then_inc(self.s_done, 1)

        def transposed_scores(u, buf, kt, p, first):
            if kt == 0 and p == 0:
                pe.wait_ge(self.q_ready, u * 2 + 2)
            if not (first and kt == 0):
                pe.wait_ge(self.exp_done, u * (2 * KT) + (2 * kt + p - 1))
            for j in (2 * p, 2 * p + 1):
                last = pe.matmul(PS[:, 2 + j, :], self.Ks[buf][:, j % self.KH, kt * P:(kt + 1) * P],
                                 self.Qs[buf][:, j, :], start=True, stop=True)
            last.then_inc(self.st_done, 1)

        def values(u, buf, kt, first=False):
            pe.wait_ge(self.exp_done, u * (2 * KT) + (2 * kt + 2))
            if kt == 0:
                if not first:
                    pe.wait_ge(self.o_copied, u)
            for j in range(GH):
                last = pe.matmul(PS[32 * j:32 * j + 32, 6, :], self.Vs[buf][:, kt, j % self.KH, :],
                                 self.E[kt % 2][:, j, :], start=(kt == 0), stop=(kt == KT - 1),
                                 skip_group_check=True)
            last.then_inc(self.av_done, 1)

        def maxima_transposes(u, first=False):
            pe.wait_ge(self.m_ready, u + 1)
            for qt in range(TB):
                last = pe.transpose(PS[:, 7, :].bitcast(BF16)[:, qt * P:(qt + 1) * P],
                                    self.MT[:, qt, :, :].rearrange("p j c -> p (j c)"), self.identb[:, :])
            last.then_inc(self.mT_done, 1)

        def output_transposes(u):
            pe.wait_ge(self.o_copied, u + 1)
            for qt in range(TB):
                last = pe.transpose(PS[:, 7, qt * P:(qt + 1) * P], self.Oraw[:, qt * P:(qt + 1) * P],
                                    self.ident[:, :])
            last.then_inc(self.oT_done, 1)

        def step(u, buf, first=False, last=False):
            for kt in range(KT):
                if not last:
                    scores(u + 1, (buf + 1) % 3, kt, 0)
                if kt > 0:
                    values(u, buf, kt - 1, first)
                elif not first:
                    values(u - 1, (buf + 2) % 3, KT - 1)
                transposed_scores(u, buf, kt, 0, first)
                if not last:
                    scores(u + 1, (buf + 1) % 3, kt, 1)
                transposed_scores(u, buf, kt, 1, first)
                if kt == 1 and not first:
                    output_transposes(u - 1)
            if not last:
                if not first:
                    pe.wait_ge(self.o_normed, u)
                maxima_transposes(u + 1)

        for c in range(C):
            for p in range(2):
                scores(0, 0, c, p, first=True)
        maxima_transposes(0, first=True)
        self.steps(pe, step)
        values(UNITS - 1, (UNITS - 1) % 3, KT - 1)
        pe.wait_ge(self.o_normed, UNITS - 1)
        output_transposes(UNITS - 1)

    def vector(self, dve):
        PS, C = self.PS, self.C

        def maxima(u, buf, c):
            qt, half = divmod(c, C // TB)
            for p in range(2):
                dve.wait_ge(self.s_done, u * (2 * C) + (2 * c + p + 1))
                dve.tensor_reduce(self.mx[:, qt, 2 * p:2 * p + 2, half], PS[:, 0:2, :], AX.X,
                                  ALU.max).then_inc(self.max_done, 1)

        def negated(u, first=False):
            dve.wait_ge(self.max_done, (u + 1) * (2 * C))
            if C > TB:
                dve.tensor_tensor(self.m[:, :, :], self.mx[:, :, :, 0], self.mx[:, :, :, 1],
                                  ALU.max).then_inc(self.m_final, 1)
            else:
                dve.tensor_copy(self.m[:, :, :], self.mx[:, :, :, 0]).then_inc(self.m_final, 1)
            dve.wait_ge(self.m_final, u * 2 + 1)
            if not first:
                dve.wait_ge(self.mT_done, u)
            dve.tensor_scalar(self.MT[:, :, :, 0], self.m[:, :, :], -1.0, None, ALU.mult).then_inc(self.m_final, 1)
            dve.wait_ge(self.m_final, u * 2 + 2)
            dve.scalar_tensor_tensor(out=self.MT[:, :, :, 1], in0=self.m[:, :, :], scalar=-1.0,
                                     in1=self.MT[:, :, :, 0], op0=ALU.mult,
                                     op1=ALU.subtract).then_inc(self.m_ready, 1)

        def tails(u, buf):
            dve.wait_ge(self.mT_done, u + 1)
            for j in (2, 3):
                last = dve.tensor_copy(self.Qs[buf][TAIL:P, j, :],
                                       PS[32 * j:32 * j + 32, 7, :].bitcast(BF16)[:, 0:S])
            last.then_inc(self.q_ready, 1)

        def normalise(u):
            src = PS[:, 7, :].rearrange("p (t j c) -> p t j c", t=TB, j=GH)
            dve.wait_ge(self.oT_done, u + 1)
            dve.reciprocal(self.rc[:, :, :], src[:, :, :, HD]).then_inc(self.own, 1)
            dve.wait_ge(self.own, u + 1)
            for qt in range(TB):
                last = dve.tensor_tensor(
                    self.Otok[:, bass.ds(u, 1), qt, :]
                    .rearrange("p u (j c) -> p (u j) c", j=GH),
                    src[:, qt, :, 0:HD], self.rc[:, qt, :].unsqueeze(2).to_broadcast([P, GH, HD]), ALU.mult)
            last.then_inc(self.o_normed, 1)

        def step(u, buf, first=False, last=False):
            if not last:
                for c in range(2):
                    maxima(u + 1, (buf + 1) % 3, c)
            if not first:
                normalise(u - 1)
            if not last:
                for c in range(2, C):
                    maxima(u + 1, (buf + 1) % 3, c)
                negated(u + 1)
                tails(u + 1, (buf + 1) % 3)

        dve.memset(self.MT[:, :, :, :], 0.0).then_inc(self.mt_set, 1)
        dve.wait_ge(self.mt_set, 1)
        dve.memset(self.MT[:, :, :, 2], 1.0).then_inc(self.mt_set, 1)
        dve.wait_ge(self.mt_set, 2)
        for c in range(C):
            maxima(0, 0, c)
        negated(0, first=True)
        tails(0, 0)
        self.steps(dve, step)
        normalise(UNITS - 1)

    def scalar(self, act):
        PS, KT = self.PS, self.KT

        def tails(u, buf):
            act.wait_ge(self.mT_done, u + 1)
            for j in (0, 1):
                last = act.activation(self.Qs[buf][TAIL:P, j, :],
                                      PS[32 * j:32 * j + 32, 7, :].bitcast(BF16)[:, 0:S], ACT.Copy)
            last.then_inc(self.q_ready, 1)

        def copy_output(u, last=False):
            act.wait_ge(self.av_done, (u + 1) * KT)
            if last:
                act.wait_ge(self.oT_done, u)
            else:
                act.wait_ge(self.mT_done, u + 2)
            act.activation(self.Oraw[:, :], PS[:, 6, :], ACT.Copy).then_inc(self.o_copied, 1)

        def step(u, buf, first=False, last=False):
            for kt in range(KT):
                for p in range(2):
                    act.wait_ge(self.st_done, u * (2 * KT) + (2 * kt + p + 1))
                    if not (first and kt < 2):
                        act.wait_ge(self.av_done, u * KT + (kt - 1))
                    act.activation(self.E[kt % 2][:, 2 * p:2 * p + 2, :], PS[:, 2 + 2 * p:4 + 2 * p, :],
                                   ACT.Exp, scale=0.25).then_inc(self.exp_done, 1)
                if kt == 0 and not first:
                    copy_output(u - 1)
            if not last:
                tails(u + 1, (buf + 1) % 3)

        tails(0, 0)
        self.steps(act, step)
        copy_output(UNITS - 1, last=True)


class Splitter:

    def __init__(self, nc, ctx, stage, name, dst, rows, n):
        self.F = [stage.enter_context(nc.sbuf_tensor(f"{name}F{i}", [P, BANK], F32)) for i in range(2)]
        self.R = [stage.enter_context(nc.sbuf_tensor(f"{name}R{i}", [P, BANK], F32)) for i in range(2)]
        self.dst, self.rows, self.n = dst, rows, n
        self.f_ready, self.p0_ready, self.r_ready, self.p1_ready, self.p2_ready = (
            ctx.enter_context(nc.semaphore(f"{name}{s}"))
            for s in ("f_ready", "p0_ready", "r_ready", "p1_ready", "p2_ready"))

    def buffer(self, dve, n):
        if n >= 2:
            dve.wait_ge(self.r_ready, n - 1)
        return self.F[n % 2][0:self.rows[n], :]

    def scalar(self, act, lo, hi, before=None):
        for n in range(lo, hi + 1):
            if n < hi:
                if before:
                    before(n)
                act.wait_ge(self.f_ready, n + 1)
                act.activation(self.dst(n, 0), self.F[n % 2][0:self.rows[n], :], ACT.Copy).then_inc(self.p0_ready, 1)
            if n > lo:
                act.wait_ge(self.r_ready, n)
                act.activation(self.dst(n - 1, 1), self.R[(n - 1) % 2][0:self.rows[n - 1], :],
                               ACT.Copy).then_inc(self.p1_ready, 1)

    def gpsimd(self, pool, lo, hi):
        for n in range(lo, hi):
            f, r = self.F[n % 2][0:self.rows[n], :], self.R[n % 2][0:self.rows[n], :]
            pool.wait_ge(self.p0_ready, n + 1)
            if n >= 2:
                pool.wait_ge(self.p2_ready, n - 1)
            pool.tensor_tensor(r, f, self.dst(n, 0), ALU.subtract).then_inc(self.r_ready, 1)
            pool.wait_ge(self.p1_ready, n + 1)
            pool.tensor_tensor(self.dst(n, 2), r, self.dst(n, 1), ALU.subtract).then_inc(self.p2_ready, 1)


def load_unit(sp, at, q_parts, k_parts, k_tail, values):
    def load(u, buf):
        done = at.loaded[buf]
        for blk in range(NBLK):
            rows = slice(blk * HD, (blk + 1) * HD)
            k = k_parts[K_PARTS[blk], bass.ds(u, 1), :, :]
            q = q_parts[Q_PARTS[blk], bass.ds(u, 1), :, :]
            sp.dma_start(at.Ks[buf][rows, :, :], k.rearrange("u (h d) n -> d (u h) n", d=HD)).then_inc(done, 16)
            sp.dma_start(at.Qs[buf][rows, :, :], q.rearrange("u (h d) n -> d (u h) n", d=HD)).then_inc(done, 16)
        for h in range(at.KH):
            sp.dma_start(at.Ks[buf][TAIL:P, h, :],
                         k_tail[bass.ds(u, 1), :, :].rearrange("u r n -> (u r) n")).then_inc(done, 16)
        sp.dma_start(at.Qs[buf][TAIL:P, :, :], at.qtail[TAIL:P, :, :]).then_inc(done, 16)
        sp.dma_start(at.Vs[buf][:, :, :, :],
                     values[:, bass.ds(u, 1), :, :, :].rearrange("p u t h c -> p (u t) h c")).then_inc(done, 16)
    return load


def project_out(nc, at, sh, sem, w, w_in, w_val):
    PS, X, XT = sh.PS, sh.X, sh.XT
    oT_done, oT_ready, out_mm = sem("po_oT_done"), sem("po_oT_ready"), sem("po_out_mm")
    out_taken, o_placed = sem("po_out_taken"), sem("po_o_placed")

    def tensor(pe):
        pe.wait_ge(o_placed, B)
        for k in range(KD):
            for b in range(B):
                for qt in range(TB):
                    last = pe.transpose(PS[:, 2 * k + b, qt * P:(qt + 1) * P], sh.XN[:, b * TB + qt, k * P:(k + 1) * P],
                                        sh.ident[:, :])
                last.then_inc(oT_done, 1)
        pe.wait_ge(oT_ready, KD * B)
        pe.wait_ge(w_in, w_val)
        for i in range(NT):
            if i >= 4:
                pe.wait_ge(out_taken, i - 3)
            for k in range(KD):
                last = pe.matmul(PS[:, 4 + i % 4, 0:D], XT[:, k, i * P:(i + 1) * P], w[:, k, :],
                                 start=(k == 0), stop=(k == KD - 1))
            last.then_inc(out_mm, 1)

    def scalar(act):
        for g in range(KD * B):
            k, b = divmod(g, B)
            act.wait_ge(oT_done, g + 1)
            act.activation(XT[:, k, b * S:(b + 1) * S], PS[:, g, :], ACT.Copy).then_inc(oT_ready, 1)

    def vector(dve):
        dve.wait_ge(at.o_normed, UNITS)
        for b in range(B):
            dve.tensor_copy(sh.XN[:, b * TB:(b + 1) * TB, :].rearrange("p t (g c) -> p g t c", g=NG),
                            at.Otok[:, b * NG:(b + 1) * NG, :, :]).then_inc(o_placed, 1)
        for i in range(NT):
            dve.wait_ge(out_mm, i + 1)
            dve.tensor_tensor(X[:, i, :], X[:, i, :], PS[:, 4 + i % 4, 0:D], ALU.add).then_inc(out_taken, 1)

    return tensor, scalar, vector


class Norm:

    def __init__(self, nc, ctx, stage, sh, name, eps=1e-05):
        def sb(n, shape):
            return stage.enter_context(nc.sbuf_tensor(name + n, shape, F32))
        self.sh, self.eps = sh, eps
        self.st6, self.mv, self.rstd = sb("st6", [P, NT, 6]), sb("mv", [P, NT, 2]), sb("rstd", [P, NT])
        self.own, self.var_ready, self.eps_added, self.rstd_ready, self.xn_ready, self.xT_done, self.xT_ready = (
            ctx.enter_context(nc.semaphore(name + n))
            for n in ("own", "var_ready", "eps_added", "rstd_ready", "xn_ready", "xT_done", "xT_ready"))

    def vector(self, dve):
        c = Chain(dve, self.own)
        layernorm_vector(dve, c.link, self.sh.X, self.sh.XN, self.st6, self.mv, self.rstd,
                         self.var_ready, self.rstd_ready).then_inc(self.xn_ready, 1)

    def gpsimd(self, pool):
        pool.wait_ge(self.var_ready, 1)
        pool.tensor_scalar(self.rstd[:, :], self.mv[:, :, 1], self.eps, None, ALU.add).then_inc(self.eps_added, 1)
        pool.wait_ge(self.eps_added, 1)
        pool.tensor_tensor(self.rstd[:, :], self.rstd[:, :], self.sh.mhalf[:, :], ALU.pow).then_inc(self.rstd_ready, 1)

    def tensor(self, pe):
        pe.wait_ge(self.xn_ready, 1)
        transposes_tensor(pe, self.sh.PS, self.sh.XN, self.sh.ident, self.xT_done)

    def scalar(self, act):
        for g in range(KD * B):
            k, b = divmod(g, B)
            act.wait_ge(self.xT_done, g + 1)
            act.activation(self.sh.XT[:, k, b * S:(b + 1) * S], self.sh.PS[:, g, :], ACT.Copy).then_inc(self.xT_ready, 1)


def cross_stage(nc, ctx, sh, A):
    NK = 1024
    PS, X, XN, XT = sh.PS, sh.X, sh.XN, sh.XT
    stage = ExitStack()

    def sb(name, shape, dt=F32):
        return stage.enter_context(nc.sbuf_tensor("c_" + name, shape, dt))

    def sem(name):
        return ctx.enter_context(nc.semaphore("c_" + name))

    early = ExitStack()

    def sbe(name, shape, dt=F32):
        return early.enter_context(nc.sbuf_tensor("c_" + name, shape, dt))

    nm = Norm(nc, ctx, stage, sh, "c_n")
    wo, bo = sb("wo", [P, KD, D]), sb("bo", [P, D])
    VB = sb("VB", [P, UNITS, NK // P, GH, VW])
    at = Attention(nc, ctx, stage, PS, "c_a", NK, GH, 2 * NBLK + GH + 2, sh.ident, sh.identb)
    ctxT = sbe("ctxT", [P, KD, B * NK])
    wq, wk, wv = (sbe(n, [P, KD, D]) for n in ("wq", "wk", "wv"))
    bq, bk = sbe("bq", [P, KD]), sbe("bk", [P, KD])
    bv = sbe("bv", [P, D])
    maski = at.E[0][:, :, :].rearrange("p j s -> p (j s)").bitcast(I32).rearrange("p (b n) -> p b n", b=B)
    ind = sbe("ind", [P, B, NK])
    ktc = sbe("ktc", [32, 2])
    ktail = sbe("ktail", [32, B, NK], BF16)
    KP = [sbe(f"KP{n}", [P, NK], BF16) for n in range(6)]
    QP = [sbe(f"QP{n}", [P, KD, T], BF16) for n in range(3)]
    q_parts = nc.dram_tensor("c_q_parts", [3, UNITS, GH * HD, S], BF16, kind="Internal").ap()
    k_parts = nc.dram_tensor("c_k_parts", [3, UNITS, GH * HD, NK], BF16, kind="Internal").ap()
    k_tail = nc.dram_tensor("c_k_tail", [UNITS, 32, NK], BF16, kind="Internal").ap()

    small_in, ctx_in, wv_in, wo_in, mask_in = (sem(n) for n in ("small_in", "ctx_in", "wv_in", "wo_in", "mask_in"))
    proj_done, proj_taken = sem("proj_done"), sem("proj_taken")
    ind_ready, tail_ready, k_stored, q_stored, tail_stored = (
        sem(n) for n in ("ind_ready", "tail_ready", "k_stored", "q_stored", "tail_stored"))
    v_ones, xb_ready, qtail_set = sem("v_ones"), sem("xb_ready"), sem("qtail_set")
    NKC = B * KD * 2
    NV = B * NK // P
    NQC = B * KD

    def k_chunk(n):
        return n // 4, n // 2 % 2, n % 2

    def dst(n, part):
        if n < NKC:
            b, m, half = k_chunk(n)
            return KP[3 * (n // 2 % 2) + part][:, half * BANK:(half + 1) * BANK]
        b, m = divmod(n - NKC, KD)
        return QP[part][:, m, b * S:(b + 1) * S]

    sp_l = Splitter(nc, ctx, early, "c_s", dst, [P] * (NKC + NQC), NKC + NQC)
    po_t, po_s, po_v = project_out(nc, at, sh, sem, wo, wo_in, 16)

    with stage, early, nc.Block() as block:

        @block.sync
        def _(sp):
            for n, (d, s) in enumerate(((wk, "c_wk"), (bk, "c_bk"), (ktc, "c_ktc"), (bq, "c_bq"), (bv, "c_bv"),
                                        )):
                sp.dma_start(d[tuple(slice(None) for _ in d.shape)], A[s]).then_inc(small_in, 16)
            for b in range(B):
                sp.dma_start(ctxT[:, :, b * NK:(b + 1) * NK], A["ctxT"][:, :, b * NK:(b + 1) * NK]).then_inc(ctx_in, 16)
            sp.dma_start(maski, A["mask"].unsqueeze(0).to_broadcast([P, B, NK])).then_inc(mask_in, 16)
            sp.dma_start(wv[:, :, :], A["c_wv"]).then_inc(wv_in, 16)
            sp.dma_start(wq[:, :, :], A["c_wq"]).then_inc(wv_in, 16)
            sp.dma_start(wo[:, :, :], A["c_wo"]).then_inc(wo_in, 16)
            sp.dma_start(bo[:, :], A["c_bo"]).then_inc(wo_in, 16)
            sp.wait_ge(tail_ready, B)
            for u in range(UNITS):
                sp.dma_start(k_tail[u], ktail[:, u // NG, :]).then_inc(tail_stored, 16)
            for n in range(1, NKC, 2):
                b, m, _ = k_chunk(n)
                sp.wait_ge(sp_l.p2_ready, n + 1)
                for part in range(3):
                    sp.dma_start(k_parts[part, b * NG + 2 * m:b * NG + 2 * m + 2].rearrange("u r n -> (u r) n"),
                                 KP[3 * (n // 2 % 2) + part][:, :]).then_inc(k_stored, 16)
            for n in range(NQC):
                b, m = divmod(n, KD)
                sp.wait_ge(sp_l.p2_ready, NKC + n + 1)
                for part in range(3):
                    sp.dma_start(q_parts[part, b * NG + 2 * m:b * NG + 2 * m + 2].rearrange("u r n -> (u r) n"),
                                 QP[part][:, m, b * S:(b + 1) * S]).then_inc(q_stored, 16)
            sp.wait_ge(tail_stored, 16 * UNITS)
            sp.wait_ge(k_stored, 16 * 3 * NKC // 2)
            sp.wait_ge(q_stored, 16 * 3 * NQC)
            sp.wait_ge(qtail_set, 2)
            sp.wait_ge(proj_taken, NV)
            at.sync(sp, load_unit(sp, at, q_parts, k_parts, k_tail, VB))

        @block.gpsimd
        def _(pool):
            pool.memset(VB[:, :, :, :, :], 1.0).then_inc(v_ones, 1)
            nm.gpsimd(pool)
            pool.memset(at.qtail[:, :, :], 0.0).then_inc(qtail_set, 1)
            pool.wait_ge(small_in, 16 * 5)
            pool.wait_ge(qtail_set, 1)
            pool.tensor_scalar(at.qtail[TAIL:P, :, :], at.qtail[TAIL:P, :, :], sh.row98[TAIL:P, 0:1], None,
                               ALU.add).then_inc(qtail_set, 1)
            pool.wait_ge(qtail_set, 2)
            sp_l.gpsimd(pool, 0, NKC + NQC)
            pool.wait_ge(wo_in, 32)
            pool.wait_ge(nm.xn_ready, 1)
            for i in range(NT):
                last = pool.tensor_tensor(X[:, i, :], X[:, i, :], bo[:, :], ALU.add)
            last.then_inc(xb_ready, 1)
        @block.vector
        def _(dve):
            nm.vector(dve)
            dve.wait_ge(mask_in, 16)
            dve.tensor_scalar(ind[:, :, :], maski, 0.0, None, ALU.not_equal).then_inc(ind_ready, 1)
            dve.wait_ge(ind_ready, 1)
            dve.wait_ge(small_in, 16 * 5)
            for b in range(B):
                dve.tensor_scalar(ktail[:, b, :], ind[0:32, b, :], ktc[:, 0:1], ktc[:, 1:2], ALU.mult,
                                  ALU.add).then_inc(tail_ready, 1)
            for n in range(NKC):
                b, m, half = k_chunk(n)
                dve.wait_ge(proj_done, n + 1)
                f = sp_l.buffer(dve, n)
                dve.scalar_tensor_tensor(out=f, in0=PS[:, 4 + n % 4, :], scalar=bk[:, m:m + 1],
                                         in1=ind[:, b, half * BANK:(half + 1) * BANK], op0=ALU.add,
                                         op1=ALU.mult).then_inc(sp_l.f_ready, 1)
            dve.wait_ge(v_ones, 1)
            for t in range(NV):
                n = NKC + t
                b, kt = divmod(t, NK // P)
                dve.wait_ge(proj_done, n + 1)
                dve.tensor_tensor(VB[:, b * NG:(b + 1) * NG, kt, :, 0:HD],
                                  PS[:, 4 + n % 4, 0:D].rearrange("p (g h c) -> p g h c", g=NG, h=GH),
                                  bv[:, :].rearrange("p (g h c) -> p g h c", g=NG, h=GH),
                                  ALU.add).then_inc(proj_taken, 1)
            for n in range(NKC, NKC + NQC):
                b, m = divmod(n - NKC, KD)
                j = n + NV
                dve.wait_ge(proj_done, j + 1)
                f = sp_l.buffer(dve, n)
                dve.tensor_scalar(f, PS[:, 4 + j % 4, :], bq[:, m:m + 1], None, ALU.add).then_inc(sp_l.f_ready, 1)
            at.vector(dve)
            dve.wait_ge(xb_ready, 1)
            po_v(dve)

        @block.scalar
        def _(act):
            sp_l.scalar(act, 0, NKC, before=lambda n: act.wait_ge(k_stored, 16 * 3 * (n // 2 - 1))
                        if n >= 4 and n % 2 == 0 else None)
            nm.scalar(act)
            sp_l.scalar(act, NKC, NKC + NQC)
            at.scalar(act)
            po_s(act)

        @block.tensor
        def _(pe):
            pe.wait_ge(small_in, 16 * 5)

            def bank_free(j):
                o = j - 4
                if o < 0:
                    return
                if o < NKC:
                    pe.wait_ge(sp_l.f_ready, o + 1)
                elif o < NKC + NV:
                    pe.wait_ge(proj_taken, o - NKC + 1)
                else:
                    pe.wait_ge(sp_l.f_ready, o - NV + 1)

            for n in range(NKC):
                b, m, half = k_chunk(n)
                pe.wait_ge(ctx_in, 16 * B)
                bank_free(n)
                for k in range(KD):
                    c0 = b * NK + half * BANK
                    last = pe.matmul(PS[:, 4 + n % 4, :], wk[:, k, m * P:(m + 1) * P], ctxT[:, k, c0:c0 + BANK],
                                     start=(k == 0), stop=(k == KD - 1))
                last.then_inc(proj_done, 1)
            pe.wait_ge(wv_in, 32)
            for t in range(NV):
                j = NKC + t
                bank_free(j)
                for k in range(KD):
                    last = pe.matmul(PS[:, 4 + j % 4, 0:D], ctxT[:, k, t * P:(t + 1) * P], wv[:, k, :],
                                     start=(k == 0), stop=(k == KD - 1))
                last.then_inc(proj_done, 1)
            nm.tensor(pe)
            pe.wait_ge(nm.xT_ready, KD * B)
            for n in range(NQC):
                b, m = divmod(n, KD)
                j = NKC + NV + n
                bank_free(j)
                for k in range(KD):
                    last = pe.matmul(PS[:, 4 + j % 4, :], wq[:, k, m * P:(m + 1) * P], XT[:, k, b * S:(b + 1) * S],
                                     start=(k == 0), stop=(k == KD - 1))
                last.then_inc(proj_done, 1)
            pe.wait_ge(sp_l.f_ready, NKC + NQC)
            at.tensor(pe)
            po_t(pe)


def shared_kv_stage(nc, ctx, sh, A):
    H, DK = 8, 128
    UN = B * H
    G = UN * TB
    LAG = 2
    PS, X, XN, XT = sh.PS, sh.X, sh.XN, sh.XT
    stage = ExitStack()

    def sb(name, shape, dt=F32):
        return stage.enter_context(nc.sbuf_tensor("s_" + name, shape, dt))

    def sem(name):
        return ctx.enter_context(nc.semaphore("s_" + name))

    nm = Norm(nc, ctx, stage, sh, "s_n")
    wq, wo = sb("wq", [P, H, KD, DK]), sb("wo", [P, H, D])
    wk, wv = sb("wk", [P, KD, DK]), sb("wv", [P, KD, DK])
    KTr, V = sb("KT", [P, T]), sb("V", [P, NT, DK])
    QT = [sb(f"QT{n}", [P, S]) for n in range(2)]
    NPB = 4
    Pr = [sb(f"Pr{n}", [P, S]) for n in range(NPB)]
    Pn = [sb(f"Pn{n}", [P, S]) for n in range(NPB)]
    mx, nmx, sm, rs = (sb(n, [P, NPB]) for n in ("mx", "nmx", "sm", "rs"))
    PT = [sb(f"PT{n}", [P, TB, S]) for n in range(2)]
    OT = [sb(f"OT{n}", [P, S]) for n in range(2)]

    wkv_in, wq_in, wo_in = sem("wkv_in"), sem("wq_in"), sem("wo_in")
    kv_mm, k_ready, v_ready = sem("kv_mm"), sem("k_ready"), sem("v_ready")
    q_mm, q_ready = sem("q_mm"), sem("q_ready")
    s_mm, mx_ready, nmx_ready, p_ready, rs_ready, pn_ready, t_mm, pt_ready = (
        sem(n) for n in ("s_mm", "mx_ready", "nmx_ready", "p_ready", "rs_ready", "pn_ready", "t_mm", "pt_ready"))
    o_mm, o_ready, y_mm, y_taken = sem("o_mm"), sem("o_ready"), sem("y_mm"), sem("y_taken")

    with stage, nc.Block() as block:

        @block.sync
        def _(sp):
            sp.dma_start(wk[:, :, :], A["s_wk"]).then_inc(wkv_in, 16)
            sp.dma_start(wv[:, :, :], A["s_wv"]).then_inc(wkv_in, 16)
            sp.dma_start(wq[:, :, :, :], A["s_wq"]).then_inc(wq_in, 16)
            sp.dma_start(wo[:, :, :], A["s_wo"]).then_inc(wo_in, 16)

        @block.gpsimd
        def _(pool):
            nm.gpsimd(pool)
            for g in range(G):
                pool.wait_ge(rs_ready, g + 1)
                if g >= NPB:
                    pool.wait_ge(t_mm, g - NPB + 1)
                pool.tensor_scalar(Pn[g % NPB][:, :], Pr[g % NPB][:, :], rs[:, g % NPB:g % NPB + 1], None,
                                   ALU.mult).then_inc(pn_ready, 1)

        @block.vector
        def _(dve):
            nm.vector(dve)
            for b in range(B):
                for i in range(0, TB, 2):
                    n = B + (b * TB + i) // 2
                    dve.wait_ge(kv_mm, n + 1)
                    dve.tensor_copy(V[:, b * TB + i:b * TB + i + 2, :],
                                    PS[:, 4 + n % 4, 0:2 * DK].rearrange("p (i c) -> p i c", i=2)).then_inc(v_ready, 1)

            def maximum(g):
                dve.wait_ge(s_mm, g + 1)
                if g >= NPB:
                    dve.wait_ge(p_ready, g - NPB + 1)
                dve.tensor_reduce(mx[:, g % NPB:g % NPB + 1], PS[:, g % 2, :], AX.X, ALU.max).then_inc(mx_ready, 1)
                dve.wait_ge(mx_ready, g + 1)
                dve.tensor_scalar(nmx[:, g % NPB:g % NPB + 1], mx[:, g % NPB:g % NPB + 1], -1.0, None,
                                  ALU.mult).then_inc(nmx_ready, 1)

            def inverse_sum(g):
                dve.wait_ge(p_ready, g + 1)
                if g >= NPB:
                    dve.wait_ge(pn_ready, g - NPB + 1)
                dve.reciprocal(rs[:, g % NPB:g % NPB + 1], sm[:, g % NPB:g % NPB + 1]).then_inc(rs_ready, 1)

            def take_transposes(g):
                n, qt = divmod(g, TB)
                dve.wait_ge(t_mm, g + 1)
                if n >= 2:
                    dve.wait_ge(o_mm, n - 1)
                dve.tensor_copy(PT[n % 2][:, :, qt * P:(qt + 1) * P],
                                PS[:, 2 + g % 2, :].rearrange("p (m q) -> p m q", m=TB)).then_inc(pt_ready, 1)

            def take_output(b):
                for bank in range(2):
                    dve.wait_ge(y_mm, (b + 1) * H)
                    i = b * TB + 2 * bank
                    dve.tensor_tensor(X[:, i:i + 2, :], X[:, i:i + 2, :],
                                      PS[:, 6 + bank, :].rearrange("p (i d) -> p i d", i=2),
                                      ALU.add).then_inc(y_taken, 1)

            for g in range(G + LAG + 1):
                if g < G:
                    maximum(g)
                if 1 <= g <= G:
                    inverse_sum(g - 1)
                if g > LAG:
                    take_transposes(g - LAG - 1)
                if g == TB * H + TB + 1:
                    take_output(0)
            take_output(1)

        @block.scalar
        def _(act):
            nm.scalar(act)
            for b in range(B):
                act.wait_ge(kv_mm, b + 1)
                act.activation(KTr[:, b * S:(b + 1) * S], PS[:, 4 + b, :], ACT.Copy).then_inc(k_ready, 1)

            def take_q(n):
                act.wait_ge(q_mm, n + 1)
                if n >= 2:
                    act.wait_ge(s_mm, (n - 1) * TB)
                act.activation(QT[n % 2][:, :], PS[:, 4, :], ACT.Copy).then_inc(q_ready, 1)

            def take_o(n):
                act.wait_ge(o_mm, n + 1)
                if n >= 2:
                    act.wait_ge(y_mm, n - 1)
                act.activation(OT[n % 2][:, :], PS[:, 5, :], ACT.Copy).then_inc(o_ready, 1)

            take_q(0)
            for g in range(G):
                n, qt = divmod(g, TB)
                act.wait_ge(nmx_ready, g + 1)
                if g >= NPB:
                    act.wait_ge(pn_ready, g - NPB + 1)
                act.activation(Pr[g % NPB][:, :], PS[:, g % 2, :], ACT.Exp, bias=nmx[:, g % NPB:g % NPB + 1],
                               accum_out=sm[:, g % NPB:g % NPB + 1]).then_inc(p_ready, 1)
                if qt == 1 and n + 1 < UN:
                    take_q(n + 1)
                if qt == 2 and n >= 1:
                    take_o(n - 1)
            take_o(UN - 1)

        @block.tensor
        def _(pe):
            nm.tensor(pe)
            pe.wait_ge(nm.xT_ready, KD * B)
            pe.wait_ge(wkv_in, 32)
            for b in range(B):
                for k in range(KD):
                    last = pe.matmul(PS[:, 4 + b, :], wk[:, k, :], XT[:, k, b * S:(b + 1) * S],
                                     start=(k == 0), stop=(k == KD - 1))
                last.then_inc(kv_mm, 1)
            for i in range(0, NT, 2):
                n = B + i // 2
                if n >= 4:
                    pe.wait_ge(k_ready, n - 3)
                for j in range(2):
                    for k in range(KD):
                        last = pe.matmul(PS[:, 4 + n % 4, j * DK:(j + 1) * DK], XT[:, k, (i + j) * P:(i + j + 1) * P],
                                         wv[:, k, :], start=(k == 0), stop=(k == KD - 1))
                last.then_inc(kv_mm, 1)
            pe.wait_ge(k_ready, B)
            pe.wait_ge(v_ready, NT // 2)
            pe.wait_ge(wq_in, 16)
            pe.wait_ge(wo_in, 16)

            def queries(n):
                b, h = divmod(n, H)
                if n >= 1:
                    pe.wait_ge(q_ready, n)
                for k in range(KD):
                    last = pe.matmul(PS[:, 4, :], wq[:, h, k, :], XT[:, k, b * S:(b + 1) * S],
                                     start=(k == 0), stop=(k == KD - 1))
                last.then_inc(q_mm, 1)

            def scores(g):
                n, qt = divmod(g, TB)
                b = n // H
                pe.wait_ge(q_ready, n + 1)
                if g >= 2:
                    pe.wait_ge(p_ready, g - 1)
                pe.matmul(PS[:, g % 2, :], QT[n % 2][:, qt * P:(qt + 1) * P], KTr[:, b * S:(b + 1) * S],
                          start=True, stop=True).then_inc(s_mm, 1)

            def transposes(g):
                pe.wait_ge(pn_ready, g + 1)
                if g >= 2:
                    pe.wait_ge(pt_ready, g - 1)
                for m in range(TB):
                    last = pe.transpose(PS[:, 2 + g % 2, m * P:(m + 1) * P], Pn[g % NPB][:, m * P:(m + 1) * P],
                                        sh.ident[:, :])
                last.then_inc(t_mm, 1)

            def outputs(n):
                b = n // H
                pe.wait_ge(pt_ready, (n + 1) * TB)
                if n >= 1:
                    pe.wait_ge(o_ready, n)
                for m in range(TB):
                    last = pe.matmul(PS[:, 5, :], V[:, b * TB + m, :], PT[n % 2][:, m, :], start=(m == 0),
                                     stop=(m == TB - 1))
                last.then_inc(o_mm, 1)

            def project(n):
                b, h = divmod(n, H)
                pe.wait_ge(o_ready, n + 1)
                if h == 0 and b > 0:
                    pe.wait_ge(y_taken, 2 * b)
                for i in range(TB):
                    last = pe.matmul(PS[:, 6 + i // 2, (i % 2) * D:(i % 2 + 1) * D], OT[n % 2][:, i * P:(i + 1) * P],
                                     wo[:, h, :], start=(h == 0 and i % 2 == 0), stop=(h == H - 1 and i % 2 == 1),
                                     skip_group_check=True)
                last.then_inc(y_mm, 1)

            queries(0)
            for g in range(G + LAG):
                n, qt = divmod(g, TB)
                if g < G:
                    scores(g)
                if qt == 0 and n + 1 < UN:
                    queries(n + 1)
                if g >= LAG:
                    transposes(g - LAG)
                if qt == 2 and 1 <= n < UN:
                    outputs(n - 1)
                if qt == 0 and n >= 2:
                    project(n - 2)
            outputs(UN - 1)
            project(UN - 1)


def hard_cross_stage(nc, ctx, sh, A):
    NK = 1024
    NKT = B * NK // P
    PS, X, XN, XT = sh.PS, sh.X, sh.XN, sh.XT
    stage = ExitStack()

    def sb(name, shape, dt=F32):
        return stage.enter_context(nc.sbuf_tensor("h_" + name, shape, dt))

    def sem(name):
        return ctx.enter_context(nc.semaphore("h_" + name))

    nm = Norm(nc, ctx, stage, sh, "h_n")
    wc = sb("wc", [P, KD, D])
    VB = sb("VB", [P, UNITS, TB, 1, VW])
    at = Attention(nc, ctx, stage, PS, "h_a", S, 1, 2 * NBLK + 3, sh.ident, sh.identb)
    ctxT = sb("ctxT", [P, KD, B * NK])
    wq, wkv = sb("wq", [P, KD, D]), sb("wkv", [P, KD, 2 * HD])
    MK = sb("MK", [P, NKT, 2 * HD])
    QF = sb("QF", [P, KD, T])
    QP = [sb(f"QP{n}", [P, KD, T], BF16) for n in range(3)]
    KP = [sb(f"KP{n}", [HD, B, S], BF16) for n in range(3)]
    ktail = sb("ktail", [32, S], BF16)
    ktc = sb("ktc", [32, 1])
    top = sb("top", [P, NT, 8])
    idx = sb("idx", [P, NT, 8], U32)
    row = sb("row", [P, NT], U32)
    GM = sb("GM", [P, NT, 2 * HD])
    mkv_rows = nc.dram_tensor("h_mkv", [B * NK, 2 * HD], F32, kind="Internal").ap()
    q_parts = nc.dram_tensor("h_q_parts", [3, UNITS, GH * HD, S], BF16, kind="Internal").ap()
    k_parts = nc.dram_tensor("h_k_parts", [3, UNITS, HD, S], BF16, kind="Internal").ap()
    k_tail = nc.dram_tensor("h_k_tail", [UNITS, 32, S], BF16, kind="Internal").ap()

    small_in, ctx_in, w_in, wc_in = sem("small_in"), sem("ctx_in"), sem("w_in"), sem("wc_in")
    mk_mm, mk_ready, mk_stored, qf_mm, qf_ready = (sem(n) for n in ("mk_mm", "mk_ready", "mk_stored", "qf_mm", "qf_ready"))
    sc_mm, top_ready, idx_ready, row_ready = (sem(n) for n in ("sc_mm", "top_ready", "idx_ready", "row_ready"))
    found, kT_mm, v_ones, v_ready, qtail_set = (sem(n) for n in ("found", "kT_mm", "v_ones", "v_ready", "qtail_set"))
    tail_zero, tail_ready, tail_stored, q_stored, k_stored = (
        sem(n) for n in ("tail_zero", "tail_ready", "tail_stored", "q_stored", "k_stored"))
    NQC = B * KD

    def dst(n, part):
        if n < NQC:
            b, m = divmod(n, KD)
            return QP[part][:, m, b * S:(b + 1) * S]
        return KP[part][:, n - NQC, :]

    spl = Splitter(nc, ctx, stage, "h_s", dst, [P] * NQC + [HD] * B, NQC + B)
    po_t, po_s, po_v = project_out(nc, at, sh, sem, wc, wc_in, 16)

    with stage, nc.Block() as block:

        @block.sync
        def _(sp):
            sp.dma_start(ktc[:, :], A["h_ktc"]).then_inc(small_in, 16)
            sp.dma_start(wkv[:, :, :], A["h_wkv"]).then_inc(w_in, 16)
            sp.dma_start(wq[:, :, :], A["h_wq"]).then_inc(w_in, 16)
            sp.dma_start(ctxT[:, :, :], A["ctxT"]).then_inc(ctx_in, 16)
            sp.dma_start(wc[:, :, :], A["h_wc"]).then_inc(wc_in, 16)
            sp.wait_ge(mk_ready, 1)
            sp.dma_start(mkv_rows.rearrange("(t p) c -> p t c", p=P), MK[:, :, :]).then_inc(mk_stored, 16)
            sp.wait_ge(tail_ready, 1)
            for u in range(UNITS):
                sp.dma_start(k_tail[u], ktail[:, :]).then_inc(tail_stored, 16)
            for n in range(NQC):
                b, m = divmod(n, KD)
                sp.wait_ge(spl.p2_ready, n + 1)
                for part in range(3):
                    sp.dma_start(q_parts[part, b * NG + 2 * m:b * NG + 2 * m + 2].rearrange("u r n -> (u r) n"),
                                 QP[part][:, m, b * S:(b + 1) * S]).then_inc(q_stored, 16)
            for b in range(B):
                sp.wait_ge(spl.p2_ready, NQC + b + 1)
                for part in range(3):
                    for u in range(b * NG, (b + 1) * NG):
                        sp.dma_start(k_parts[part, u], KP[part][:, b, :]).then_inc(k_stored, 16)
            sp.wait_ge(tail_stored, 16 * UNITS)
            sp.wait_ge(k_stored, 16 * 3 * UNITS)
            sp.wait_ge(q_stored, 16 * 3 * NQC)
            sp.wait_ge(qtail_set, 2)
            sp.wait_ge(v_ready, B)
            at.sync(sp, load_unit(sp, at, q_parts, k_parts, k_tail, VB))

        @block.gpsimd
        def _(pool):
            nm.gpsimd(pool)
            pool.memset(VB[:, :, :, :, :], 1.0).then_inc(v_ones, 1)
            pool.memset(at.qtail[:, :, :], 0.0).then_inc(qtail_set, 1)
            pool.wait_ge(qtail_set, 1)
            pool.wait_ge(v_ones, 1)
            pool.tensor_scalar(at.qtail[TAIL:P, :, :], at.qtail[TAIL:P, :, :], sh.row98[TAIL:P, 0:1], None,
                               ALU.add).then_inc(qtail_set, 1)
            pool.memset(ktail[:, :], 0.0).then_inc(tail_zero, 1)
            pool.wait_ge(small_in, 16)
            pool.wait_ge(tail_zero, 1)
            pool.wait_ge(qtail_set, 2)
            pool.tensor_scalar(ktail[:, :], ktail[:, :], ktc[:, 0:1], None, ALU.add).then_inc(tail_ready, 1)
            pool.wait_ge(tail_ready, 1)
            spl.gpsimd(pool, 0, NQC)
            pool.wait_ge(mk_stored, 16)
            for i in range(NT):
                pool.wait_ge(row_ready, i + 1)
                pool.indirect_dma_start(out=GM[:, i, :], out_offset=None, in_=mkv_rows,
                                        in_offset=bass.IndirectOffsetOnAxis(ap=row[:, i:i + 1], axis=0),
                                        ).then_inc(found, 16)
            for b in range(B):
                spl.gpsimd(pool, NQC + b, NQC + b + 1)

        @block.vector
        def _(dve):
            nm.vector(dve)
            dve.wait_ge(mk_mm, 1)
            dve.tensor_copy(MK[:, :, :], PS[:, 4, :].rearrange("p (t c) -> p t c", t=NKT)).then_inc(mk_ready, 1)
            for n in range(NQC):
                dve.wait_ge(qf_mm, n + 1)
                dve.tensor_copy(spl.buffer(dve, n), PS[:, 4 + n, :]).then_inc(spl.f_ready, 1)
            for i in range(NT):
                b = i // TB
                bank = 2 * (i % 2)
                dve.wait_ge(sc_mm, i + 1)
                dve.max(top[:, i, :], PS[:, bank:bank + 2, :]).then_inc(top_ready, 1)
                dve.wait_ge(top_ready, i + 1)
                dve.max_index(idx[:, i, :], top[:, i, :], PS[:, bank:bank + 2, :].rearrange("p h n -> p (h n)")).then_inc(idx_ready, 1)
                dve.wait_ge(idx_ready, i + 1)
                dve.tensor_scalar(row[:, i:i + 1], idx[:, i, 0:1], float(b * NK), None, ALU.add).then_inc(row_ready, 1)
            dve.wait_ge(v_ones, 1)
            for b in range(B):
                dve.wait_ge(kT_mm, b + 1)
                dve.tensor_copy(spl.buffer(dve, NQC + b), PS[0:HD, 4 + b, :]).then_inc(spl.f_ready, 1)
                for g in range(NG):
                    last = dve.tensor_copy(VB[:, b * NG + g, :, 0, 0:HD], GM[:, b * TB:(b + 1) * TB, HD:2 * HD])
                last.then_inc(v_ready, 1)
            at.vector(dve)
            po_v(dve)

        @block.scalar
        def _(act):
            nm.scalar(act)
            for n in range(NQC):
                b, m = divmod(n, KD)
                act.wait_ge(spl.f_ready, n + 1)
                act.activation(QF[:, m, b * S:(b + 1) * S], spl.F[n % 2][:, :], ACT.Copy).then_inc(qf_ready, 1)
                spl.scalar(act, n, n + 1)
            spl.scalar(act, NQC, NQC + B)
            at.scalar(act)
            po_s(act)

        @block.tensor
        def _(pe):
            pe.wait_ge(w_in, 32)
            pe.wait_ge(ctx_in, 16)
            for t in range(NKT):
                for k in range(KD):
                    last = pe.matmul(PS[:, 4, t * 2 * HD:(t + 1) * 2 * HD], ctxT[:, k, t * P:(t + 1) * P],
                                     wkv[:, k, :], start=(k == 0), stop=(k == KD - 1), skip_group_check=True)
            last.then_inc(mk_mm, 1)
            nm.tensor(pe)
            pe.wait_ge(nm.xT_ready, KD * B)
            pe.wait_ge(mk_ready, 1)
            for n in range(NQC):
                b, m = divmod(n, KD)
                for k in range(KD):
                    last = pe.matmul(PS[:, 4 + n, :], wq[:, k, m * P:(m + 1) * P], XT[:, k, b * S:(b + 1) * S],
                                     start=(k == 0), stop=(k == KD - 1))
                last.then_inc(qf_mm, 1)
            for i in range(NT):
                b = i // TB
                pe.wait_ge(qf_ready, KD * (b + 1))
                if i >= 2:
                    pe.wait_ge(idx_ready, i - 1)
                for half in range(2):
                    for k in range(KD):
                        c0 = b * NK + half * BANK
                        last = pe.matmul(PS[:, 2 * (i % 2) + half, :], QF[:, k, i * P:(i + 1) * P],
                                         ctxT[:, k, c0:c0 + BANK], start=(k == 0), stop=(k == KD - 1))
                last.then_inc(sc_mm, 1)
            pe.wait_ge(spl.f_ready, NQC)
            for b in range(B):
                pe.wait_ge(found, 16 * NT)
                for i in range(TB):
                    last = pe.transpose(PS[0:HD, 4 + b, i * P:(i + 1) * P], GM[:, b * TB + i, 0:HD], sh.ident[:, :])
                last.then_inc(kT_mm, 1)
            pe.wait_ge(spl.f_ready, NQC + B)
            pe.wait_ge(idx_ready, NT)
            at.tensor(pe)
            po_t(pe)


def experts_stage(nc, ctx, sh, A, layer):
    EXP = 8
    first = layer == 0
    F = 512 if first else 1024
    KF, NB1 = F // P, F // BANK
    SLOT_TILES = NT + EXP - 1
    SLOTS = SLOT_TILES * P
    PS, X, XN, XT = sh.PS, sh.X, sh.XN, sh.XT
    pre = "e_" if first else "g_"
    stage = ExitStack()

    def sb(name, shape, dt=F32):
        return stage.enter_context(nc.sbuf_tensor(pre + name, shape, dt))

    def sem(name):
        return ctx.enter_context(nc.semaphore(pre + name))

    nm = Norm(nc, ctx, stage, sh, pre + "n")
    wr, br = sb("wr", [P, KD, EXP]), sb("br", [P, EXP])
    W1 = sb("W1", [P, KD, EXP * F])
    W2 = sb("W2", [P, KF, (EXP if first else 1) * D])
    B1 = sb("B1", [P, EXP * F])
    B2 = sb("B2", [P, (EXP if first else 1) * D])
    tri, ones = sb("tri", [P, P]), sb("ones", [P, P])
    iota = sb("iota", [P, 16])
    iotaP = sb("iotaP", [P, EXP])
    lg, ex = sb("lg", [P, NT, EXP]), sb("ex", [P, NT, EXP])
    mx, prob, den = sb("mx", [P, NT]), sb("prob", [P, NT]), sb("den", [P, NT])
    top, idx = sb("top", [P, NT, 8]), sb("idx", [P, NT, 8], U32)
    idxf = sb("idxf", [P, NT])
    OH = sb("OH", [P, NT, EXP])
    before = sb("before", [P, NT + 1, EXP])
    cmp_ = sb("cmp", [P, EXP, EXP])
    tiles, upto, base = sb("tiles", [P, EXP]), sb("upto", [P, EXP]), sb("base", [P, EXP])
    pos = sb("pos", [P, NT, EXP])
    slotf, slot = sb("slotf", [P, NT]), sb("slot", [P, NT], U32)
    cmps = sb("cmps", [P, 16, EXP])
    exf, ext = sb("exf", [P, 16]), sb("ext", [P, 16], I32)
    zero = sb("zero", [P, D])
    gb = None if first else sb("gb", [P, 2, D])
    own2 = sem("own2")
    Xs = [sb(f"Xs{n}", [P, D]) for n in range(2)]
    XsT = [sb(f"XsT{n}", [P, KD, P]) for n in range(2)]
    Hs = [sb(f"H{n}", [P, F]) for n in range(2)]
    HT = [sb(f"HT{n}", [P, KF, P]) for n in range(2)]
    Ys = [sb(f"Y{n}", [P, D]) for n in range(2)]
    YG = sb("YG", [P, NT, D])
    xs = nc.dram_tensor(pre + "xs", [SLOTS, D], F32, kind="Internal").ap()
    ys = nc.dram_tensor(pre + "ys", [SLOTS, D], F32, kind="Internal").ap()

    small_in, w1_in, w2_in, zero_set, zeroed = (sem(n) for n in ("small_in", "w1_in", "w2_in", "zero_set", "zeroed"))
    own, lg_mm, lg_ready, ex_ready, oh_ready, rank_mm, slot_ready, ext_ready = (
        sem(n) for n in ("own", "lg_mm", "lg_ready", "ex_ready", "oh_ready", "rank_mm", "slot_ready", "ext_ready"))
    scattered = sem("scattered")
    xs_in = [sem(f"xs_in{n}") for n in range(2)]
    xsT_mm, xsT_ready, w1_mm, h_sum, h_ready, hT_mm, hT_ready, w2_mm, y_ready, gathered = (
        sem(n) for n in ("xsT_mm", "xsT_ready", "w1_mm", "h_sum", "h_ready", "hT_mm", "hT_ready", "w2_mm",
                         "y_ready", "gathered"))
    stored = [sem(f"stored{n}") for n in range(2)]
    xb_ready, var2_ready, rstd2_ready, eps2_ready = (
        sem(n) for n in ("xb_ready", "var2_ready", "rstd2_ready", "eps2_ready"))
    NSMALL = 6

    def tiles_loop(eng, step):
        for t in range(2):
            step(t, t)
        with eng.Fori(0, (SLOT_TILES - 5) // 2) as i:
            step(i * 2 + 2, 0)
            step(i * 2 + 3, 1)
        for t in range(SLOT_TILES - 3, SLOT_TILES):
            step(t, t % 2)

    def known_below(t, n):
        return isinstance(t, int) and t < n

    def rows(t):
        return bass.ds(t * P, P)

    with stage, nc.Block() as block:

        @block.sync
        def _(sp):
            small = [(wr, "wr"), (tri, "tris"), (iota, "iota"), (iotaP, "iotaP"), (B2, pre + "b2")]
            small += [(br, pre + "br")] if first else []
            for d, s in small:
                sp.dma_start(d[tuple(slice(None) for _ in d.shape)], A[pre + "wr" if s == "wr" else s]).then_inc(small_in, 16)
            sp.dma_start(B1[:, :], A[pre + "b1"].to_broadcast([P, EXP * F])).then_inc(w1_in, 16)
            for k in range(KD):
                sp.dma_start(W1[:, k, :].rearrange("p (e f) -> p e f", e=EXP), A[pre + "w1"][k]).then_inc(w1_in, 16)
            sp.wait_ge(zero_set, 1)
            for t in range(SLOT_TILES):
                sp.dma_start(xs[t * P:(t + 1) * P, :], zero[:, :]).then_inc(zeroed, 16)
            sp.dma_start(W2[:, :, :], A[pre + "w2"]).then_inc(w2_in, 16)
            sp.wait_ge(scattered, 16 * NT)

            def load(t, p):
                if not known_below(t, 2):
                    sp.wait_ge(xsT_mm, t - 1)
                sp.dma_start(Xs[p][:, :], xs[rows(t), :]).then_inc(xs_in[p], 16)

            def step(t, p):
                if t is not None and not (isinstance(t, int) and t + 2 >= SLOT_TILES):
                    load(t + 2, p)
                sp.wait_ge(y_ready, t + 1)
                sp.dma_start(ys[rows(t), :], Ys[p][:, :]).then_inc(stored[p], 16)

            load(0, 0)
            load(1, 1)
            tiles_loop(sp, step)
            for p in range(2):
                sp.wait_ge(stored[p], 16 * ((SLOT_TILES + 1 - p) // 2))

        @block.gpsimd
        def _(pool):
            pool.memset(zero[:, :], 0.0).then_inc(zero_set, 1)
            pool.memset(ones[:, :], 1.0).then_inc(zero_set, 1)
            nm.gpsimd(pool)
            pool.wait_ge(nm.xn_ready, 1)
            pool.wait_ge(zeroed, 16 * SLOT_TILES)
            pool.wait_ge(slot_ready, 1)
            for i in range(NT):
                pool.indirect_dma_start(out=xs, out_offset=bass.IndirectOffsetOnAxis(ap=slot[:, i:i + 1], axis=0),
                                        in_=XN[:, i, :], in_offset=None).then_inc(scattered, 16)
            if not first:
                pool.wait_ge(scattered, 16 * NT)
                pool.wait_ge(nm.xT_done, KD * B)
                pool.wait_ge(small_in, 16 * NSMALL)
                for i in range(NT):
                    last = pool.tensor_tensor(XN[:, i, :], XN[:, i, :], B2[:, :], ALU.add)
                last.then_inc(xb_ready, 1)
            for p in range(2):
                pool.wait_ge(stored[p], 16 * ((SLOT_TILES + 1 - p) // 2))
            for i in range(NT):
                pool.indirect_dma_start(out=YG[:, i, :], out_offset=None, in_=ys,
                                        in_offset=bass.IndirectOffsetOnAxis(ap=slot[:, i:i + 1], axis=0),
                                        ).then_inc(gathered, 16)
            if not first:
                pool.wait_ge(var2_ready, 1)
                pool.tensor_scalar(nm.rstd[:, :], nm.mv[:, :, 1], 1e-12, None, ALU.add).then_inc(eps2_ready, 1)
                pool.wait_ge(eps2_ready, 1)
                pool.tensor_tensor(nm.rstd[:, :], nm.rstd[:, :], sh.mhalf[:, :], ALU.pow).then_inc(rstd2_ready, 1)

        @block.vector
        def _(dve):
            nm.vector(dve)
            c = Chain(dve, own)
            dve.wait_ge(small_in, 16 * NSMALL)
            dve.wait_ge(lg_mm, 1)
            src = PS[:, 4, 0:NT * EXP].rearrange("p (i e) -> p i e", i=NT)
            if first:
                c.link(dve.tensor_tensor(lg[:, :, :], src, br[:, :].unsqueeze(1).to_broadcast([P, NT, EXP]), ALU.add))
            else:
                c.link(dve.tensor_copy(lg[:, :, :], src))
            for i in range(NT):
                last = dve.max(top[:, i, :], lg[:, i, :])
            c.link(last)
            for i in range(NT):
                last = dve.max_index(idx[:, i, :], top[:, i, :], lg[:, i, :])
            c.link(last)
            c.link(dve.tensor_copy(idxf[:, :], idx[:, :, 0]))
            dve.tensor_tensor(OH[:, :, :], iota[:, 0:EXP].unsqueeze(1).to_broadcast([P, NT, EXP]),
                              idxf[:, :].unsqueeze(2).to_broadcast([P, NT, EXP]), ALU.is_equal).then_inc(oh_ready, 1)
            if first:
                dve.tensor_tensor(lg[:, :, :], lg[:, :, :], top[:, :, 0:1].to_broadcast([P, NT, EXP]),
                                  ALU.subtract).then_inc(lg_ready, 1)
            c.link(dve.memset(before[:, 0, :], 0.0))
            dve.wait_ge(rank_mm, 1)
            NE = NT * EXP
            for i in range(NT):
                c.link(dve.tensor_tensor(before[:, i + 1, :], before[:, i, :],
                                         PS[:, 5, NE + i * EXP:NE + (i + 1) * EXP], ALU.add))
            c.link(dve.tensor_tensor(cmp_[:, :, :], before[:, NT, :].unsqueeze(2).to_broadcast([P, EXP, EXP]),
                                     iotaP[:, :].unsqueeze(1).to_broadcast([P, EXP, EXP]), ALU.is_gt))
            c.link(dve.tensor_reduce(tiles[:, :], cmp_[:, :, :], AX.X, ALU.add))
            dve.wait_ge(zero_set, 2)
            c.link(dve.tensor_tensor_scan(upto[:, :], ones[:, 0:EXP], tiles[:, :], 0.0, ALU.mult, ALU.add))
            c.link(dve.tensor_tensor(base[:, :], upto[:, :], tiles[:, :], ALU.subtract))
            c.link(dve.tensor_tensor(pos[:, :, :], before[:, 0:NT, :],
                                     PS[:, 5, 0:NE].rearrange("p (i e) -> p i e", i=NT), ALU.add))
            c.link(dve.scalar_tensor_tensor(out=pos[:, :, :], in0=base[:, :].unsqueeze(1).to_broadcast([P, NT, EXP]),
                                            scalar=float(P), in1=pos[:, :, :], op0=ALU.mult, op1=ALU.add))
            c.link(dve.tensor_tensor(pos[:, :, :], pos[:, :, :], OH[:, :, :], ALU.mult))
            c.link(dve.tensor_reduce(slotf[:, :], pos[:, :, :], AX.X, ALU.add))
            dve.tensor_copy(slot[:, :], slotf[:, :]).then_inc(slot_ready, 1)
            c.link(dve.tensor_tensor(cmps[:, :, :], upto[:, :].unsqueeze(1).to_broadcast([P, 16, EXP]),
                                     iota[:, :].unsqueeze(2).to_broadcast([P, 16, EXP]), ALU.is_le))
            c.link(dve.tensor_reduce(exf[:, :], cmps[:, :, :], AX.X, ALU.add))
            c.link(dve.tensor_scalar(exf[:, :], exf[:, :], EXP - 1.0, None, ALU.min))
            dve.tensor_copy(ext[:, :], exf[:, :]).then_inc(ext_ready, 1)
            if first:
                dve.wait_ge(ex_ready, 1)
                c.link(dve.tensor_reduce(den[:, :], ex[:, :, :], AX.X, ALU.add))
                c.link(dve.reciprocal(prob[:, :], den[:, :]))

            dve.wait_ge(ext_ready, 1)
            dve.wait_ge(w1_in, 16 * (KD + 1))

            def hidden(t, p):
                e = dve.value_load(ext[0:1, bass.ds(t, 1)], min_val=0, max_val=EXP - 1)
                dve.wait_ge(w1_mm, t + 1)
                if not known_below(t, 2):
                    dve.wait_ge(hT_mm, t - 1)
                b0 = 1 + p * NB1
                dve.tensor_tensor(Hs[p][:, :], PS[:, b0:b0 + NB1, :].rearrange("p h n -> p (h n)"),
                                  B1[:, bass.ds(e * F, F)], ALU.add).then_inc(h_sum, 1)

            def result(t, p):
                if first:
                    e = dve.value_load(ext[0:1, bass.ds(t, 1)], min_val=0, max_val=EXP - 1)
                dve.wait_ge(w2_mm, t + 1)
                if not known_below(t, 2):
                    dve.wait_ge(stored[p], (t - p) * 8)
                if first:
                    last = dve.tensor_tensor(Ys[p][:, :], PS[:, 7, 0:D], B2[:, bass.ds(e * D, D)], ALU.add)
                else:
                    last = dve.tensor_copy(Ys[p][:, :], PS[:, 7, 0:D])
                last.then_inc(y_ready, 1)

            def step(t, p):
                if not (isinstance(t, int) and t + 1 >= SLOT_TILES):
                    hidden(t + 1, 1 - p)
                result(t, p)

            hidden(0, 0)
            tiles_loop(dve, step)
            if first:
                for i in range(NT):
                    dve.wait_ge(gathered, 16 * NT)
                    dve.scalar_tensor_tensor(out=X[:, i, :], in0=YG[:, i, :], scalar=prob[:, i:i + 1],
                                             in1=X[:, i, :], op0=ALU.mult, op1=ALU.add).then_inc(xb_ready, 1)
            else:
                dve.wait_ge(xb_ready, 1)
                for i in range(NT):
                    dve.wait_ge(gathered, 16 * NT)
                    last = dve.tensor_tensor(XN[:, i, :], XN[:, i, :], YG[:, i, :], ALU.add)
                c.link(last)
                layernorm_vector(dve, c.link, XN, XN, nm.st6, nm.mv, nm.rstd, var2_ready, rstd2_ready).then_inc(own2, 1)
                dve.wait_ge(own2, 1)
                for i in range(NT):
                    last = dve.tensor_tensor(XN[:, i, :], XN[:, i, :], gb[:, 0, :], ALU.mult)
                last.then_inc(own2, 1)
                dve.wait_ge(own2, 2)
                for i in range(NT):
                    last = dve.tensor_tensor(XN[:, i, :], XN[:, i, :], gb[:, 1, :], ALU.add)
                last.then_inc(own2, 1)
                dve.wait_ge(own2, 3)
                for i in range(NT):
                    dve.tensor_tensor(X[:, i, :], X[:, i, :], XN[:, i, :], ALU.add).then_inc(own2, 1)

        @block.scalar
        def _(act):
            if not first:
                act.dma_start(gb[:, :, :], A["g_gb"]).then_inc(small_in, 16)
            nm.scalar(act)
            if first:
                act.wait_ge(lg_ready, 1)
                act.activation(ex[:, :, :], lg[:, :, :], ACT.Exp).then_inc(ex_ready, 1)

            def take_x(t, p):
                act.wait_ge(xsT_mm, t + 1)
                if not known_below(t, 2):
                    act.wait_ge(w1_mm, t - 1)
                act.activation(XsT[p][:, :, :], PS[:, 0, 0:D].rearrange("p (k n) -> p k n", k=KD),
                               ACT.Copy).then_inc(xsT_ready, 1)

            def gelu(t, p):
                act.wait_ge(h_sum, t + 1)
                act.activation(Hs[p][:, :], Hs[p][:, :], ACT.Gelu).then_inc(h_ready, 1)

            def take_h(t, p):
                act.wait_ge(hT_mm, t + 1)
                if not known_below(t, 2):
                    act.wait_ge(w2_mm, t - 1)
                b0, n = (5 + p, 1) if first else (5, 2)
                act.activation(HT[p][:, :, :].rearrange("p k n -> p (k n)"),
                               PS[:, b0:b0 + n, :].rearrange("p h n -> p (h n)"),
                               ACT.Relu if first else ACT.Copy).then_inc(hT_ready, 1)

            def step(t, p):
                if not (isinstance(t, int) and t + 2 >= SLOT_TILES):
                    take_x(t + 2, p)
                take_h(t, p)
                if not first and not (isinstance(t, int) and t + 1 >= SLOT_TILES):
                    gelu(t + 1, 1 - p)

            take_x(0, 0)
            take_x(1, 1)
            if not first:
                gelu(0, 0)
            tiles_loop(act, step)

        @block.tensor
        def _(pe):
            nm.tensor(pe)
            pe.wait_ge(small_in, 16 * NSMALL)
            pe.wait_ge(nm.xT_ready, KD * B)
            for i in range(NT):
                for k in range(KD):
                    last = pe.matmul(PS[:, 4, i * EXP:(i + 1) * EXP], XT[:, k, i * P:(i + 1) * P], wr[:, k, :],
                                     start=(k == 0), stop=(k == KD - 1), skip_group_check=True)
            last.then_inc(lg_mm, 1)
            pe.wait_ge(oh_ready, 1)
            pe.wait_ge(zero_set, 2)
            hot = OH[:, :, :].rearrange("p i e -> p (i e)")
            pe.matmul(PS[:, 5, 0:NT * EXP], tri[:, :], hot, start=True, stop=True)
            pe.matmul(PS[:, 5, NT * EXP:2 * NT * EXP], ones[:, :], hot, start=True, stop=True).then_inc(rank_mm, 1)
            pe.wait_ge(ext_ready, 1)
            pe.wait_ge(w1_in, 16 * (KD + 1))

            def transpose_x(t, p):
                pe.wait_ge(xs_in[p], (t - p) * 8 + 16)
                if not known_below(t, 1):
                    pe.wait_ge(xsT_ready, t)
                for k in range(KD):
                    last = pe.transpose(PS[:, 0, k * P:(k + 1) * P], Xs[p][:, k * P:(k + 1) * P], sh.ident[:, :])
                last.then_inc(xsT_mm, 1)

            def up(t, p):
                e = pe.value_load(ext[0:1, bass.ds(t, 1)], min_val=0, max_val=EXP - 1)
                pe.wait_ge(xsT_ready, t + 1)
                if not known_below(t, 2):
                    pe.wait_ge(h_sum, t - 1)
                for half in range(NB1):
                    for k in range(KD):
                        last = pe.matmul(PS[:, 1 + p * NB1 + half, :], XsT[p][:, k, :],
                                         W1[:, k, bass.ds(e * F + half * BANK, BANK)],
                                         start=(k == 0), stop=(k == KD - 1))
                last.then_inc(w1_mm, 1)

            def transpose_h(t, p):
                pe.wait_ge(h_sum if first else h_ready, t + 1)
                if first:
                    if not known_below(t, 2):
                        pe.wait_ge(hT_ready, t - 1)
                elif not known_below(t, 1):
                    pe.wait_ge(hT_ready, t)
                for k in range(KF):
                    bank = 5 + p if first else 5 + k // TB
                    last = pe.transpose(PS[:, bank, k % TB * P:(k % TB + 1) * P], Hs[p][:, k * P:(k + 1) * P],
                                        sh.ident[:, :])
                last.then_inc(hT_mm, 1)

            def down(t, p):
                e = pe.value_load(ext[0:1, bass.ds(t, 1)], min_val=0, max_val=EXP - 1) if first else 0
                pe.wait_ge(hT_ready, t + 1)
                if not known_below(t, 1):
                    pe.wait_ge(y_ready, t)
                for k in range(KF):
                    last = pe.matmul(PS[:, 7, 0:D], HT[p][:, k, :], W2[:, k, bass.ds(e * D, D)],
                                     start=(k == 0), stop=(k == KF - 1))
                last.then_inc(w2_mm, 1)

            def step(t, p):
                if not (isinstance(t, int) and t + 2 >= SLOT_TILES):
                    transpose_x(t + 2, p)
                transpose_h(t, p)
                if not (isinstance(t, int) and t + 1 >= SLOT_TILES):
                    up(t + 1, 1 - p)
                down(t, p)

            transpose_x(0, 0)
            transpose_x(1, 1)
            up(0, 0)
            pe.wait_ge(w2_in, 16)
            tiles_loop(pe, step)


def experts0_stage(nc, ctx, sh, A):
    experts_stage(nc, ctx, sh, A, 0)


def experts1_stage(nc, ctx, sh, A):
    experts_stage(nc, ctx, sh, A, 1)


def layouts(np, I):
    def ktile(w):
        return w.reshape(-1, P, w.shape[-1]).transpose(1, 0, 2)

    def cols(v):
        return v.reshape(-1, P).T

    def rows(v):
        return np.broadcast_to(v, (P, v.shape[-1]))

    A = {}
    A["x"] = I["x"].reshape(NT, P, D).transpose(1, 0, 2)
    A["ident"] = np.eye(P, dtype=np.float32)
    A["tri"] = np.triu(np.ones((P, P), np.float32))
    A["sel"] = np.broadcast_to(np.eye(8, dtype=np.float32)[:, :, None], (8, 8, P))
    A["m_nw"] = rows(I["L0_attn_norm_w"])
    A["m_rw1"] = ktile(I["L0_attn_r_w1"].T)
    A["m_rw2"] = I["L0_attn_r_w2"].T
    A["m_rb1"] = I["L0_attn_r_b1"][:, None]
    A["m_rb2"] = rows(I["L0_attn_r_b2"])
    cw, cb = I["L0_attn_conv_w"], I["L0_attn_conv_b"]
    A["m_cwx"] = ktile(cw[0:512])
    A["m_cbx"] = cols(cb[0:512])
    A["m_cwbc"] = cw[512:].reshape(2, 64, 4).transpose(1, 0, 2)
    A["m_cbbc"] = cb[512:].reshape(2, 64).T
    A["m_hp"] = np.stack([I["L0_attn_dt_bias"], I["L0_attn_A_log"]], 1)
    A["m_D"] = cols(np.repeat(I["L0_attn_D_param"], 64))
    A["m_gw"] = cols(I["L0_attn_gnorm_w"])
    A["m_win"] = ktile(I["L0_attn_in_proj_w"].T)
    A["m_wout"] = ktile(I["L0_attn_out_proj_w"].T)
    A["row98"] = np.zeros((P, 1), np.float32)
    A["row98"][TAIL + 2] = 1.0
    A["ctxT"] = I["ctx_1024"].transpose(2, 0, 1).reshape(KD, P, -1).transpose(1, 0, 2)
    A["mask"] = I["mask_Bx1x1xS2_if1"].reshape(B, -1)
    for n in ("q", "k", "v", "o"):
        A["c_w" + n] = ktile(I["L0_xattn_w" + n].T)
    A["c_bq"], A["c_bk"] = cols(I["L0_xattn_bq"]), cols(I["L0_xattn_bk"])
    A["c_bv"], A["c_bo"] = rows(I["L0_xattn_bv"]), rows(I["L0_xattn_bo"])
    A["tris"] = np.triu(np.ones((P, P), np.float32), 1)
    A["iota"] = rows(np.arange(16, dtype=np.float32))
    A["iotaP"] = rows(P * np.arange(8, dtype=np.float32))
    A["e_wr"], A["e_br"] = ktile(I["L0_ffn_w_router"]), rows(I["L0_ffn_b_router"])
    A["e_w1"] = I["L0_ffn_w1"].reshape(8, KD, P, -1).transpose(1, 2, 0, 3)
    A["e_b1"] = I["L0_ffn_b1"].reshape(1, -1)
    A["e_w2"] = I["L0_ffn_w2"].reshape(8, 4, P, D).transpose(2, 1, 0, 3).reshape(P, 4, -1)
    A["e_b2"] = rows(I["L0_ffn_b2"].reshape(-1))
    A["g_wr"] = ktile(I["L1_ffn_Wr"].T)
    A["g_w1"] = I["L1_ffn_W1"].reshape(8, KD, P, -1).transpose(1, 2, 0, 3)
    A["g_b1"] = I["L1_ffn_b1"].reshape(1, -1)
    A["g_w2"] = ktile(I["L1_ffn_Wo"])
    A["g_b2"] = rows(I["L1_ffn_bo"])
    A["g_gb"] = np.broadcast_to(np.stack([I["L1_ffn_gamma"], I["L1_ffn_beta"]]), (P, 2, D))
    A["s_wq"] = I["L1_attn_proj_q"].reshape(8, KD, P, P).transpose(2, 0, 1, 3)
    A["s_wk"], A["s_wv"] = ktile(I["L1_attn_proj_k"]), ktile(I["L1_attn_proj_v"])
    A["s_wo"] = I["L1_attn_proj_o"].transpose(2, 0, 1)
    A["h_wq"], A["h_wkv"], A["h_wc"] = (ktile(I["L1_xattn_" + n].T) for n in ("Wq", "Wkv", "Wc"))
    A["h_ktc"] = (np.arange(32) < 2).astype(np.float32)[:, None]
    ktc = np.zeros((32, 2), np.float32)
    ktc[0:2, 1] = 1.0
    ktc[2] = MASKED, -MASKED
    A["c_ktc"] = ktc
    return {k: np.ascontiguousarray(v) for k, v in A.items()}


STAGES = [mamba_stage, cross_stage, experts0_stage, shared_kv_stage, hard_cross_stage, experts1_stage]


def constants(nc, ctx, sh, A):
    const_in, identb_made = ctx.enter_context(nc.semaphore("const_in")), ctx.enter_context(nc.semaphore("identb_made"))
    with nc.Block() as block:
        @block.sync
        def _(sp):
            sp.dma_start(sh.X[:, :, :], A["x"]).then_inc(const_in, 16)
            sp.dma_start(sh.ident[:, :], A["ident"]).then_inc(const_in, 16)
            sp.dma_start(sh.row98[:, :], A["row98"]).then_inc(const_in, 16)
            sp.wait_ge(const_in, 48)

        @block.gpsimd
        def _(pool):
            pool.memset(sh.mhalf[:, :], -0.5)

        @block.vector
        def _(dve):
            dve.wait_ge(const_in, 48)
            dve.tensor_copy(sh.identb[:, :], sh.ident[:, :]).then_inc(identb_made, 1)
            dve.wait_ge(identb_made, 1)


def decoder(nc, A, out, stages=None):
    ctx = ExitStack()
    with ctx:
        sh = Shared()
        sh.PS = ctx.enter_context(nc.psum_tensor("PS", [P, 8, BANK], F32))
        sh.X = ctx.enter_context(nc.sbuf_tensor("X", [P, NT, D], F32))
        sh.XN = ctx.enter_context(nc.sbuf_tensor("XN", [P, NT, D], F32))
        sh.XT = ctx.enter_context(nc.sbuf_tensor("XT", [P, KD, T], F32))
        sh.mhalf = ctx.enter_context(nc.sbuf_tensor("mhalf", [P, NT], F32))
        sh.ident = ctx.enter_context(nc.sbuf_tensor("ident", [P, P], F32))
        sh.identb = ctx.enter_context(nc.sbuf_tensor("identb", [P, P], BF16))
        sh.row98 = ctx.enter_context(nc.sbuf_tensor("row98", [P, 1], F32))
        constants(nc, ctx, sh, A)
        for s in (STAGES if stages is None else stages):
            s(nc, own := StageSemaphores(nc), sh, A)
            own.clear()
        stored = ctx.enter_context(nc.semaphore("stored"))
        with nc.Block() as block:
            @block.sync
            def _(sp):
                sp.dma_start(out, sh.X[:, :, :]).then_inc(stored, 16)
                sp.wait_ge(stored, 16)


def kernel(**inputs):
    import numpy as _np
    import concourse.bacc as _bacc
    from concourse import mybir as _mybir
    from concourse.bass_utils import run_bass_kernel_spmd as _run

    nc = _bacc.Bacc("TRN2", target_bir_lowering=False, num_devices=1)
    arrays = layouts(_np, {k: _np.asarray(v) for k, v in inputs.items()})
    A = {k: nc.dram_tensor("in_" + k, v.shape, _mybir.dt.from_np(v.dtype), kind="ExternalInput").ap()
         for k, v in arrays.items()}
    out = nc.dram_tensor("out_x", (P, NT, D), F32, kind="ExternalOutput").ap()
    decoder(nc, A, out)
    r = _run(nc, [{"in_" + k: v for k, v in arrays.items()}], core_ids=[0])
    y = r.results[0]["out_x"]
    return y.transpose(1, 0, 2).reshape(B, S, D)
```

```python
from contextlib import ExitStack

import concourse.bass as bass
from concourse import mybir

ALU = mybir.AluOpType
ACT = mybir.ActivationFunctionType
AX = mybir.AxisListType
F32 = mybir.dt.float32
BF16 = mybir.dt.bfloat16
I32 = mybir.dt.int32
U32 = mybir.dt.uint32

P = 128
B, S, D = 2, 512, 256
T = B * S
NT = T // P
TB = S // P
AREA = 17160
KD = D // P
BANK = 512


class Chain:

    def __init__(self, eng, sem):
        self.eng, self.sem, self.n = eng, sem, 0

    def link(self, ins):
        self.n += 1
        ins.then_inc(self.sem, 1)
        self.eng.wait_ge(self.sem, self.n)


def layernorm_vector(dve, link, src, dst, st6, mv, rstd, var_ready, rstd_ready, normed):
    for b in range(B):
        for i in range(b * TB, (b + 1) * TB):
            last = dve.bn_stats(st6[:, i, :], src[:, i, :])
        link(last)
        for i in range(b * TB, (b + 1) * TB):
            last = dve.bn_aggr(mv[:, i, :], st6[:, i, :])
        last.then_inc(var_ready, 1)
    dve.wait_ge(var_ready, B)
    for b in range(B):
        dve.wait_ge(rstd_ready, b + 1)
        for i in range(b * TB, (b + 1) * TB):
            last = dve.tensor_scalar(dst[:, i, :], src[:, i, :], mv[:, i, 0:1], rstd[:, i:i + 1],
                                     ALU.subtract, ALU.mult)
        last.then_inc(normed, 1)


def inverse_deviations_gpsimd(pool, mhalf, mv, rstd, eps, var_ready, eps_added, rstd_ready):
    for b in range(B):
        tiles = slice(b * TB, (b + 1) * TB)
        pool.wait_ge(var_ready, b + 1)
        pool.tensor_scalar(rstd[:, tiles], mv[:, tiles, 1], eps, None, ALU.add).then_inc(eps_added, 1)
        pool.wait_ge(eps_added, b + 1)
        pool.tensor_tensor(rstd[:, tiles], rstd[:, tiles], mhalf[:, tiles], ALU.pow).then_inc(rstd_ready, 1)
    pool.wait_ge(rstd_ready, B)


def transposes_tensor(pe, PS, XN, ident, ready, per_batch, done):
    for b in range(B):
        pe.wait_ge(ready, (b + 1) * per_batch)
        for k in range(KD):
            for i in range(TB):
                last = pe.transpose(PS[:, KD * b + k, i * P:(i + 1) * P],
                                    XN[:, b * TB + i, k * P:(k + 1) * P], ident[:, :])
            last.then_inc(done, 1)


class Shared:
    pass


class Area:

    def __init__(self, whole):
        self.whole, self.used = whole, 0

    def take(self, shape, dt=F32):
        words = 1
        for n in shape[1:]:
            words *= n
        words = words * mybir.dt.size(dt) // 4
        flat = self.whole[0:shape[0], self.used:self.used + words]
        self.used += words
        if dt != F32:
            flat = flat.bitcast(dt)
        names = "abcd"[:len(shape) - 1]
        return flat.rearrange(f"p ({' '.join(names)}) -> p {' '.join(names)}", **dict(zip(names, shape[1:])))


class ExpertWeights:

    EXP = 8

    def __init__(self, nc, ctx, sh, A, layer):
        self.first = layer == 0
        self.pre = "e_" if self.first else "g_"
        self.F = 512 if self.first else 1024
        self.KF = self.F // P
        area = Area(sh.area)
        self.W1 = area.take([P, KD, self.EXP * self.F])
        self.W2 = area.take([P, self.KF, self.EXP * D]) if self.first else None
        self.A = A
        self.loaded = ctx.enter_context(nc.semaphore(self.pre + "weights_loaded"))
        self.loads = (2 if self.first else 1) * self.EXP

    def load_expert(self, eng, e):
        def cut(name):
            return self.A[self.pre + name][bass.ds(e, 1), :, :, :].rearrange("e p k f -> p (e k) f")
        F = self.F
        eng.dma_start(self.W1[:, :, bass.ds(e * F, F)], cut("w1")).then_inc(self.loaded, 16)
        if self.first:
            eng.dma_start(self.W2[:, :, bass.ds(e * D, D)], cut("w2")).then_inc(self.loaded, 16)


SLOT_TILES = NT + ExpertWeights.EXP - 1
SLOTS = SLOT_TILES * P


class StageSemaphores:

    def __init__(self, nc):
        self.nc, self.held = nc, []

    def enter_context(self, semaphore):
        handle = semaphore.__enter__()
        self.held.append((semaphore, handle))
        return handle

    def clear(self):
        nums = sorted(h.num for _, h in self.held)
        starts = [n for n in nums if n - 1 not in nums]
        ends = [n + 1 for n in nums if n + 1 not in nums]
        for lo, hi in zip(starts, ends):
            self.nc.all_engine_barrier(sems_to_clear=range(lo, hi))
        for semaphore, _ in self.held:
            semaphore.__exit__(None, None, None)


def mamba_stage(nc, ctx, sh, A):
    HEADS, HD, DI, DS, TAPS = 8, 64, 512, 64, 4
    MX = DI // P
    PAD = TAPS - 1
    DT0, B0, C0, X0, Z0 = 2 * DI + 2 * DS, 2 * DI, 2 * DI + DS, DI, 0
    RMS_EPS, GN_EPS, LN_EPS = 1.1920929e-07, 1e-05, 1e-05
    PS, X, XN, XT, ident = sh.PS, sh.X, sh.XN, sh.XT, sh.ident

    stage = ExitStack()
    mhalf = sh.mhalf

    def sb(name, shape, dt=F32):
        return stage.enter_context(nc.sbuf_tensor("m_" + name, shape, dt))

    def sem(name):
        return ctx.enter_context(nc.semaphore("m_" + name))

    area = Area(sh.area)
    w_in = sb("w_in", [P, KD, 2 * DI + 2 * DS + HEADS])
    w_out = sb("w_out", [P, MX, D])
    rw1, rw2 = sb("rw1", [P, KD, 32]), sb("rw2", [32, 3])
    rb1, rb2 = sb("rb1", [32, 1]), sb("rb2", [P, 3])
    cwx, cbx = sb("cwx", [P, MX, TAPS]), sb("cbx", [P, MX])
    cwbc, cbbc = sb("cwbc", [DS, 2, TAPS]), sb("cbbc", [DS, 2])
    hp = sb("hp", [HEADS, 2])
    negA = sb("negA", [HEADS, 1])
    Dv, gw = sb("Dv", [P, MX]), sb("gw", [P, MX])
    tri = sb("tri", [P, P])
    sel = sb("sel", [HEADS, HEADS, P])
    XL = sb("XL", [P, NT, D])
    st6, mv, rstd = sb("st6", [P, NT, 6]), sb("mv", [P, NT, 2]), sb("rstd", [P, NT])
    ms = sb("ms", [P, NT])
    rr, rms = sb("rr", [P, NT]), sb("rms", [P, NT])
    xsum = sb("xsum", [P, KD, B])
    hid, hidB = sb("hid", [32, B]), sb("hidB", [32, B, P])
    lg, mxl, pr, psm = sb("lg", [P, B, 3]), sb("mxl", [P, B]), sb("pr", [P, B, 3]), sb("psm", [P, B])
    pmam = sb("pmam", [P, B])
    dtr, ab, sp, dt = (sb(n, [HEADS, T]) for n in ("dtr", "ab", "sp", "dt"))
    La = sb("La", [HEADS, T])
    TD = sb("TD", [P, 2, NT, HEADS])
    XC = [sb(f"XC{n}", [P, B, PAD + S]) for n in range(2)]
    CV = [sb(f"CV{n}", [P, B, S]) for n in range(2)]
    nw, ones = area.take([P, D]), area.take([P, S])
    XH = area.take([P, MX, T])
    BC = sb("BC", [DS, 2, T])
    SZ = area.take([P, MX, T])
    XD = area.take([P, NT, DI])
    GT = area.take([P, B, TB * BANK])
    Lm = [sb(f"Lm{n}", [P, TB, P]) for n in range(2)]
    E = [sb(f"E{n}", [P, 5 * BANK]) for n in range(2)]
    W = [sb(f"W{n}", [P, TB * BANK]) for n in range(2)]
    SQ, YG, YW = XH, SZ, SZ
    base = XL
    gr = sb("gr", [P, NT])
    yt = sb("yt", [P, S])

    small_in, w_in_in, w_out_in = sem("small_in"), sem("w_in_in"), sem("w_out_in")
    normed, squared, xn_ready = sem("normed"), sem("squared"), sem("xn_ready")
    xT_done, xT_ready = sem("xT_done"), sem("xT_ready")
    proj_done, proj_taken = sem("proj_done"), sem("proj_taken")
    hid_mm, hid_ready, hidB_ready, lg_mm, lg_ready, pr_ready = (
        sem(n) for n in ("hid_mm", "hid_ready", "hidB_ready", "lg_mm", "lg_ready", "pr_ready"))
    negA_ready, sp_ready, dt_ready, La_ready = sem("negA_ready"), sem("sp_ready"), sem("dt_ready"), sem("La_ready")
    td_mm, td_ready = sem("td_mm"), sem("td_ready")
    padded, conv_ready, silu_ready = sem("padded"), sem("conv_ready"), sem("silu_ready")
    xh_mm, xd_ready = sem("xh_mm"), sem("xd_ready")
    g_mm, g_copied, g_ready = sem("g_mm"), sem("g_copied"), sem("g_ready")
    decay_mm, diag_ready, e_ready, w_ready, y_mm, yg_ready = (
        sem(n) for n in ("decay_mm", "diag_ready", "e_ready", "w_ready", "y_mm", "yg_ready"))
    sq_ready, yw_ready, ss_mm, gr_ready, out_mm, base_ready = (
        sem(n) for n in ("sq_ready", "yw_ready", "ss_mm", "gr_ready", "out_mm", "base_ready"))
    var_ready, eps_added, rstd_ready, ms_ready, rms_ready = (
        sem(n) for n in ("var_ready", "eps_added", "rstd_ready", "ms_ready", "rms_ready"))
    own_v, own_a, own_p = sem("own_v"), sem("own_a"), sem("own_p")
    out_taken = sem("out_taken")

    mtiles = ([("dt", DT0, HEADS, 0), ("bc", B0, DS, 0), ("bc", C0, DS, 1)]
              + [("x", X0 + P * m, P, m) for m in range(MX)]
              + [("z", Z0 + P * m, P, m) for m in range(MX)])
    convs = [t for t in mtiles if t[0] in ("bc", "x")]
    NSMALL = 14

    with stage, nc.Block() as block:

        @block.sync
        def _(sp_):
            for dst, name in ((nw, "m_nw"), (rw1, "m_rw1"), (rw2, "m_rw2"), (rb1, "m_rb1"),
                              (rb2, "m_rb2"), (cwx, "m_cwx"), (cbx, "m_cbx"), (cwbc, "m_cwbc"),
                              (cbbc, "m_cbbc"), (hp, "m_hp"), (Dv, "m_D"), (gw, "m_gw"),
                              (tri, "tri"), (sel, "sel")):
                src = A[name]
                sp_.dma_start(dst[tuple(slice(None) for _ in dst.shape)], src).then_inc(small_in, 16)
            sp_.dma_start(w_in[:, :, :], A["m_win"]).then_inc(w_in_in, 16)
            sp_.dma_start(w_out[:, :, :], A["m_wout"]).then_inc(w_out_in, 16)
            zero_slots(sp_, sh)

        @block.gpsimd
        def _(pool):
            c = Chain(pool, own_p)
            for n in range(2):
                last = pool.memset(XC[n][:, :, 0:PAD], 0.0)
            pool.memset(ones[:, :], 1.0).then_inc(padded, 1)
            inverse_deviations_gpsimd(pool, mhalf, mv, rstd, LN_EPS, var_ready, eps_added, rstd_ready)
            for b in range(B):
                tiles = slice(b * TB, (b + 1) * TB)
                pool.wait_ge(ms_ready, b + 1)
                pool.tensor_tensor(rms[:, tiles], rr[:, tiles], mhalf[:, tiles], ALU.pow).then_inc(rms_ready, 1)
            pool.wait_ge(xn_ready, NT)
            c.link(pool.tensor_tensor(base[:, :, :], X[:, :, :], XL[:, :, :], ALU.add))
            pool.wait_ge(pr_ready, 1)
            pool.wait_ge(xT_done, KD * B)
            for i in range(NT):
                b = i // TB
                last = pool.tensor_scalar(XN[:, i, :], XN[:, i, :], pr[:, b, 0:1], None, ALU.mult)
            c.link(last)
            pool.tensor_tensor(base[:, :, :], base[:, :, :], XN[:, :, :], ALU.add).then_inc(base_ready, 1)
            pool.wait_ge(ms_ready, B + 1)
            pool.tensor_tensor(rr[:, :], gr[:, :], mhalf[:, :], ALU.pow).then_inc(rms_ready, 1)

        @block.vector
        def _(dve):
            c = Chain(dve, own_v)
            layernorm_vector(dve, c.link, X, XL, st6, mv, rstd, var_ready, rstd_ready, normed)
            for b in range(B):
                tiles = slice(b * TB, (b + 1) * TB)
                dve.wait_ge(squared, (b + 1) * TB)
                dve.tensor_scalar(rr[:, tiles], ms[:, tiles], 1.0 / D, RMS_EPS, ALU.mult, ALU.add).then_inc(ms_ready, 1)
            dve.wait_ge(small_in, 16 * NSMALL)
            for i in range(NT):
                dve.wait_ge(rms_ready, i // TB + 1)
                dve.scalar_tensor_tensor(out=XN[:, i, :], in0=XL[:, i, :], scalar=rms[:, i:i + 1],
                                         in1=nw[:, :], op0=ALU.mult, op1=ALU.mult).then_inc(xn_ready, 1)

            dve.wait_ge(hid_ready, 1)
            dve.tensor_copy(hidB[:, :, :], hid[:, :].unsqueeze(2).to_broadcast([32, B, P])).then_inc(hidB_ready, 1)

            dve.wait_ge(sp_ready, 1)
            c.link(dve.tensor_scalar(ab[:, :], dtr[:, :], 0.0, None, ALU.max))
            c.link(dve.tensor_tensor(dt[:, :], ab[:, :], sp[:, :], ALU.add))
            dve.wait_ge(negA_ready, 1)
            c.link(dve.tensor_scalar(ab[:, :], dt[:, :], negA[:, 0:1], -1.0, ALU.mult, ALU.mult))
            dve.wait_ge(padded, 1)
            for b in range(B):
                cols = slice(b * S, (b + 1) * S)
                last = dve.tensor_tensor_scan(La[:, cols], ones[0:HEADS, :], ab[:, cols], 0.0,
                                              ALU.mult, ALU.add)
            last.then_inc(La_ready, 1)

            dve.wait_ge(lg_mm, 1)
            c.link(dve.tensor_tensor(lg[:, :, :], PS[:, 1, 0:3 * B].rearrange("p (b e) -> p b e", b=B),
                                     rb2[:, :].unsqueeze(1).to_broadcast([P, B, 3]), ALU.add))
            c.link(dve.tensor_reduce(mxl[:, :], lg[:, :, :], AX.X, ALU.max))
            dve.tensor_tensor(lg[:, :, :], lg[:, :, :], mxl[:, :].unsqueeze(2).to_broadcast([P, B, 3]),
                              ALU.subtract).then_inc(lg_ready, 1)
            for n, (what, _, rows, m) in enumerate(convs):
                w = cwbc[:, m, :] if what == "bc" else cwx[:, m, :]
                xc, cv = XC[n % 2], CV[n % 2]
                dve.wait_ge(proj_taken, 2 * (n + 2))
                if n >= 2:
                    dve.wait_ge(silu_ready, n - 1)
                c.link(dve.tensor_scalar(cv[0:rows, :, :], xc[0:rows, :, 0:S], w[0:rows, 0:1], None, ALU.mult))
                for tap in range(1, TAPS):
                    last = dve.scalar_tensor_tensor(out=cv[0:rows, :, :], in0=xc[0:rows, :, tap:tap + S],
                                                    scalar=w[0:rows, tap:tap + 1], in1=cv[0:rows, :, :],
                                                    op0=ALU.mult, op1=ALU.add)
                    if tap < TAPS - 1:
                        c.link(last)
                last.then_inc(conv_ready, 1)
                if n == 1:
                    dve.wait_ge(td_mm, 1)
                    c.link(dve.tensor_copy(TD[:, 0, :, :], PS[:, 2, 0:NT * HEADS].rearrange("p (i h) -> p i h", i=NT)))
                    dve.tensor_scalar(TD[:, 1, :, :], PS[:, 2, NT * HEADS:2 * NT * HEADS].rearrange("p (i h) -> p i h", i=NT),
                                      -1.0, None, ALU.mult).then_inc(td_ready, 1)

            dve.wait_ge(lg_ready, 2)
            c.link(dve.tensor_reduce(psm[:, :], pr[:, :, :], AX.X, ALU.add))
            c.link(dve.reciprocal(mxl[:, :], psm[:, :]))
            c.link(dve.tensor_tensor(pr[:, :, :], pr[:, :, :], mxl[:, :].unsqueeze(2).to_broadcast([P, B, 3]),
                                     ALU.mult))
            dve.tensor_tensor(pmam[:, :], pr[:, :, 1], pr[:, :, 2], ALU.add).then_inc(pr_ready, 1)

            for n in range(B * TB):
                b, s = divmod(n, TB)
                dve.wait_ge(g_copied, n + 1)
                o = s * (BANK + P)
                dve.tensor_tensor(GT[:, b, o:o + P], GT[:, b, o:o + P], tri[:, :], ALU.mult).then_inc(g_ready, 1)

            for i in range(NT):
                dve.wait_ge(xh_mm, i + 1)
                dve.tensor_tensor(XD[:, i, :].rearrange("p (h c) -> p h c", h=HEADS),
                                  PS[:, 6 + i % 2, :].rearrange("p (h c) -> p h c", h=HEADS),
                                  TD[:, 0, i, :].unsqueeze(2).to_broadcast([P, HEADS, HD]),
                                  ALU.mult).then_inc(xd_ready, 1)

            def diagonal(n):
                b, h = divmod(n, HEADS)
                dve.wait_ge(decay_mm, n + 1)
                if n >= 2:
                    dve.wait_ge(e_ready, n - 1)
                for s in range(TB):
                    last = dve.tensor_scalar(Lm[n % 2][:, s, :], PS[:, n % 2, s * P:(s + 1) * P],
                                             TD[:, 1, b * TB + s, h:h + 1], 0.0, ALU.add, ALU.min)
                last.then_inc(diag_ready, 1)

            def weights(n):
                b = n // HEADS
                dve.wait_ge(e_ready, n + 1)
                if n >= 2:
                    dve.wait_ge(y_mm, n - 1)
                for s in range(TB):
                    o, m = s * BANK + s * P, S - s * P
                    last = dve.tensor_tensor(W[n % 2][:, o:o + m], E[n % 2][:, o:o + m], GT[:, b, o:o + m], ALU.mult)
                last.then_inc(w_ready, 1)

            def gate(n):
                b, h = divmod(n, HEADS)
                m = h // 2
                cols = slice(b * S, (b + 1) * S)
                dve.wait_ge(y_mm, n + 1)
                c.link(dve.scalar_tensor_tensor(out=yt[:, :], in0=XH[:, m, cols], scalar=Dv[:, m:m + 1],
                                                in1=PS[:, 2 + (n // 2) % 2, :], op0=ALU.mult, op1=ALU.add))
                dve.tensor_tensor(YG[:, m, cols], yt[:, :], SZ[:, m, cols], ALU.mult).then_inc(yg_ready, 1)

            diagonal(0)
            for n in range(B * HEADS):
                if n + 1 < B * HEADS:
                    diagonal(n + 1)
                weights(n)
                if n >= 2 and n % 2 == 0:
                    gate(n - 1)
            gate(B * HEADS - 1)

            dve.wait_ge(sq_ready, B * MX)
            for m in range(MX):
                last = dve.tensor_scalar(YW[:, m, :], YG[:, m, :], gw[:, m:m + 1], None, ALU.mult)
            last.then_inc(yw_ready, 1)
            dve.wait_ge(ss_mm, 1)
            dve.tensor_scalar(gr[:, :], PS[:, 6, 0:NT], 1.0 / DI, GN_EPS, ALU.mult, ALU.add).then_inc(ms_ready, 1)
            dve.wait_ge(rms_ready, B + 1)
            c.link(dve.tensor_tensor(gr[:, :].rearrange("p (b i) -> p b i", b=B),
                                     rr[:, :].rearrange("p (b i) -> p b i", b=B),
                                     pmam[:, :].unsqueeze(2).to_broadcast([P, B, TB]), ALU.mult))
            dve.wait_ge(base_ready, 1)
            for i in range(NT):
                dve.wait_ge(out_mm, i + 1)
                dve.scalar_tensor_tensor(out=X[:, i, :], in0=PS[:, i % 4, 0:D], scalar=gr[:, i:i + 1],
                                         in1=base[:, i, :], op0=ALU.mult, op1=ALU.add).then_inc(out_taken, 1)

        def silu_of(act, n):
            if n >= len(convs):
                return
            what, _, rows, m = convs[n]
            bias = cbbc[:, m:m + 1] if what == "bc" else cbx[:, m:m + 1]
            dst = BC if what == "bc" else XH
            act.wait_ge(conv_ready, n + 1)
            act.activation(dst[:, m, :], CV[n % 2][0:rows, :, :], ACT.Silu, bias=bias).then_inc(silu_ready, 1)

        @block.scalar
        def _(act):
            c = Chain(act, own_a)
            for i in range(NT):
                act.wait_ge(normed, i // TB + 1)
                act.activation(XN[:, i, :], XL[:, i, :], ACT.Square, accum_out=ms[:, i:i + 1]).then_inc(squared, 1)
            for g in range(KD * B):
                act.wait_ge(xT_done, g + 1)
                b, k = divmod(g, KD)
                act.activation(XT[:, k, b * S:(b + 1) * S], PS[:, g, :], ACT.Identity,
                               accum_out=xsum[:, k, b:b + 1]).then_inc(xT_ready, 1)
            act.wait_ge(small_in, 16 * NSMALL)
            act.activation(negA[:, :], hp[:, 1:2], ACT.Exp).then_inc(negA_ready, 1)
            for n, (what, _, rows, m) in enumerate(mtiles):
                for b in range(B):
                    j = 2 * n + b
                    act.wait_ge(proj_done, j + 1)
                    src = PS[0:rows, 4 + j % 4, :]
                    if what == "dt":
                        dst = dtr[:, b * S:(b + 1) * S]
                        act.activation(dst, src, ACT.Identity, bias=hp[:, 0:1]).then_inc(proj_taken, 1)
                    elif what == "z":
                        act.activation(SZ[:, m, b * S:(b + 1) * S], src, ACT.Silu).then_inc(proj_taken, 1)
                    else:
                        k = n - 1
                        if b == 0 and k >= 2:
                            act.wait_ge(conv_ready, k - 1)
                        if k == 0 and b == 0:
                            act.wait_ge(padded, 1)
                        act.activation(XC[k % 2][0:rows, b, PAD:PAD + S], src, ACT.Copy).then_inc(proj_taken, 1)
                if what == "dt":
                    act.wait_ge(proj_taken, 2)
                    c.link(act.activation(ab[:, :], dtr[:, :], ACT.Abs))
                    c.link(act.activation(dt[:, :], ab[:, :], ACT.Exp, scale=-1.0))
                    act.activation(sp[:, :], dt[:, :], ACT.Ln, bias=1.0).then_inc(sp_ready, 1)
                if n == 1:
                    act.wait_ge(hid_mm, 1)
                    act.activation(hid[:, :], PS[0:32, 0, 0:B], ACT.Silu, bias=rb1[:, 0:1],
                                   scale=1.0 / S).then_inc(hid_ready, 1)
                if n >= 2:
                    silu_of(act, n - 2)
            act.wait_ge(lg_ready, 1)
            act.activation(pr[:, :, :], lg[:, :, :], ACT.Exp).then_inc(lg_ready, 1)

            for n in range(B * TB):
                b, s = divmod(n, TB)
                act.wait_ge(g_mm, n + 1)
                o, m = s * (BANK + P), S - s * P
                act.activation(GT[:, b, o:o + m], PS[:, 4 + n % 2, s * P:S], ACT.Copy).then_inc(g_copied, 1)

            for n in range(B * HEADS):
                b, h = divmod(n, HEADS)
                e = E[n % 2]
                act.wait_ge(diag_ready, n + 1)
                if n >= 2:
                    act.wait_ge(w_ready, n - 1)
                for s in range(TB - 1):
                    o, m = s * BANK + (s + 1) * P, S - (s + 1) * P
                    act.activation(e[:, o:o + m], PS[:, n % 2, (s + 1) * P:S], ACT.Exp,
                                   bias=TD[:, 1, b * TB + s, h:h + 1])
                act.activation(e[:, :].rearrange("p (s c) -> p s c", s=TB)[:, :, 0:P], Lm[n % 2][:, :, :],
                               ACT.Exp).then_inc(e_ready, 1)
            for n in range(B * MX):
                b, m = divmod(n, MX)
                act.wait_ge(yg_ready, n + 1)
                cols = slice(b * S, (b + 1) * S)
                act.activation(SQ[:, m, cols], YG[:, m, cols], ACT.Square).then_inc(sq_ready, 1)

        @block.tensor
        def _(pe):
            pe.wait_ge(small_in, 16 * NSMALL)
            transposes_tensor(pe, PS, XN, ident, xn_ready, TB, xT_done)
            pe.wait_ge(w_in_in, 16)
            for n, (what, col, rows, m) in enumerate(mtiles):
                for b in range(B):
                    j = 2 * n + b
                    pe.wait_ge(xT_ready, KD * B)
                    if j >= 4:
                        pe.wait_ge(proj_taken, j - 3)
                    for k in range(KD):
                        last = pe.matmul(PS[0:rows, 4 + j % 4, :], w_in[:, k, col:col + rows],
                                         XT[:, k, b * S:(b + 1) * S], start=(k == 0), stop=(k == KD - 1))
                    last.then_inc(proj_done, 1)
                if n == 0:
                    for k in range(KD):
                        last = pe.matmul(PS[0:32, 0, 0:B], rw1[:, k, :], xsum[:, k, :], start=(k == 0),
                                         stop=(k == KD - 1))
                    last.then_inc(hid_mm, 1)
                if n == 3:
                    pe.wait_ge(hidB_ready, 1)
                    for b in range(B):
                        last = pe.matmul(PS[:, 1, 3 * b:3 * b + 3], hidB[:, b, :], rw2[:, :], start=True, stop=True)
                    last.then_inc(lg_mm, 1)
                if n == 4:
                    pe.wait_ge(La_ready, 1)
                    for a, src in enumerate((dt, La)):
                        for i in range(NT):
                            o = (a * NT + i) * HEADS
                            last = pe.transpose(PS[:, 2, o:o + HEADS], src[:, i * P:(i + 1) * P],
                                                ident[0:HEADS, 0:HEADS])
                    last.then_inc(td_mm, 1)
            pe.wait_ge(silu_ready, 2)
            pe.wait_ge(td_ready, 1)
            pe.wait_ge(lg_ready, 1)
            pe.wait_ge(proj_taken, 2 * len(mtiles))
            for n in range(B * TB):
                b, s = divmod(n, TB)
                if n >= 2:
                    pe.wait_ge(g_copied, n - 1)
                pe.matmul(PS[:, 4 + n % 2, s * P:S], BC[:, 0, b * S + s * P:b * S + (s + 1) * P],
                          BC[:, 1, b * S + s * P:(b + 1) * S], start=True, stop=True).then_inc(g_mm, 1)
            pe.wait_ge(silu_ready, len(convs))
            for i in range(NT):
                if i >= 2:
                    pe.wait_ge(xd_ready, i - 1)
                for m in range(MX):
                    last = pe.transpose(PS[:, 6 + i % 2, m * P:(m + 1) * P], XH[:, m, i * P:(i + 1) * P], ident[:, :])
                last.then_inc(xh_mm, 1)

            def decay(n):
                b, h = divmod(n, HEADS)
                if n >= 2:
                    pe.wait_ge(e_ready, n - 1)
                pe.matmul(PS[:, n % 2, :], sel[:, h, :], La[:, b * S:(b + 1) * S], start=True,
                          stop=True).then_inc(decay_mm, 1)

            decay(0)
            decay(1)
            pe.wait_ge(xd_ready, NT)
            for n in range(B * HEADS):
                b, h = divmod(n, HEADS)
                half = slice((h % 2) * HD, (h % 2 + 1) * HD)
                if n + 2 < B * HEADS:
                    decay(n + 2)
                pe.wait_ge(w_ready, n + 1)
                if n >= 4 and n % 2 == 0:
                    pe.wait_ge(yg_ready, n // 2 - 1)
                for s in range(TB):
                    o, m = s * BANK + s * P, S - s * P
                    last = pe.matmul(PS[half, 2 + (n // 2) % 2, s * P:S], XD[:, b * TB + s, h * HD:(h + 1) * HD],
                                     W[n % 2][:, o:o + m], start=(s == 0), stop=(s == TB - 1),
                                     skip_group_check=True)
                last.then_inc(y_mm, 1)
            pe.wait_ge(sq_ready, B * MX)
            for i in range(NT):
                for m in range(MX):
                    last = pe.matmul(PS[:, 6, i:i + 1], SQ[:, m, i * P:(i + 1) * P], ones[:, 0:1],
                                     start=(m == 0), stop=(m == MX - 1))
            last.then_inc(ss_mm, 1)
            pe.wait_ge(w_out_in, 16)
            pe.wait_ge(yw_ready, 1)
            for i in range(NT):
                if i >= 4:
                    pe.wait_ge(out_taken, i - 3)
                for m in range(MX):
                    last = pe.matmul(PS[:, i % 4, 0:D], YW[:, m, i * P:(i + 1) * P], w_out[:, m, :],
                                     start=(m == 0), stop=(m == MX - 1))
                last.then_inc(out_mm, 1)


HEADS, HD = 16, 16
GH = 4
NG = HEADS // GH
UNITS = B * NG
VW = 32
NBLK = 6
K_ROWS = (2, 1, 0)
Q_ROWS = (0, 1, 2, 0)
K_RUNS = (0, HD, 2 * HD)
Q_RUNS = (0, 0, 3 * HD)
STACK_RUNS = (0, 3 * HD, 5 * HD, NBLK * HD + 3)
TAIL = NBLK * HD
TAIL_ROWS = 3
ROWS = TAIL + TAIL_ROWS
K_DRAM, Q_DRAM = len(K_ROWS) * HD + TAIL_ROWS, len(Q_ROWS) * HD + TAIL_ROWS
MASKED = 2.0 ** 32


class Attention:

    LOADS = 7

    def __init__(self, nc, ctx, stage, PS, name, NK, KH, ident, identb):
        def sb(n, shape, dt=F32):
            return stage.enter_context(nc.sbuf_tensor(name + n, shape, dt))

        def sem(n):
            return ctx.enter_context(nc.semaphore(name + n))

        self.PS, self.ident, self.identb = PS, ident, identb
        self.NK, self.KT, self.C, self.KH = NK, NK // P, TB * NK // BANK, KH
        self.Qs = [sb(f"Qs{n}", [ROWS, GH, S], BF16) for n in range(3)]
        self.Ks = [sb(f"Ks{n}", [ROWS, KH, NK], BF16) for n in range(3)]
        self.Vs = [sb(f"Vs{n}", [P, NK // P, KH, VW]) for n in range(3)]
        self.qtail = sb("qtail", [TAIL_ROWS, GH * S], BF16)
        self.E = [sb(f"E{n}", [P, GH, S]) for n in range(2)]
        self.mx = sb("mx", [P, TB, GH, 2])
        self.m = sb("m", [P, TB, GH])
        self.MT = sb("MT", [P, TB, GH, VW], BF16)
        self.Oraw = sb("Oraw", [P, S])
        self.rc = sb("rc", [P, TB, GH])
        self.Otok = sb("Otok", [P, UNITS, TB, GH * HD])
        self.loaded = [sem(f"loaded{n}") for n in range(3)]
        (self.s_done, self.max_done, self.m_ready, self.mT_done, self.q_ready,
         self.st_done, self.exp_done, self.av_done, self.o_copied, self.oT_done, self.o_normed, self.own) = (
            sem(n) for n in ("s_done", "max_done", "m_ready", "mT_done", "q_ready",
                             "st_done", "exp_done", "av_done", "o_copied", "oT_done", "o_normed", "own"))
        self.m_final, self.mt_set = sem("m_final"), sem("mt_set")

    def steps(self, eng, step):
        step(0, 0, 0, first=True)
        with eng.Fori(0, (UNITS - 2) // 3) as i:
            for n in range(1, 4):
                step(i * 3 + n, n % 3, i + (n + 1) // 3)
        step(UNITS - 1, (UNITS - 1) % 3, None, last=True)

    def sync(self, sp, load, between, also=None):
        for u in range(2):
            load(u, u)
        between()
        with sp.Fori(0, (UNITS - 2) // 3) as i:
            for n in range(2, 5):
                u = i * 3 + n
                sp.wait_ge(self.av_done, (u - 2) * (2 * self.KT))
                load(u, n % 3)
                if also:
                    also(u)

    def tensor(self, pe, between=None):
        PS, KT, C = self.PS, self.KT, self.C

        def scores(u, buf, rnd, c, j, first=False):
            qt, half = divmod(c, C // TB)
            if c == 0 and j == 0:
                pe.wait_ge(self.loaded[buf], (rnd + 1) * (16 * self.LOADS))
            if not (first and c == 0 and j < 2):
                pe.wait_ge(self.max_done, u * (GH * C) + (GH * c + j - 1))
            pe.matmul(PS[:, j % 2, :], self.Qs[buf][:, j, qt * P:(qt + 1) * P],
                      self.Ks[buf][:, j % self.KH, half * BANK:(half + 1) * BANK],
                      start=True, stop=True).then_inc(self.s_done, 1)

        def transposed_scores(u, buf, kt, p, first):
            if kt == 0 and p == 0:
                pe.wait_ge(self.q_ready, u * 2 + 2)
            if not (first and kt == 0):
                pe.wait_ge(self.exp_done, u * (2 * KT) + (2 * kt + p - 1))
            for j in (2 * p, 2 * p + 1):
                last = pe.matmul(PS[:, 2 + j, :], self.Ks[buf][:, j % self.KH, kt * P:(kt + 1) * P],
                                 self.Qs[buf][:, j, :], start=True, stop=True)
            last.then_inc(self.st_done, 1)

        def values(u, buf, kt, p, first=False):
            pe.wait_ge(self.exp_done, u * (2 * KT) + (2 * kt + p + 1))
            if kt == 0 and p == 0 and not first:
                pe.wait_ge(self.o_copied, u)
            for j in (2 * p, 2 * p + 1):
                last = pe.matmul(PS[32 * j:32 * j + 32, 6, :], self.Vs[buf][:, kt, j % self.KH, :],
                                 self.E[kt % 2][:, j, :], start=(kt == 0), stop=(kt == KT - 1),
                                 skip_group_check=True)
            last.then_inc(self.av_done, 1)

        def maxima_transposes(u):
            pe.wait_ge(self.m_ready, u + 1)
            for qt in range(TB):
                last = pe.transpose(PS[:, 7, :].bitcast(BF16)[:, qt * P:(qt + 1) * P],
                                    self.MT[:, qt, :, :].rearrange("p j c -> p (j c)"), self.identb[:, :])
            last.then_inc(self.mT_done, 1)

        def output_transposes(u):
            pe.wait_ge(self.o_copied, u + 1)
            for qt in range(TB):
                last = pe.transpose(PS[:, 7, qt * P:(qt + 1) * P], self.Oraw[:, qt * P:(qt + 1) * P],
                                    self.ident[:, :])
            last.then_inc(self.oT_done, 1)

        def step(u, buf, nxt, first=False, last=False):
            for p in range(2):
                if not last:
                    scores(u + 1, (buf + 1) % 3, nxt, 0, p)
            maxima_transposes(u)
            if not first:
                for p in range(2):
                    values(u - 1, (buf + 2) % 3, KT - 1, p)
            for kt in range(KT):
                for p in range(2):
                    if not last and kt > 0:
                        scores(u + 1, (buf + 1) % 3, nxt, kt, 2 * p)
                    transposed_scores(u, buf, kt, p, first)
                    if not last:
                        scores(u + 1, (buf + 1) % 3, nxt, kt, 2 + p if kt == 0 else 2 * p + 1)
                    if kt > 0:
                        values(u, buf, kt - 1, p, first)
                if kt == 1 and not first:
                    output_transposes(u - 1)

        for c in range(C):
            for j in range(GH):
                scores(0, 0, 0, c, j, first=True)
        if between:
            between()
        self.steps(pe, step)
        for p in range(2):
            values(UNITS - 1, (UNITS - 1) % 3, KT - 1, p)
        pe.wait_ge(self.o_normed, UNITS - 1)
        output_transposes(UNITS - 1)

    def vector(self, dve, between=None):
        PS, C = self.PS, self.C

        def maxima(u, c, heads=range(GH)):
            qt, half = divmod(c, C // TB)
            for j in heads:
                dve.wait_ge(self.s_done, u * (GH * C) + (GH * c + j + 1))
                dve.tensor_reduce(self.mx[:, qt, j, half:half + 1], PS[:, j % 2, :], AX.X,
                                  ALU.max).then_inc(self.max_done, 1)

        def negated(u, first=False):
            dve.wait_ge(self.max_done, (u + 1) * (GH * C))
            if C > TB:
                dve.tensor_tensor(self.m[:, :, :], self.mx[:, :, :, 0], self.mx[:, :, :, 1],
                                  ALU.max).then_inc(self.m_final, 1)
            else:
                dve.tensor_copy(self.m[:, :, :], self.mx[:, :, :, 0]).then_inc(self.m_final, 1)
            dve.wait_ge(self.m_final, u * 2 + 1)
            if not first:
                dve.wait_ge(self.mT_done, u)
            dve.tensor_scalar(self.MT[:, :, :, 0], self.m[:, :, :], -1.0, None, ALU.mult).then_inc(self.m_final, 1)
            dve.wait_ge(self.m_final, u * 2 + 2)
            dve.scalar_tensor_tensor(out=self.MT[:, :, :, 1], in0=self.m[:, :, :], scalar=-1.0,
                                     in1=self.MT[:, :, :, 0], op0=ALU.mult,
                                     op1=ALU.subtract).then_inc(self.m_ready, 1)

        def tails(u, buf):
            dve.wait_ge(self.mT_done, u + 1)
            for j in (2, 3):
                last = dve.tensor_copy(self.Qs[buf][TAIL:ROWS, j, :],
                                       PS[32 * j:32 * j + TAIL_ROWS, 7, :].bitcast(BF16)[:, 0:S])
            last.then_inc(self.q_ready, 1)

        def normalise(u):
            src = PS[:, 7, :].rearrange("p (t j c) -> p t j c", t=TB, j=GH)
            dve.wait_ge(self.oT_done, u + 1)
            dve.reciprocal(self.rc[:, :, :], src[:, :, :, HD]).then_inc(self.own, 1)
            dve.wait_ge(self.own, u + 1)
            for qt in range(TB):
                last = dve.tensor_tensor(
                    self.Otok[:, bass.ds(u, 1), qt, :]
                    .rearrange("p u (j c) -> p (u j) c", j=GH),
                    src[:, qt, :, 0:HD], self.rc[:, qt, :].unsqueeze(2).to_broadcast([P, GH, HD]), ALU.mult)
            last.then_inc(self.o_normed, 1)

        def step(u, buf, nxt, first=False, last=False):
            if not last:
                maxima(u + 1, 0, (0, 1))
            tails(u, buf)
            if not last:
                maxima(u + 1, 0, (2, 3))
                maxima(u + 1, 1)
            if not first:
                normalise(u - 1)
            if not last:
                for c in range(2, C):
                    maxima(u + 1, c)
                negated(u + 1)

        dve.memset(self.MT[:, :, :, :], 0.0).then_inc(self.mt_set, 1)
        dve.wait_ge(self.mt_set, 1)
        dve.memset(self.MT[:, :, :, 2], 1.0).then_inc(self.mt_set, 1)
        dve.wait_ge(self.mt_set, 2)
        for c in range(C):
            maxima(0, c)
        negated(0, first=True)
        if between:
            between()
        self.steps(dve, step)
        normalise(UNITS - 1)

    def scalar(self, act):
        PS, KT = self.PS, self.KT

        def tails(u, buf):
            act.wait_ge(self.mT_done, u + 1)
            for j in (0, 1):
                last = act.activation(self.Qs[buf][TAIL:ROWS, j, :],
                                      PS[32 * j:32 * j + TAIL_ROWS, 7, :].bitcast(BF16)[:, 0:S], ACT.Copy)
            last.then_inc(self.q_ready, 1)

        def copy_output(u, last=False):
            act.wait_ge(self.av_done, (u + 1) * (2 * KT))
            if last:
                act.wait_ge(self.oT_done, u)
            else:
                act.wait_ge(self.mT_done, u + 2)
            act.activation(self.Oraw[:, :], PS[:, 6, :], ACT.Copy).then_inc(self.o_copied, 1)

        def step(u, buf, nxt, first=False, last=False):
            tails(u, buf)
            for kt in range(KT):
                for p in range(2):
                    act.wait_ge(self.st_done, u * (2 * KT) + (2 * kt + p + 1))
                    if not (first and kt < 2):
                        act.wait_ge(self.av_done, u * (2 * KT) + (2 * kt + p - 3))
                    act.activation(self.E[kt % 2][:, 2 * p:2 * p + 2, :], PS[:, 2 + 2 * p:4 + 2 * p, :],
                                   ACT.Exp, scale=0.25).then_inc(self.exp_done, 1)
                if kt == 0 and not first:
                    copy_output(u - 1)

        self.steps(act, step)
        copy_output(UNITS - 1, last=True)


class Splitter:

    def __init__(self, nc, ctx, space, name, dst, rows, n):
        self.F, self.R = [space[:, i, :] for i in range(2)], [space[:, 2 + i, :] for i in range(2)]
        self.dst, self.rows, self.n = dst, rows, n
        self.f_ready, self.p0_ready, self.r_ready, self.p1_ready, self.p2_ready = (
            ctx.enter_context(nc.semaphore(f"{name}{s}"))
            for s in ("f_ready", "p0_ready", "r_ready", "p1_ready", "p2_ready"))

    def buffer(self, dve, n):
        if n >= 2:
            dve.wait_ge(self.r_ready, n - 1)
        return self.F[n % 2][0:self.rows[n]]

    def scalar(self, act, lo, hi):
        for n in range(lo, hi + 1):
            if n < hi:
                act.wait_ge(self.f_ready, n + 1)
                act.activation(self.dst(n, 0), self.F[n % 2][0:self.rows[n]], ACT.Copy).then_inc(self.p0_ready, 1)
            if n > lo:
                act.wait_ge(self.r_ready, n)
                act.activation(self.dst(n - 1, 1), self.R[(n - 1) % 2][0:self.rows[n - 1]],
                               ACT.Copy).then_inc(self.p1_ready, 1)

    def gpsimd(self, pool, lo, hi):
        for n in range(lo, hi):
            f, r = self.F[n % 2][0:self.rows[n]], self.R[n % 2][0:self.rows[n]]
            pool.wait_ge(self.p0_ready, n + 1)
            if n >= 2:
                pool.wait_ge(self.p2_ready, n - 1)
            pool.tensor_tensor(r, f, self.dst(n, 0), ALU.subtract).then_inc(self.r_ready, 1)
            pool.wait_ge(self.p1_ready, n + 1)
            pool.tensor_tensor(self.dst(n, 2), r, self.dst(n, 1), ALU.subtract).then_inc(self.p2_ready, 1)


K_STORES, Q_STORES = 2 * len(K_ROWS), 2 * len(Q_ROWS)


def store_query_tails(sp, q_stack, qtail, done):
    sp.dma_start(q_stack[:, Q_DRAM - TAIL_ROWS:, :, :].rearrange("u r h n -> r u (h n)"),
                 qtail[:, :].unsqueeze(1).to_broadcast([TAIL_ROWS, UNITS, GH * S])).then_inc(done, 16)


def store_parts(sp, stack, order, parts, b, done):
    groups = NG // KD
    for slot, part in enumerate(order):
        for g in range(groups):
            dst = stack[b * NG:(b + 1) * NG, slot * HD:(slot + 1) * HD, :, :]
            dst = dst.rearrange("(m g) d h n -> g (d h) m n", m=KD)[g]
            src = parts(part)[g * GH * HD:(g + 1) * GH * HD, :, :]
            sp.dma_start(dst, src).then_inc(done, 16)


def load_unit(sp, at, q_stack, k_stack, values):
    def load(u, buf):
        for dst, src, runs in ((at.Ks[buf], k_stack, K_RUNS), (at.Qs[buf], q_stack, Q_RUNS)):
            for r, row in enumerate(runs):
                lo, hi = STACK_RUNS[r], STACK_RUNS[r + 1]
                sp.dma_start(dst[lo:hi, :, :], src[bass.ds(u, 1), row:row + hi - lo, :, :]
                             .rearrange("u r h n -> r (u h) n")).then_inc(at.loaded[buf], 16)
        sp.dma_start(at.Vs[buf][:, :, :, :],
                     values[:, bass.ds(u, 1), :, :, :].rearrange("p u t h c -> p (u t) h c")).then_inc(at.loaded[buf], 16)
    return load


def project_out(nc, at, sh, sem, w, w_in, w_val):
    PS, X, XT = sh.PS, sh.X, sh.XT
    oT_done, oT_ready, out_mm = sem("po_oT_done"), sem("po_oT_ready"), sem("po_out_mm")
    out_taken, o_placed = sem("po_out_taken"), sem("po_o_placed")

    def tensor(pe):
        pe.wait_ge(o_placed, B)
        for k in range(KD):
            for b in range(B):
                for qt in range(TB):
                    last = pe.transpose(PS[:, 2 * k + b, qt * P:(qt + 1) * P], sh.XN[:, b * TB + qt, k * P:(k + 1) * P],
                                        sh.ident[:, :])
                last.then_inc(oT_done, 1)
        pe.wait_ge(oT_ready, KD * B)
        pe.wait_ge(w_in, w_val)
        for i in range(NT):
            if i >= 4:
                pe.wait_ge(out_taken, i - 3)
            for k in range(KD):
                last = pe.matmul(PS[:, 4 + i % 4, 0:D], XT[:, k, i * P:(i + 1) * P], w[:, k, :],
                                 start=(k == 0), stop=(k == KD - 1))
            last.then_inc(out_mm, 1)

    def scalar(act):
        for g in range(KD * B):
            k, b = divmod(g, B)
            act.wait_ge(oT_done, g + 1)
            act.activation(XT[:, k, b * S:(b + 1) * S], PS[:, g, :], ACT.Copy).then_inc(oT_ready, 1)

    def vector(dve):
        dve.wait_ge(at.o_normed, UNITS)
        for b in range(B):
            dve.tensor_copy(sh.XN[:, b * TB:(b + 1) * TB, :].rearrange("p t (g c) -> p g t c", g=NG),
                            at.Otok[:, b * NG:(b + 1) * NG, :, :]).then_inc(o_placed, 1)
        for i in range(NT):
            dve.wait_ge(out_mm, i + 1)
            dve.tensor_tensor(X[:, i, :], X[:, i, :], PS[:, 4 + i % 4, 0:D], ALU.add).then_inc(out_taken, 1)

    return tensor, scalar, vector


class Norm:

    def __init__(self, nc, ctx, stage, sh, name, eps=1e-05):
        def sb(n, shape):
            return stage.enter_context(nc.sbuf_tensor(name + n, shape, F32))
        self.sh, self.eps = sh, eps
        self.st6, self.mv, self.rstd = sb("st6", [P, NT, 6]), sb("mv", [P, NT, 2]), sb("rstd", [P, NT])
        self.own, self.var_ready, self.eps_added, self.rstd_ready, self.xn_ready, self.xT_done, self.xT_ready = (
            ctx.enter_context(nc.semaphore(name + n))
            for n in ("own", "var_ready", "eps_added", "rstd_ready", "xn_ready", "xT_done", "xT_ready"))

    def vector(self, dve):
        c = Chain(dve, self.own)
        layernorm_vector(dve, c.link, self.sh.X, self.sh.XN, self.st6, self.mv, self.rstd,
                         self.var_ready, self.rstd_ready, self.xn_ready)

    def gpsimd(self, pool):
        inverse_deviations_gpsimd(pool, self.sh.mhalf, self.mv, self.rstd, self.eps, self.var_ready,
                                  self.eps_added, self.rstd_ready)

    def tensor(self, pe):
        transposes_tensor(pe, self.sh.PS, self.sh.XN, self.sh.ident, self.xn_ready, 1, self.xT_done)

    def scalar(self, act):
        for g in range(KD * B):
            b, k = divmod(g, KD)
            act.wait_ge(self.xT_done, g + 1)
            act.activation(self.sh.XT[:, k, b * S:(b + 1) * S], self.sh.PS[:, g, :], ACT.Copy).then_inc(self.xT_ready, 1)


def cross_stage(nc, ctx, sh, A):
    NK = 1024
    PS, X, XN, XT = sh.PS, sh.X, sh.XN, sh.XT
    stage = ExitStack()

    def sb(name, shape, dt=F32):
        return stage.enter_context(nc.sbuf_tensor("c_" + name, shape, dt))

    def sem(name):
        return ctx.enter_context(nc.semaphore("c_" + name))

    area = Area(sh.area)

    nm = Norm(nc, ctx, stage, sh, "c_n")
    wo, bo = sb("wo", [P, KD, D]), sb("bo", [P, D])
    VB = sb("VB", [P, UNITS, NK // P, GH, VW])
    at = Attention(nc, ctx, stage, PS, "c_a", NK, GH, sh.ident, sh.identb)
    ctxT = area.take([P, KD, B * NK])
    wq, wk, wv = (area.take([P, KD, D]) for _ in range(3))
    bq, bk = area.take([P, KD]), area.take([P, KD])
    bv = area.take([P, D])
    maski = at.E[0][:, :, :].rearrange("p j s -> p (j s)").bitcast(I32).rearrange("p (b n) -> p b n", b=B)
    ind = area.take([P, B, NK])
    ktc = area.take([TAIL_ROWS, 2])
    otok = at.Otok[0:TAIL_ROWS, :, :, :].rearrange("r u t c -> r (u t c)").bitcast(BF16)
    ktail = otok[:, 0:B * NK].rearrange("r (b n) -> r b n", b=B)
    KP = [area.take([P, B, KD, NK], BF16) for _ in range(3)]
    QP = [area.take([P, KD, T], BF16) for _ in range(3)]
    q_stack = nc.dram_tensor("c_q_stack", [UNITS, Q_DRAM, GH, S], BF16, kind="Internal").ap()
    k_stack = nc.dram_tensor("c_k_stack", [UNITS, K_DRAM, GH, NK], BF16, kind="Internal").ap()

    small_in, wv_in, wo_in, mask_in = (sem(n) for n in ("small_in", "wv_in", "wo_in", "mask_in"))
    ctx_in = [sem(f"ctx_in{b}") for b in range(B)]
    NSMALL = 6
    proj_done, proj_taken = sem("proj_done"), sem("proj_taken")
    ind_ready, tail_ready, tail_stored = sem("ind_ready"), sem("tail_ready"), sem("tail_stored")
    k_stored = [sem(f"k_stored{b}") for b in range(B)]
    q_stored = [sem(f"q_stored{b}") for b in range(B)]
    v_ones, xb_ready, qtail_set = sem("v_ones"), sem("xb_ready"), sem("qtail_set")
    NKC = B * KD * 2
    NV = B * NK // P
    NQC = B * KD

    def k_chunk(n):
        n -= NQC
        return n // 4, n // 2 % 2, n % 2

    def dst(n, part):
        if n >= NQC:
            b, m, half = k_chunk(n)
            return KP[part][:, b, m, half * BANK:(half + 1) * BANK]
        b, m = divmod(n, KD)
        return QP[part][:, m, b * S:(b + 1) * S]

    sp_l = Splitter(nc, ctx, at.E[1][:, :, :], "c_s", dst, [P] * (NKC + NQC), NKC + NQC)
    po_t, po_s, po_v = project_out(nc, at, sh, sem, wo, wo_in, 16)

    with stage, nc.Block() as block:

        @block.sync
        def _(sp):
            for d, name in ((wq, "c_wq"), (bq, "c_bq"), (wk, "c_wk"), (bk, "c_bk"), (ktc, "c_ktc"), (bv, "c_bv")):
                sp.dma_start(d[tuple(slice(None) for _ in d.shape)], A[name]).then_inc(small_in, 16)
            sp.dma_start(maski, A["mask"].unsqueeze(0).to_broadcast([P, B, NK])).then_inc(mask_in, 16)
            for b in range(B):
                sp.dma_start(ctxT[:, :, b * NK:(b + 1) * NK], A["ctxT"][:, :, b * NK:(b + 1) * NK]).then_inc(ctx_in[b], 16)
            sp.dma_start(wv[:, :, :], A["c_wv"]).then_inc(wv_in, 16)
            sp.dma_start(wo[:, :, :], A["c_wo"]).then_inc(wo_in, 16)
            sp.dma_start(bo[:, :], A["c_bo"]).then_inc(wo_in, 16)
            sp.wait_ge(qtail_set, 2)
            store_query_tails(sp, q_stack, at.qtail, tail_stored)
            sp.wait_ge(tail_ready, B)
            for b in range(B):
                for h in range(GH):
                    sp.dma_start(k_stack[b * NG:(b + 1) * NG, K_DRAM - TAIL_ROWS:, h, :].rearrange("u r n -> r u n"),
                                 ktail[:, b, :].unsqueeze(1).to_broadcast([TAIL_ROWS, NG, NK])).then_inc(tail_stored, 16)

            for b in range(B):
                sp.wait_ge(sp_l.p2_ready, (b + 1) * KD)
                store_parts(sp, q_stack, Q_ROWS, lambda part: QP[part][:, :, b * S:(b + 1) * S], b, q_stored[b])

            def store_k(b):
                sp.wait_ge(sp_l.p2_ready, NQC + (b + 1) * NKC // B)
                store_parts(sp, k_stack, K_ROWS, lambda part: KP[part][:, b, :, :], b, k_stored[b])

            def rest():
                store_k(1)
                sp.wait_ge(k_stored[1], 16 * K_STORES)
                sp.wait_ge(q_stored[1], 16 * Q_STORES)

            store_k(0)
            sp.wait_ge(tail_stored, 16 * (1 + B * GH))
            sp.wait_ge(k_stored[0], 16 * K_STORES)
            sp.wait_ge(q_stored[0], 16 * Q_STORES)
            sp.wait_ge(proj_taken, NV)
            weights = sh.weights[0]
            at.sync(sp, load_unit(sp, at, q_stack, k_stack, VB), rest, also=lambda u: weights.load_expert(sp, u))
            for e in range(2):
                weights.load_expert(sp, e)

        @block.gpsimd
        def _(pool):
            pool.memset(at.qtail[:, :], 0.0).then_inc(qtail_set, 1)
            nm.gpsimd(pool)
            pool.wait_ge(qtail_set, 1)
            pool.tensor_scalar(at.qtail[:, :], at.qtail[:, :], sh.query_tail[:, 0:1], None,
                               ALU.add).then_inc(qtail_set, 1)
            pool.wait_ge(qtail_set, 2)
            for g in range(UNITS):
                last = pool.memset(VB[:, g, :, :, HD:VW], 1.0)
            last.then_inc(v_ones, 1)
            sp_l.gpsimd(pool, 0, NKC + NQC)
            pool.wait_ge(wo_in, 32)
            pool.wait_ge(nm.xn_ready, B)
            for i in range(NT):
                last = pool.tensor_tensor(X[:, i, :], X[:, i, :], bo[:, :], ALU.add)
            last.then_inc(xb_ready, 1)
        @block.vector
        def _(dve):
            nm.vector(dve)
            dve.wait_ge(small_in, 16 * NSMALL)
            for n in range(NQC):
                b, m = divmod(n, KD)
                dve.wait_ge(proj_done, n + 1)
                f = sp_l.buffer(dve, n)
                dve.tensor_scalar(f, PS[:, 4 + n % 4, :], bq[:, m:m + 1], None, ALU.add).then_inc(sp_l.f_ready, 1)
            dve.wait_ge(mask_in, 16)
            dve.tensor_scalar(ind[:, :, :], maski, 0.0, None, ALU.not_equal).then_inc(ind_ready, 1)
            dve.wait_ge(ind_ready, 1)
            for b in range(B):
                dve.tensor_scalar(ktail[:, b, :], ind[0:TAIL_ROWS, b, :], ktc[:, 0:1], ktc[:, 1:2], ALU.mult,
                                  ALU.add).then_inc(tail_ready, 1)
            for n in range(NQC, NQC + NKC):
                b, m, half = k_chunk(n)
                dve.wait_ge(proj_done, n + 1)
                f = sp_l.buffer(dve, n)
                dve.scalar_tensor_tensor(out=f, in0=PS[:, 4 + n % 4, :], scalar=bk[:, m:m + 1],
                                         in1=ind[:, b, half * BANK:(half + 1) * BANK], op0=ALU.add,
                                         op1=ALU.mult).then_inc(sp_l.f_ready, 1)
            dve.wait_ge(v_ones, 1)
            for t in range(NV):
                n = NQC + NKC + t
                b, kt = divmod(t, NK // P)
                dve.wait_ge(proj_done, n + 1)
                dve.tensor_tensor(VB[:, b * NG:(b + 1) * NG, kt, :, 0:HD],
                                  PS[:, 4 + n % 4, 0:D].rearrange("p (g h c) -> p g h c", g=NG, h=GH),
                                  bv[:, :].rearrange("p (g h c) -> p g h c", g=NG, h=GH),
                                  ALU.add).then_inc(proj_taken, 1)
            at.vector(dve)
            dve.wait_ge(xb_ready, 1)
            po_v(dve)

        @block.scalar
        def _(act):
            nm.scalar(act)
            sp_l.scalar(act, 0, NQC + NKC)
            act.wait_ge(sp_l.p2_ready, NQC + NKC)
            at.scalar(act)
            po_s(act)

        @block.tensor
        def _(pe):
            nm.tensor(pe)
            pe.wait_ge(small_in, 16 * NSMALL)
            NF = NQC + NKC

            def bank_free(j):
                if 4 <= j < NF + 4:
                    pe.wait_ge(sp_l.f_ready, j - 3)
                elif j >= NF + 4:
                    pe.wait_ge(proj_taken, j - 3 - NF)

            for n in range(NQC):
                b, m = divmod(n, KD)
                if m == 0:
                    pe.wait_ge(nm.xT_ready, KD * (b + 1))
                bank_free(n)
                for k in range(KD):
                    last = pe.matmul(PS[:, 4 + n % 4, :], wq[:, k, m * P:(m + 1) * P], XT[:, k, b * S:(b + 1) * S],
                                     start=(k == 0), stop=(k == KD - 1))
                last.then_inc(proj_done, 1)
            for n in range(NQC, NF):
                b, m, half = k_chunk(n)
                pe.wait_ge(ctx_in[b], 16)
                bank_free(n)
                for k in range(KD):
                    c0 = b * NK + half * BANK
                    last = pe.matmul(PS[:, 4 + n % 4, :], wk[:, k, m * P:(m + 1) * P], ctxT[:, k, c0:c0 + BANK],
                                     start=(k == 0), stop=(k == KD - 1))
                last.then_inc(proj_done, 1)
            pe.wait_ge(wv_in, 16)
            for t in range(NV):
                j = NF + t
                bank_free(j)
                for k in range(KD):
                    last = pe.matmul(PS[:, 4 + j % 4, 0:D], ctxT[:, k, t * P:(t + 1) * P], wv[:, k, :],
                                     start=(k == 0), stop=(k == KD - 1))
                last.then_inc(proj_done, 1)
            pe.wait_ge(proj_taken, NV)
            at.tensor(pe)
            po_t(pe)


def shared_kv_stage(nc, ctx, sh, A):
    H, DK = 8, 128
    UN = B * H
    G = UN * TB
    LAG = 2
    PS, X, XN, XT = sh.PS, sh.X, sh.XN, sh.XT
    stage = ExitStack()

    def sb(name, shape, dt=F32):
        return stage.enter_context(nc.sbuf_tensor("s_" + name, shape, dt))

    def sem(name):
        return ctx.enter_context(nc.semaphore("s_" + name))

    nm = Norm(nc, ctx, stage, sh, "s_n")
    wq, wo = sb("wq", [P, H, KD, DK]), sb("wo", [P, H, D])
    wk, wv = sb("wk", [P, KD, DK]), sb("wv", [P, KD, DK])
    KTr, V = sb("KT", [P, T]), sb("V", [P, NT, DK])
    QT = [sb(f"QT{n}", [P, S]) for n in range(2)]
    NPB = 4
    Pr = [sb(f"Pr{n}", [P, S]) for n in range(NPB)]
    Pn = [sb(f"Pn{n}", [P, S]) for n in range(NPB)]
    mx, nmx, sm, rs = (sb(n, [P, NPB]) for n in ("mx", "nmx", "sm", "rs"))
    PT = [sb(f"PT{n}", [P, TB, S]) for n in range(2)]
    OT = [sb(f"OT{n}", [P, S]) for n in range(2)]

    wkv_in, wq_in, wo_in = sem("wkv_in"), sem("wq_in"), sem("wo_in")
    kv_mm, k_ready, v_ready = sem("kv_mm"), sem("k_ready"), sem("v_ready")
    q_mm, q_ready = sem("q_mm"), sem("q_ready")
    s_mm, mx_ready, nmx_ready, p_ready, rs_ready, pn_ready, t_mm, pt_ready = (
        sem(n) for n in ("s_mm", "mx_ready", "nmx_ready", "p_ready", "rs_ready", "pn_ready", "t_mm", "pt_ready"))
    o_mm, o_ready, y_mm, y_taken = sem("o_mm"), sem("o_ready"), sem("y_mm"), sem("y_taken")

    with stage, nc.Block() as block:

        @block.sync
        def _(sp):
            sp.dma_start(wk[:, :, :], A["s_wk"]).then_inc(wkv_in, 16)
            sp.dma_start(wv[:, :, :], A["s_wv"]).then_inc(wkv_in, 16)
            sp.dma_start(wq[:, :, :, :], A["s_wq"]).then_inc(wq_in, 16)
            sp.dma_start(wo[:, :, :], A["s_wo"]).then_inc(wo_in, 16)
            for e in range(ExpertWeights.EXP):
                sh.weights[1].load_expert(sp, e)

        @block.gpsimd
        def _(pool):
            nm.gpsimd(pool)
            for g in range(G):
                pool.wait_ge(rs_ready, g + 1)
                if g >= NPB:
                    pool.wait_ge(t_mm, g - NPB + 1)
                pool.tensor_scalar(Pn[g % NPB][:, :], Pr[g % NPB][:, :], rs[:, g % NPB:g % NPB + 1], None,
                                   ALU.mult).then_inc(pn_ready, 1)

        @block.vector
        def _(dve):
            nm.vector(dve)
            for b in range(B):
                for i in range(0, TB, 2):
                    n = B + (b * TB + i) // 2
                    dve.wait_ge(kv_mm, n + 1)
                    dve.tensor_copy(V[:, b * TB + i:b * TB + i + 2, :],
                                    PS[:, 4 + n % 4, 0:2 * DK].rearrange("p (i c) -> p i c", i=2)).then_inc(v_ready, 1)

            def maximum(g):
                dve.wait_ge(s_mm, g + 1)
                if g >= NPB:
                    dve.wait_ge(p_ready, g - NPB + 1)
                dve.tensor_reduce(mx[:, g % NPB:g % NPB + 1], PS[:, g % 2, :], AX.X, ALU.max).then_inc(mx_ready, 1)
                dve.wait_ge(mx_ready, g + 1)
                dve.tensor_scalar(nmx[:, g % NPB:g % NPB + 1], mx[:, g % NPB:g % NPB + 1], -1.0, None,
                                  ALU.mult).then_inc(nmx_ready, 1)

            def inverse_sum(g):
                dve.wait_ge(p_ready, g + 1)
                if g >= NPB:
                    dve.wait_ge(pn_ready, g - NPB + 1)
                dve.reciprocal(rs[:, g % NPB:g % NPB + 1], sm[:, g % NPB:g % NPB + 1]).then_inc(rs_ready, 1)

            def take_transposes(g):
                n, qt = divmod(g, TB)
                dve.wait_ge(t_mm, g + 1)
                if n >= 2:
                    dve.wait_ge(o_mm, n - 1)
                dve.tensor_copy(PT[n % 2][:, :, qt * P:(qt + 1) * P],
                                PS[:, 2 + g % 2, :].rearrange("p (m q) -> p m q", m=TB)).then_inc(pt_ready, 1)

            def take_output(b):
                for bank in range(2):
                    dve.wait_ge(y_mm, (b + 1) * H)
                    i = b * TB + 2 * bank
                    dve.tensor_tensor(X[:, i:i + 2, :], X[:, i:i + 2, :],
                                      PS[:, 6 + bank, :].rearrange("p (i d) -> p i d", i=2),
                                      ALU.add).then_inc(y_taken, 1)

            for g in range(G + LAG + 1):
                if g < G:
                    maximum(g)
                if 1 <= g <= G:
                    inverse_sum(g - 1)
                if g > LAG:
                    take_transposes(g - LAG - 1)
                if g == TB * H + TB + 1:
                    take_output(0)
            take_output(1)

        @block.scalar
        def _(act):
            nm.scalar(act)
            for b in range(B):
                act.wait_ge(kv_mm, b + 1)
                act.activation(KTr[:, b * S:(b + 1) * S], PS[:, 4 + b, :], ACT.Copy).then_inc(k_ready, 1)

            def take_q(n):
                act.wait_ge(q_mm, n + 1)
                if n >= 2:
                    act.wait_ge(s_mm, (n - 1) * TB)
                act.activation(QT[n % 2][:, :], PS[:, 4, :], ACT.Copy).then_inc(q_ready, 1)

            def take_o(n):
                act.wait_ge(o_mm, n + 1)
                if n >= 2:
                    act.wait_ge(y_mm, n - 1)
                act.activation(OT[n % 2][:, :], PS[:, 5, :], ACT.Copy).then_inc(o_ready, 1)

            take_q(0)
            for g in range(G):
                n, qt = divmod(g, TB)
                act.wait_ge(nmx_ready, g + 1)
                if g >= NPB:
                    act.wait_ge(pn_ready, g - NPB + 1)
                act.activation(Pr[g % NPB][:, :], PS[:, g % 2, :], ACT.Exp, bias=nmx[:, g % NPB:g % NPB + 1],
                               accum_out=sm[:, g % NPB:g % NPB + 1]).then_inc(p_ready, 1)
                if qt == 1 and n + 1 < UN:
                    take_q(n + 1)
                if qt == 2 and n >= 1:
                    take_o(n - 1)
            take_o(UN - 1)

        @block.tensor
        def _(pe):
            nm.tensor(pe)
            pe.wait_ge(nm.xT_ready, KD * B)
            pe.wait_ge(wkv_in, 32)
            for b in range(B):
                for k in range(KD):
                    last = pe.matmul(PS[:, 4 + b, :], wk[:, k, :], XT[:, k, b * S:(b + 1) * S],
                                     start=(k == 0), stop=(k == KD - 1))
                last.then_inc(kv_mm, 1)
            for i in range(0, NT, 2):
                n = B + i // 2
                if n >= 4:
                    pe.wait_ge(k_ready, n - 3)
                for j in range(2):
                    for k in range(KD):
                        last = pe.matmul(PS[:, 4 + n % 4, j * DK:(j + 1) * DK], XT[:, k, (i + j) * P:(i + j + 1) * P],
                                         wv[:, k, :], start=(k == 0), stop=(k == KD - 1))
                last.then_inc(kv_mm, 1)
            pe.wait_ge(k_ready, B)
            pe.wait_ge(v_ready, NT // 2)
            pe.wait_ge(wq_in, 16)
            pe.wait_ge(wo_in, 16)

            def queries(n):
                b, h = divmod(n, H)
                if n >= 1:
                    pe.wait_ge(q_ready, n)
                for k in range(KD):
                    last = pe.matmul(PS[:, 4, :], wq[:, h, k, :], XT[:, k, b * S:(b + 1) * S],
                                     start=(k == 0), stop=(k == KD - 1))
                last.then_inc(q_mm, 1)

            def scores(g):
                n, qt = divmod(g, TB)
                b = n // H
                pe.wait_ge(q_ready, n + 1)
                if g >= 2:
                    pe.wait_ge(p_ready, g - 1)
                pe.matmul(PS[:, g % 2, :], QT[n % 2][:, qt * P:(qt + 1) * P], KTr[:, b * S:(b + 1) * S],
                          start=True, stop=True).then_inc(s_mm, 1)

            def transposes(g):
                pe.wait_ge(pn_ready, g + 1)
                if g >= 2:
                    pe.wait_ge(pt_ready, g - 1)
                for m in range(TB):
                    last = pe.transpose(PS[:, 2 + g % 2, m * P:(m + 1) * P], Pn[g % NPB][:, m * P:(m + 1) * P],
                                        sh.ident[:, :])
                last.then_inc(t_mm, 1)

            def outputs(n):
                b = n // H
                pe.wait_ge(pt_ready, (n + 1) * TB)
                if n >= 1:
                    pe.wait_ge(o_ready, n)
                for m in range(TB):
                    last = pe.matmul(PS[:, 5, :], V[:, b * TB + m, :], PT[n % 2][:, m, :], start=(m == 0),
                                     stop=(m == TB - 1))
                last.then_inc(o_mm, 1)

            def project(n):
                b, h = divmod(n, H)
                pe.wait_ge(o_ready, n + 1)
                if h == 0 and b > 0:
                    pe.wait_ge(y_taken, 2 * b)
                for i in range(TB):
                    last = pe.matmul(PS[:, 6 + i // 2, (i % 2) * D:(i % 2 + 1) * D], OT[n % 2][:, i * P:(i + 1) * P],
                                     wo[:, h, :], start=(h == 0 and i % 2 == 0), stop=(h == H - 1 and i % 2 == 1),
                                     skip_group_check=True)
                last.then_inc(y_mm, 1)

            queries(0)
            for g in range(G + LAG):
                n, qt = divmod(g, TB)
                if g < G:
                    scores(g)
                if qt == 0 and n + 1 < UN:
                    queries(n + 1)
                if g >= LAG:
                    transposes(g - LAG)
                if qt == 2 and 1 <= n < UN:
                    outputs(n - 1)
                if qt == 0 and n >= 2:
                    project(n - 2)
            outputs(UN - 1)
            project(UN - 1)


def hard_cross_stage(nc, ctx, sh, A):
    NK = 1024
    NKT = B * NK // P
    PS, X, XN, XT = sh.PS, sh.X, sh.XN, sh.XT
    stage = ExitStack()

    def sb(name, shape, dt=F32):
        return stage.enter_context(nc.sbuf_tensor("h_" + name, shape, dt))

    def sem(name):
        return ctx.enter_context(nc.semaphore("h_" + name))

    nm = Norm(nc, ctx, stage, sh, "h_n")
    wc = sb("wc", [P, KD, D])
    VB = sb("VB", [P, UNITS, TB, 1, VW])
    at = Attention(nc, ctx, stage, PS, "h_a", S, 1, sh.ident, sh.identb)
    ctxT = sb("ctxT", [P, KD, B * NK])
    wq, wkv = sb("wq", [P, KD, D]), sb("wkv", [P, KD, 2 * HD])
    MK = sb("MK", [P, NKT, 2 * HD])
    QF = sb("QF", [P, KD, T])
    QP = [sb(f"QP{n}", [P, KD, T], BF16) for n in range(3)]
    KP = [sb(f"KP{n}", [HD, B, S], BF16) for n in range(3)]
    ktail = sb("ktail", [TAIL_ROWS, S], BF16)
    ktc = sb("ktc", [TAIL_ROWS, 1])
    top = sb("top", [P, NT, 8])
    idx = sb("idx", [P, NT, 8], U32)
    row = sb("row", [P, NT], U32)
    GM = sb("GM", [P, NT, 2 * HD])
    mkv_rows = nc.dram_tensor("h_mkv", [B * NK, 2 * HD], F32, kind="Internal").ap()
    q_stack = nc.dram_tensor("h_q_stack", [UNITS, Q_DRAM, GH, S], BF16, kind="Internal").ap()
    k_stack = nc.dram_tensor("h_k_stack", [UNITS, K_DRAM, 1, S], BF16, kind="Internal").ap()

    small_in, ctx_in, w_in, wc_in = sem("small_in"), sem("ctx_in"), sem("w_in"), sem("wc_in")
    mk_mm, mk_ready, mk_stored, qf_mm, qf_ready = (sem(n) for n in ("mk_mm", "mk_ready", "mk_stored", "qf_mm", "qf_ready"))
    sc_mm, top_ready, idx_ready, row_ready = (sem(n) for n in ("sc_mm", "top_ready", "idx_ready", "row_ready"))
    kT_mm, v_ones, v_ready, qtail_set = (sem(n) for n in ("kT_mm", "v_ones", "v_ready", "qtail_set"))
    tail_zero, tail_ready, tail_stored = (sem(n) for n in ("tail_zero", "tail_ready", "tail_stored"))
    k_stored = [sem(f"k_stored{b}") for b in range(B)]
    q_stored = [sem(f"q_stored{b}") for b in range(B)]
    found = [sem(f"found{b}") for b in range(B)]
    NQC = B * KD

    def dst(n, part):
        if n < NQC:
            b, m = divmod(n, KD)
            return QP[part][:, m, b * S:(b + 1) * S]
        return KP[part][:, n - NQC, :]

    LATER = 2
    spl = Splitter(nc, ctx, at.E[1][:, :, :], "h_s", dst, [P] * NQC + [HD] * B, NQC + B)
    po_t, po_s, po_v = project_out(nc, at, sh, sem, wc, wc_in, 16)

    with stage, nc.Block() as block:

        @block.sync
        def _(sp):
            sp.dma_start(ktc[:, :], A["h_ktc"]).then_inc(small_in, 16)
            sp.dma_start(wkv[:, :, :], A["h_wkv"]).then_inc(w_in, 16)
            sp.dma_start(wq[:, :, :], A["h_wq"]).then_inc(w_in, 16)
            sp.dma_start(ctxT[:, :, :], A["h_ctxT"]).then_inc(ctx_in, 16)
            sp.dma_start(wc[:, :, :], A["h_wc"]).then_inc(wc_in, 16)
            sp.wait_ge(mk_ready, 1)
            sp.dma_start(mkv_rows.rearrange("(t p) c -> p t c", p=P), MK[:, :, :]).then_inc(mk_stored, 16)
            sp.wait_ge(qtail_set, 2)
            store_query_tails(sp, q_stack, at.qtail, tail_stored)

            def spread(rows, src):
                return rows[:, :, 0, :].rearrange("u r n -> r u n"), src.unsqueeze(1).to_broadcast([src.shape[0], rows.shape[0], S])

            sp.wait_ge(tail_ready, 1)
            d, src = spread(k_stack[:, K_DRAM - TAIL_ROWS:, :, :], ktail[:, :])
            sp.dma_start(d, src).then_inc(tail_stored, 16)
            for b in range(B):
                sp.wait_ge(spl.p2_ready, (b + 1) * KD)
                store_parts(sp, q_stack, Q_ROWS, lambda part: QP[part][:, :, b * S:(b + 1) * S], b, q_stored[b])

            def store_k(b):
                sp.wait_ge(spl.p2_ready, NQC + b + 1)
                for slot, part in enumerate(K_ROWS):
                    d, src = spread(k_stack[b * NG:(b + 1) * NG, slot * HD:(slot + 1) * HD, :, :], KP[part][:, b, :])
                    sp.dma_start(d, src).then_inc(k_stored[b], 16)

            def rest():
                store_k(1)
                sp.wait_ge(k_stored[1], 16 * len(K_ROWS))
                sp.wait_ge(q_stored[1], 16 * Q_STORES)
                sp.wait_ge(v_ready, B)

            store_k(0)
            sp.wait_ge(tail_stored, 16 * 2)
            sp.wait_ge(k_stored[0], 16 * len(K_ROWS))
            sp.wait_ge(q_stored[0], 16 * Q_STORES)
            sp.wait_ge(v_ready, 1)
            at.sync(sp, load_unit(sp, at, q_stack, k_stack, VB), rest)

        @block.gpsimd
        def _(pool):
            nm.gpsimd(pool)
            pool.memset(VB[:, :, :, :, :], 1.0).then_inc(v_ones, 1)
            pool.memset(at.qtail[:, :], 0.0).then_inc(qtail_set, 1)
            pool.wait_ge(qtail_set, 1)
            pool.wait_ge(v_ones, 1)
            pool.tensor_scalar(at.qtail[:, :], at.qtail[:, :], sh.query_tail[:, 0:1], None,
                               ALU.add).then_inc(qtail_set, 1)
            pool.memset(ktail[:, :], 0.0).then_inc(tail_zero, 1)
            pool.wait_ge(small_in, 16)
            pool.wait_ge(tail_zero, 1)
            pool.wait_ge(qtail_set, 2)
            pool.tensor_scalar(ktail[:, :], ktail[:, :], ktc[:, 0:1], None, ALU.add).then_inc(tail_ready, 1)
            pool.wait_ge(tail_ready, 1)
            spl.gpsimd(pool, 0, NQC)
            pool.wait_ge(mk_stored, 16)

            def find(b):
                for i in range(b * TB, (b + 1) * TB):
                    pool.wait_ge(row_ready, i + 1)
                    pool.indirect_dma_start(out=GM[:, i, :], out_offset=None, in_=mkv_rows,
                                            in_offset=bass.IndirectOffsetOnAxis(ap=row[:, i:i + 1], axis=0),
                                            ).then_inc(found[b], 16)

            find(0)
            spl.gpsimd(pool, NQC, NQC + 1)
            find(1)
            spl.gpsimd(pool, NQC + 1, NQC + 2)

        @block.vector
        def _(dve):
            nm.vector(dve)
            dve.wait_ge(mk_mm, 1)
            dve.tensor_copy(MK[:, :, :], PS[:, 4, :].rearrange("p (t c) -> p t c", t=NKT)).then_inc(mk_ready, 1)
            for n in range(NQC):
                dve.wait_ge(qf_mm, n + 1)
                dve.tensor_copy(spl.buffer(dve, n), PS[:, 4 + n, :]).then_inc(spl.f_ready, 1)

            def best(i):
                b = i // TB
                bank = 2 * (i % 2)
                dve.wait_ge(sc_mm, i + 1)
                dve.max(top[:, i, :], PS[:, bank:bank + 2, :]).then_inc(top_ready, 1)
                dve.wait_ge(top_ready, i + 1)
                dve.max_index(idx[:, i, :], top[:, i, :],
                              PS[:, bank:bank + 2, :].rearrange("p h n -> p (h n)")).then_inc(idx_ready, 1)
                dve.wait_ge(idx_ready, i + 1)
                dve.tensor_scalar(row[:, i:i + 1], idx[:, i, 0:1], float(b * NK), None, ALU.add).then_inc(row_ready, 1)

            def take_found(b):
                dve.wait_ge(kT_mm, b + 1)
                dve.tensor_copy(spl.buffer(dve, NQC + b), PS[0:HD, 7, :]).then_inc(spl.f_ready, 1)
                for g in range(NG):
                    last = dve.tensor_copy(VB[:, b * NG + g, :, 0, 0:HD], GM[:, b * TB:(b + 1) * TB, HD:2 * HD])
                last.then_inc(v_ready, 1)

            for i in range(TB + LATER):
                best(i)
            dve.wait_ge(v_ones, 1)
            take_found(0)
            for i in range(TB + LATER, NT):
                best(i)
            at.vector(dve, between=lambda: take_found(1))
            po_v(dve)

        @block.scalar
        def _(act):
            nm.scalar(act)
            for n in range(NQC):
                b, m = divmod(n, KD)
                act.wait_ge(spl.f_ready, n + 1)
                act.activation(QF[:, m, b * S:(b + 1) * S], spl.F[n % 2], ACT.Copy).then_inc(qf_ready, 1)
                spl.scalar(act, n, n + 1)
            spl.scalar(act, NQC, NQC + 1)
            spl.scalar(act, NQC + 1, NQC + 2)
            act.wait_ge(spl.p2_ready, NQC + B)
            at.scalar(act)
            po_s(act)

        @block.tensor
        def _(pe):
            pe.wait_ge(w_in, 32)
            pe.wait_ge(ctx_in, 16)
            for t in range(NKT):
                for k in range(KD):
                    last = pe.matmul(PS[:, 4, t * 2 * HD:(t + 1) * 2 * HD], ctxT[:, k, t * P:(t + 1) * P],
                                     wkv[:, k, :], start=(k == 0), stop=(k == KD - 1), skip_group_check=True)
            last.then_inc(mk_mm, 1)
            nm.tensor(pe)
            pe.wait_ge(nm.xT_ready, KD * B)
            pe.wait_ge(mk_ready, 1)
            for n in range(NQC):
                b, m = divmod(n, KD)
                for k in range(KD):
                    last = pe.matmul(PS[:, 4 + n, :], wq[:, k, m * P:(m + 1) * P], XT[:, k, b * S:(b + 1) * S],
                                     start=(k == 0), stop=(k == KD - 1))
                last.then_inc(qf_mm, 1)

            def context_scores(i):
                b = i // TB
                pe.wait_ge(qf_ready, KD * (b + 1))
                if i >= 2:
                    pe.wait_ge(idx_ready, i - 1)
                for half in range(2):
                    for k in range(KD):
                        c0 = b * NK + half * BANK
                        last = pe.matmul(PS[:, 2 * (i % 2) + half, :], QF[:, k, i * P:(i + 1) * P],
                                         ctxT[:, k, c0:c0 + BANK], start=(k == 0), stop=(k == KD - 1))
                last.then_inc(sc_mm, 1)

            def found_keys(b):
                pe.wait_ge(found[b], 16 * TB)
                pe.wait_ge(spl.f_ready, NQC + b)
                for i in range(TB):
                    last = pe.transpose(PS[0:HD, 7, i * P:(i + 1) * P], GM[:, b * TB + i, 0:HD], sh.ident[:, :])
                last.then_inc(kT_mm, 1)

            for i in range(TB + LATER):
                context_scores(i)
            found_keys(0)
            for i in range(TB + LATER, NT):
                context_scores(i)
            pe.wait_ge(idx_ready, NT)

            def between():
                found_keys(1)
                pe.wait_ge(spl.f_ready, NQC + B)

            at.tensor(pe, between=between)
            po_t(pe)


def experts_stage(nc, ctx, sh, A, layer):
    first = layer == 0
    weights = sh.weights[layer]
    EXP, F, KF, pre = weights.EXP, weights.F, weights.KF, weights.pre
    NB1 = F // BANK
    PS, X, XN, XT = sh.PS, sh.X, sh.XN, sh.XT
    stage = ExitStack()

    def sb(name, shape, dt=F32):
        return stage.enter_context(nc.sbuf_tensor(pre + name, shape, dt))

    def sem(name):
        return ctx.enter_context(nc.semaphore(pre + name))

    nm = Norm(nc, ctx, stage, sh, pre + "n")
    wr, br = sb("wr", [P, KD, EXP]), sb("br", [P, EXP])
    W1 = weights.W1
    W2 = weights.W2 if first else sb("W2", [P, KF, D])
    B1 = sb("B1", [P, EXP * F])
    B2 = sb("B2", [P, (EXP if first else 1) * D])
    tri, ones = sb("tri", [P, P]), sb("ones", [P, P])
    iota = sb("iota", [P, 16])
    iotaP = sb("iotaP", [P, EXP])
    lg, ex = sb("lg", [P, NT, EXP]), sb("ex", [P, NT, EXP])
    mx, prob, den = sb("mx", [P, NT]), sb("prob", [P, NT]), sb("den", [P, NT])
    top, idx = sb("top", [P, NT, 8]), sb("idx", [P, NT, 8], U32)
    idxf = sb("idxf", [P, NT])
    OH = sb("OH", [P, NT, EXP])
    before = sb("before", [P, NT + 1, EXP])
    cmp_ = sb("cmp", [P, EXP, EXP])
    tiles, upto, base = sb("tiles", [P, EXP]), sb("upto", [P, EXP]), sb("base", [P, EXP])
    pos = sb("pos", [P, NT, EXP])
    slotf, slot = sb("slotf", [P, NT]), sb("slot", [P, NT], U32)
    cmps = sb("cmps", [P, 16, EXP])
    exf, ext = sb("exf", [P, 16]), sb("ext", [P, 16], I32)
    gb = None if first else sb("gb", [P, 2, D])
    Xs = [sb(f"Xs{n}", [P, D]) for n in range(2)]
    XsT = [sb(f"XsT{n}", [P, KD, P]) for n in range(2)]
    Hs = [sb(f"H{n}", [P, F]) for n in range(2)]
    HT = [sb(f"HT{n}", [P, KF, P]) for n in range(2)]
    Ys = [sb(f"Y{n}", [P, D]) for n in range(2)]
    YG = sb("YG", [P, NT, D])
    xs = sh.xs[layer]
    ys = nc.dram_tensor(pre + "ys", [SLOTS, D], F32, kind="Internal").ap()

    small_in, b_in, w2_in, ones_set = (sem(n) for n in ("small_in", "b_in", "w2_in", "ones_set"))
    own, lg_mm, lg_ready, ex_ready, oh_ready, rank_mm, slot_ready, ext_ready = (
        sem(n) for n in ("own", "lg_mm", "lg_ready", "ex_ready", "oh_ready", "rank_mm", "slot_ready", "ext_ready"))
    scattered = sem("scattered")
    xs_in = [sem(f"xs_in{n}") for n in range(2)]
    xsT_mm, xsT_ready, w1_mm, h_sum, h_ready, hT_mm, hT_ready, w2_mm, y_ready = (
        sem(n) for n in ("xsT_mm", "xsT_ready", "w1_mm", "h_sum", "h_ready", "hT_mm", "hT_ready", "w2_mm",
                         "y_ready"))
    gathered = [sem(f"gathered{b}") for b in range(B)]
    stored = [sem(f"stored{n}") for n in range(2)]
    xb_ready, var2_ready, rstd2_ready, eps2_ready, out_ready = (
        sem(n) for n in ("xb_ready", "var2_ready", "rstd2_ready", "eps2_ready", "out_ready"))
    NSMALL = 5

    def tiles_loop(eng, step):
        for t in range(2):
            step(t, t)
        with eng.Fori(0, (SLOT_TILES - 5) // 2) as i:
            step(i * 2 + 2, 0)
            step(i * 2 + 3, 1)
        for t in range(SLOT_TILES - 3, SLOT_TILES):
            step(t, t % 2)

    def known_below(t, n):
        return isinstance(t, int) and t < n

    def rows(t):
        return bass.ds(t * P, P)

    with stage, nc.Block() as block:

        @block.sync
        def _(sp):
            small = [(wr, "wr"), (tri, "tris"), (iota, "iota"), (iotaP, "iotaP")]
            small += [(br, pre + "br")] if first else []
            for d, s in small:
                sp.dma_start(d[tuple(slice(None) for _ in d.shape)], A[pre + "wr" if s == "wr" else s]).then_inc(small_in, 16)
            sp.dma_start(B1[:, :], A[pre + "b1"].to_broadcast([P, EXP * F])).then_inc(b_in, 16)
            sp.dma_start(B2[:, :], A[pre + "b2"]).then_inc(b_in, 16)
            if not first:
                sp.dma_start(W2[:, :, :], A["g_w2"]).then_inc(w2_in, 16)
            sp.wait_ge(scattered, 16 * NT)

            def load(t, p):
                if not known_below(t, 2):
                    sp.wait_ge(xsT_mm, t - 1)
                sp.dma_start(Xs[p][:, :], xs[rows(t), :]).then_inc(xs_in[p], 16)

            def step(t, p):
                if not (isinstance(t, int) and t + 2 >= SLOT_TILES):
                    load(t + 2, p)
                sp.wait_ge(y_ready, t + 1)
                sp.dma_start(ys[rows(t), :], Ys[p][:, :]).then_inc(stored[p], 16)

            load(0, 0)
            load(1, 1)
            tiles_loop(sp, step)
            for p in range(2):
                sp.wait_ge(stored[p], 16 * ((SLOT_TILES + 1 - p) // 2))
            if not first:
                for b in range(B):
                    tiles = slice(b * TB, (b + 1) * TB)
                    sp.wait_ge(out_ready, b + 1)
                    sp.dma_start(sh.out[:, tiles, :], X[:, tiles, :]).then_inc(sh.out_stored, 16)
                sp.wait_ge(sh.out_stored, 16 * B)

        @block.gpsimd
        def _(pool):
            pool.memset(ones[:, :], 1.0).then_inc(ones_set, 1)
            nm.gpsimd(pool)
            pool.wait_ge(nm.xn_ready, B)
            pool.wait_ge(sh.zeroed, 16 * len(sh.xs))
            pool.wait_ge(slot_ready, 1)
            for i in range(NT):
                pool.indirect_dma_start(out=xs, out_offset=bass.IndirectOffsetOnAxis(ap=slot[:, i:i + 1], axis=0),
                                        in_=XN[:, i, :], in_offset=None).then_inc(scattered, 16)
            if not first:
                pool.wait_ge(scattered, 16 * NT)
                pool.wait_ge(nm.xT_done, KD * B)
                pool.wait_ge(b_in, 32)
                for i in range(NT):
                    last = pool.tensor_tensor(XN[:, i, :], XN[:, i, :], B2[:, :], ALU.add)
                last.then_inc(xb_ready, 1)
                pool.wait_ge(small_in, 16 * NSMALL)
                pool.wait_ge(nm.xn_ready, B)
                for i in range(NT):
                    last = pool.tensor_tensor(X[:, i, :], X[:, i, :], gb[:, 1, :], ALU.add)
                last.then_inc(xb_ready, 1)
            for p in range(2):
                pool.wait_ge(stored[p], 16 * ((SLOT_TILES + 1 - p) // 2))
            for i in range(NT):
                pool.indirect_dma_start(out=YG[:, i, :], out_offset=None, in_=ys,
                                        in_offset=bass.IndirectOffsetOnAxis(ap=slot[:, i:i + 1], axis=0),
                                        ).then_inc(gathered[i // TB], 16)
            if not first:
                inverse_deviations_gpsimd(pool, sh.mhalf, nm.mv, nm.rstd, 1e-12, var2_ready, eps2_ready, rstd2_ready)

        @block.vector
        def _(dve):
            nm.vector(dve)
            c = Chain(dve, own)
            dve.wait_ge(small_in, 16 * NSMALL)
            dve.wait_ge(lg_mm, 1)
            src = PS[:, 4, 0:NT * EXP].rearrange("p (i e) -> p i e", i=NT)
            if first:
                c.link(dve.tensor_tensor(lg[:, :, :], src, br[:, :].unsqueeze(1).to_broadcast([P, NT, EXP]), ALU.add))
            else:
                c.link(dve.tensor_copy(lg[:, :, :], src))
            for i in range(NT):
                last = dve.max(top[:, i, :], lg[:, i, :])
            c.link(last)
            for i in range(NT):
                last = dve.max_index(idx[:, i, :], top[:, i, :], lg[:, i, :])
            c.link(last)
            c.link(dve.tensor_copy(idxf[:, :], idx[:, :, 0]))
            dve.tensor_tensor(OH[:, :, :], iota[:, 0:EXP].unsqueeze(1).to_broadcast([P, NT, EXP]),
                              idxf[:, :].unsqueeze(2).to_broadcast([P, NT, EXP]), ALU.is_equal).then_inc(oh_ready, 1)
            if first:
                dve.tensor_tensor(lg[:, :, :], lg[:, :, :], top[:, :, 0:1].to_broadcast([P, NT, EXP]),
                                  ALU.subtract).then_inc(lg_ready, 1)
            c.link(dve.memset(before[:, 0, :], 0.0))
            dve.wait_ge(rank_mm, 1)
            NE = NT * EXP
            for i in range(NT):
                c.link(dve.tensor_tensor(before[:, i + 1, :], before[:, i, :],
                                         PS[:, 5, NE + i * EXP:NE + (i + 1) * EXP], ALU.add))
            c.link(dve.tensor_tensor(cmp_[:, :, :], before[:, NT, :].unsqueeze(2).to_broadcast([P, EXP, EXP]),
                                     iotaP[:, :].unsqueeze(1).to_broadcast([P, EXP, EXP]), ALU.is_gt))
            c.link(dve.tensor_reduce(tiles[:, :], cmp_[:, :, :], AX.X, ALU.add))
            dve.wait_ge(ones_set, 1)
            c.link(dve.tensor_tensor_scan(upto[:, :], ones[:, 0:EXP], tiles[:, :], 0.0, ALU.mult, ALU.add))
            c.link(dve.tensor_tensor(base[:, :], upto[:, :], tiles[:, :], ALU.subtract))
            c.link(dve.tensor_tensor(pos[:, :, :], before[:, 0:NT, :],
                                     PS[:, 5, 0:NE].rearrange("p (i e) -> p i e", i=NT), ALU.add))
            c.link(dve.scalar_tensor_tensor(out=pos[:, :, :], in0=base[:, :].unsqueeze(1).to_broadcast([P, NT, EXP]),
                                            scalar=float(P), in1=pos[:, :, :], op0=ALU.mult, op1=ALU.add))
            c.link(dve.tensor_tensor(pos[:, :, :], pos[:, :, :], OH[:, :, :], ALU.mult))
            c.link(dve.tensor_reduce(slotf[:, :], pos[:, :, :], AX.X, ALU.add))
            dve.tensor_copy(slot[:, :], slotf[:, :]).then_inc(slot_ready, 1)
            c.link(dve.tensor_tensor(cmps[:, :, :], upto[:, :].unsqueeze(1).to_broadcast([P, 16, EXP]),
                                     iota[:, :].unsqueeze(2).to_broadcast([P, 16, EXP]), ALU.is_le))
            c.link(dve.tensor_reduce(exf[:, :], cmps[:, :, :], AX.X, ALU.add))
            c.link(dve.tensor_scalar(exf[:, :], exf[:, :], EXP - 1.0, None, ALU.min))
            dve.tensor_copy(ext[:, :], exf[:, :]).then_inc(ext_ready, 1)
            if first:
                dve.wait_ge(ex_ready, 1)
                c.link(dve.tensor_reduce(den[:, :], ex[:, :, :], AX.X, ALU.add))
                c.link(dve.reciprocal(prob[:, :], den[:, :]))

            dve.wait_ge(ext_ready, 1)
            dve.wait_ge(b_in, 32)

            def hidden(t, p):
                e = dve.value_load(ext[0:1, bass.ds(t, 1)], min_val=0, max_val=EXP - 1)
                dve.wait_ge(w1_mm, t + 1)
                if not known_below(t, 2):
                    dve.wait_ge(hT_mm, t - 1)
                b0 = 1 + p * NB1
                dve.tensor_tensor(Hs[p][:, :], PS[:, b0:b0 + NB1, :].rearrange("p h n -> p (h n)"),
                                  B1[:, bass.ds(e * F, F)], ALU.add).then_inc(h_sum, 1)

            def result(t, p):
                if first:
                    e = dve.value_load(ext[0:1, bass.ds(t, 1)], min_val=0, max_val=EXP - 1)
                dve.wait_ge(w2_mm, t + 1)
                if not known_below(t, 2):
                    dve.wait_ge(stored[p], (t - p) * 8)
                if first:
                    last = dve.tensor_tensor(Ys[p][:, :], PS[:, 7, 0:D], B2[:, bass.ds(e * D, D)], ALU.add)
                else:
                    last = dve.tensor_copy(Ys[p][:, :], PS[:, 7, 0:D])
                last.then_inc(y_ready, 1)

            def step(t, p):
                if not (isinstance(t, int) and t + 1 >= SLOT_TILES):
                    hidden(t + 1, 1 - p)
                result(t, p)

            hidden(0, 0)
            tiles_loop(dve, step)
            if first:
                for i in range(NT):
                    dve.wait_ge(gathered[i // TB], 16 * TB)
                    dve.scalar_tensor_tensor(out=X[:, i, :], in0=YG[:, i, :], scalar=prob[:, i:i + 1],
                                             in1=X[:, i, :], op0=ALU.mult, op1=ALU.add).then_inc(xb_ready, 1)
            else:
                dve.wait_ge(xb_ready, 2)
                for b in range(B):
                    batch = range(b * TB, (b + 1) * TB)
                    dve.wait_ge(gathered[b], 16 * TB)
                    for i in batch:
                        last = dve.tensor_tensor(XN[:, i, :], XN[:, i, :], YG[:, i, :], ALU.add)
                    c.link(last)
                    for i in batch:
                        last = dve.bn_stats(nm.st6[:, i, :], XN[:, i, :])
                    c.link(last)
                    for i in batch:
                        last = dve.bn_aggr(nm.mv[:, i, :], nm.st6[:, i, :])
                    last.then_inc(var2_ready, 1)
                dve.wait_ge(var2_ready, B)
                for b in range(B):
                    batch = range(b * TB, (b + 1) * TB)
                    for i in batch:
                        last = dve.scalar_tensor_tensor(out=YG[:, i, :], in0=XN[:, i, :], scalar=nm.mv[:, i, 0:1],
                                                        in1=gb[:, 0, :], op0=ALU.subtract, op1=ALU.mult)
                    c.link(last)
                    dve.wait_ge(rstd2_ready, b + 1)
                    for i in batch:
                        last = dve.scalar_tensor_tensor(out=X[:, i, :], in0=YG[:, i, :], scalar=nm.rstd[:, i:i + 1],
                                                        in1=X[:, i, :], op0=ALU.mult, op1=ALU.add)
                    last.then_inc(out_ready, 1)

        @block.scalar
        def _(act):
            if not first:
                act.dma_start(gb[:, :, :], A["g_gb"]).then_inc(small_in, 16)
            nm.scalar(act)
            if first:
                act.wait_ge(lg_ready, 1)
                act.activation(ex[:, :, :], lg[:, :, :], ACT.Exp).then_inc(ex_ready, 1)

            def take_x(t, p):
                act.wait_ge(xsT_mm, t + 1)
                if not known_below(t, 2):
                    act.wait_ge(w1_mm, t - 1)
                act.activation(XsT[p][:, :, :], PS[:, 0, 0:D].rearrange("p (k n) -> p k n", k=KD),
                               ACT.Copy).then_inc(xsT_ready, 1)

            def gelu(t, p):
                act.wait_ge(h_sum, t + 1)
                act.activation(Hs[p][:, :], Hs[p][:, :], ACT.Gelu).then_inc(h_ready, 1)

            def take_h(t, p):
                act.wait_ge(hT_mm, t + 1)
                if not known_below(t, 2):
                    act.wait_ge(w2_mm, t - 1)
                b0, n = (5 + p, 1) if first else (5, 2)
                act.activation(HT[p][:, :, :].rearrange("p k n -> p (k n)"),
                               PS[:, b0:b0 + n, :].rearrange("p h n -> p (h n)"),
                               ACT.Relu if first else ACT.Copy).then_inc(hT_ready, 1)

            def step(t, p):
                take_h(t, p)
                if not first and not (isinstance(t, int) and t + 1 >= SLOT_TILES):
                    gelu(t + 1, 1 - p)
                if not (isinstance(t, int) and t + 2 >= SLOT_TILES):
                    take_x(t + 2, p)

            take_x(0, 0)
            take_x(1, 1)
            if not first:
                gelu(0, 0)
            tiles_loop(act, step)

        @block.tensor
        def _(pe):
            nm.tensor(pe)
            pe.wait_ge(small_in, 16 * NSMALL)
            pe.wait_ge(nm.xT_ready, KD * B)
            for i in range(NT):
                for k in range(KD):
                    last = pe.matmul(PS[:, 4, i * EXP:(i + 1) * EXP], XT[:, k, i * P:(i + 1) * P], wr[:, k, :],
                                     start=(k == 0), stop=(k == KD - 1), skip_group_check=True)
            last.then_inc(lg_mm, 1)
            pe.wait_ge(oh_ready, 1)
            pe.wait_ge(ones_set, 1)
            hot = OH[:, :, :].rearrange("p i e -> p (i e)")
            pe.matmul(PS[:, 5, 0:NT * EXP], tri[:, :], hot, start=True, stop=True)
            pe.matmul(PS[:, 5, NT * EXP:2 * NT * EXP], ones[:, :], hot, start=True, stop=True).then_inc(rank_mm, 1)
            pe.wait_ge(ext_ready, 1)
            pe.wait_ge(weights.loaded, 16 * weights.loads)
            if not first:
                pe.wait_ge(w2_in, 16)

            def transpose_x(t, p):
                pe.wait_ge(xs_in[p], (t - p) * 8 + 16)
                if not known_below(t, 1):
                    pe.wait_ge(xsT_ready, t)
                for k in range(KD):
                    last = pe.transpose(PS[:, 0, k * P:(k + 1) * P], Xs[p][:, k * P:(k + 1) * P], sh.ident[:, :])
                last.then_inc(xsT_mm, 1)

            def up(t, p):
                e = pe.value_load(ext[0:1, bass.ds(t, 1)], min_val=0, max_val=EXP - 1)
                pe.wait_ge(xsT_ready, t + 1)
                if not known_below(t, 2):
                    pe.wait_ge(h_sum, t - 1)
                for half in range(NB1):
                    for k in range(KD):
                        last = pe.matmul(PS[:, 1 + p * NB1 + half, :], XsT[p][:, k, :],
                                         W1[:, k, bass.ds(e * F + half * BANK, BANK)],
                                         start=(k == 0), stop=(k == KD - 1))
                last.then_inc(w1_mm, 1)

            def transpose_h(t, p):
                pe.wait_ge(h_sum if first else h_ready, t + 1)
                if first:
                    if not known_below(t, 2):
                        pe.wait_ge(hT_ready, t - 1)
                elif not known_below(t, 1):
                    pe.wait_ge(hT_ready, t)
                for k in range(KF):
                    bank = 5 + p if first else 5 + k // TB
                    last = pe.transpose(PS[:, bank, k % TB * P:(k % TB + 1) * P], Hs[p][:, k * P:(k + 1) * P],
                                        sh.ident[:, :])
                last.then_inc(hT_mm, 1)

            def down(t, p):
                e = pe.value_load(ext[0:1, bass.ds(t, 1)], min_val=0, max_val=EXP - 1) if first else 0
                pe.wait_ge(hT_ready, t + 1)
                if not known_below(t, 1):
                    pe.wait_ge(y_ready, t)
                for k in range(KF):
                    last = pe.matmul(PS[:, 7, 0:D], HT[p][:, k, :], W2[:, k, bass.ds(e * D, D)],
                                     start=(k == 0), stop=(k == KF - 1))
                last.then_inc(w2_mm, 1)

            def step(t, p):
                transpose_h(t, p)
                if not (isinstance(t, int) and t + 1 >= SLOT_TILES):
                    up(t + 1, 1 - p)
                down(t, p)
                if not (isinstance(t, int) and t + 2 >= SLOT_TILES):
                    transpose_x(t + 2, p)

            transpose_x(0, 0)
            transpose_x(1, 1)
            up(0, 0)
            tiles_loop(pe, step)


def experts0_stage(nc, ctx, sh, A):
    experts_stage(nc, ctx, sh, A, 0)


def experts1_stage(nc, ctx, sh, A):
    experts_stage(nc, ctx, sh, A, 1)


def layouts(np, I):
    def ktile(w):
        return w.reshape(-1, P, w.shape[-1]).transpose(1, 0, 2)

    def cols(v):
        return v.reshape(-1, P).T

    def dim_major(w):
        return w.reshape(*w.shape[:-1], NG, GH, HD).swapaxes(-1, -2).reshape(w.shape)

    def rows(v):
        return np.broadcast_to(v, (P, v.shape[-1]))

    A = {}
    A["x"] = I["x"].reshape(NT, P, D).transpose(1, 0, 2)
    A["ident"] = np.eye(P, dtype=np.float32)
    A["tri"] = np.triu(np.ones((P, P), np.float32))
    A["sel"] = np.broadcast_to(np.eye(8, dtype=np.float32)[:, :, None], (8, 8, P))
    A["m_nw"] = rows(I["L0_attn_norm_w"])
    A["m_rw1"] = ktile(I["L0_attn_r_w1"].T)
    A["m_rw2"] = I["L0_attn_r_w2"].T
    A["m_rb1"] = I["L0_attn_r_b1"][:, None]
    A["m_rb2"] = rows(I["L0_attn_r_b2"])
    cw, cb = I["L0_attn_conv_w"], I["L0_attn_conv_b"]
    A["m_cwx"] = ktile(cw[0:512])
    A["m_cbx"] = cols(cb[0:512])
    A["m_cwbc"] = cw[512:].reshape(2, 64, 4).transpose(1, 0, 2)
    A["m_cbbc"] = cb[512:].reshape(2, 64).T
    A["m_hp"] = np.stack([I["L0_attn_dt_bias"], I["L0_attn_A_log"]], 1)
    A["m_D"] = cols(np.repeat(I["L0_attn_D_param"], 64))
    A["m_gw"] = cols(I["L0_attn_gnorm_w"])
    A["m_win"] = ktile(I["L0_attn_in_proj_w"].T)
    A["m_wout"] = ktile(I["L0_attn_out_proj_w"].T)
    A["query_tail"] = np.array([[0], [0], [1]], np.float32)
    A["ctxT"] = I["ctx_1024"].transpose(2, 0, 1).reshape(KD, P, -1).transpose(1, 0, 2)
    A["mask"] = I["mask_Bx1x1xS2_if1"].reshape(B, -1)
    for n in ("q", "k", "v", "o"):
        A["c_w" + n] = ktile(I["L0_xattn_w" + n].T)
    for n in ("c_wq", "c_wk"):
        A[n] = dim_major(A[n])
    A["c_bq"], A["c_bk"] = cols(dim_major(I["L0_xattn_bq"])), cols(dim_major(I["L0_xattn_bk"]))
    A["c_bv"], A["c_bo"] = rows(I["L0_xattn_bv"]), rows(I["L0_xattn_bo"])
    A["tris"] = np.triu(np.ones((P, P), np.float32), 1)
    A["iota"] = rows(np.arange(16, dtype=np.float32))
    A["iotaP"] = rows(P * np.arange(8, dtype=np.float32))
    A["e_wr"], A["e_br"] = ktile(I["L0_ffn_w_router"]), rows(I["L0_ffn_b_router"])
    A["e_w1"] = I["L0_ffn_w1"].reshape(8, KD, P, -1).transpose(0, 2, 1, 3)
    A["e_b1"] = I["L0_ffn_b1"].reshape(1, -1)
    A["e_w2"] = I["L0_ffn_w2"].reshape(8, 4, P, D).transpose(0, 2, 1, 3)
    A["e_b2"] = rows(I["L0_ffn_b2"].reshape(-1))
    A["g_wr"] = ktile(I["L1_ffn_Wr"].T)
    A["g_w1"] = I["L1_ffn_W1"].reshape(8, KD, P, -1).transpose(0, 2, 1, 3)
    A["g_b1"] = I["L1_ffn_b1"].reshape(1, -1)
    A["g_w2"] = ktile(I["L1_ffn_Wo"])
    A["g_b2"] = rows(I["L1_ffn_bo"])
    A["g_gb"] = np.broadcast_to(np.stack([I["L1_ffn_gamma"], I["L1_ffn_beta"]]), (P, 2, D))
    A["s_wq"] = I["L1_attn_proj_q"].reshape(8, KD, P, P).transpose(2, 0, 1, 3)
    A["s_wk"], A["s_wv"] = ktile(I["L1_attn_proj_k"]), ktile(I["L1_attn_proj_v"])
    A["s_wo"] = I["L1_attn_proj_o"].transpose(2, 0, 1)
    A["h_wq"], A["h_wc"] = ktile(I["L1_xattn_Wq"].T), ktile(I["L1_xattn_Wc"].T)
    A["h_wq"] = dim_major(A["h_wq"])
    A["h_ctxT"] = dim_major(I["ctx_1024"]).transpose(2, 0, 1).reshape(KD, P, -1).transpose(1, 0, 2)
    A["h_wkv"] = ktile(dim_major(I["L1_xattn_Wkv"]).T)
    A["h_ktc"] = np.array([[1], [1], [0]], np.float32)
    A["c_ktc"] = np.array([[0, 1], [0, 1], [MASKED, -MASKED]], np.float32)
    return {k: np.ascontiguousarray(v) for k, v in A.items()}


STAGES = [mamba_stage, cross_stage, experts0_stage, shared_kv_stage, hard_cross_stage, experts1_stage]


def zero_slots(sp, sh):
    for xs in sh.xs:
        sp.dma_start(xs.rearrange("(t p) c -> p t c", p=P),
                     sh.zero[:, :].unsqueeze(1).to_broadcast([P, SLOT_TILES, D])).then_inc(sh.zeroed, 16)


def constants(nc, ctx, sh, A):
    zero_set = ctx.enter_context(nc.semaphore("zero_set"))
    const_in, identb_made = ctx.enter_context(nc.semaphore("const_in")), ctx.enter_context(nc.semaphore("identb_made"))
    with nc.Block() as block:
        @block.sync
        def _(sp):
            sp.dma_start(sh.X[:, :, :], A["x"]).then_inc(const_in, 16)
            sp.dma_start(sh.ident[:, :], A["ident"]).then_inc(const_in, 16)
            sp.dma_start(sh.query_tail[:, :], A["query_tail"]).then_inc(const_in, 16)
            sp.wait_ge(const_in, 48)


        @block.gpsimd
        def _(pool):
            pool.memset(sh.mhalf[:, :], -0.5)
            pool.memset(sh.zero[:, :], 0.0).then_inc(zero_set, 1)
            pool.wait_ge(zero_set, 1)

        @block.vector
        def _(dve):
            dve.wait_ge(const_in, 48)
            dve.tensor_copy(sh.identb[:, :], sh.ident[:, :]).then_inc(identb_made, 1)
            dve.wait_ge(identb_made, 1)


def decoder(nc, A, out, stages=None):
    ctx = ExitStack()
    with ctx:
        sh = Shared()
        sh.PS = ctx.enter_context(nc.psum_tensor("PS", [P, 8, BANK], F32))
        sh.X = ctx.enter_context(nc.sbuf_tensor("X", [P, NT, D], F32))
        sh.XN = ctx.enter_context(nc.sbuf_tensor("XN", [P, NT, D], F32))
        sh.XT = ctx.enter_context(nc.sbuf_tensor("XT", [P, KD, T], F32))
        sh.mhalf = ctx.enter_context(nc.sbuf_tensor("mhalf", [P, NT], F32))
        sh.zero = ctx.enter_context(nc.sbuf_tensor("zero", [P, D], F32))
        sh.ident = ctx.enter_context(nc.sbuf_tensor("ident", [P, P], F32))
        sh.identb = ctx.enter_context(nc.sbuf_tensor("identb", [P, P], BF16))
        sh.query_tail = ctx.enter_context(nc.sbuf_tensor("query_tail", [TAIL_ROWS, 1], F32))
        sh.area = ctx.enter_context(nc.sbuf_tensor("area", [P, AREA], F32))
        sh.weights = [ExpertWeights(nc, ctx, sh, A, layer) for layer in range(2)]
        sh.xs = [nc.dram_tensor(f"xs{layer}", [SLOTS, D], F32, kind="Internal").ap() for layer in range(2)]
        sh.zeroed, sh.out_stored = (ctx.enter_context(nc.semaphore(n)) for n in ("zeroed", "out_stored"))
        sh.out = out
        constants(nc, ctx, sh, A)
        for s in (STAGES if stages is None else stages):
            s(nc, own := StageSemaphores(nc), sh, A)
            own.clear()


def kernel(**inputs):
    import numpy as _np
    import concourse.bacc as _bacc
    from concourse import mybir as _mybir
    from concourse.bass_utils import run_bass_kernel_spmd as _run

    nc = _bacc.Bacc("TRN2", target_bir_lowering=False, num_devices=1)
    arrays = layouts(_np, {k: _np.asarray(v) for k, v in inputs.items()})
    A = {k: nc.dram_tensor("in_" + k, v.shape, _mybir.dt.from_np(v.dtype), kind="ExternalInput").ap()
         for k, v in arrays.items()}
    out = nc.dram_tensor("out_x", (P, NT, D), F32, kind="ExternalOutput").ap()
    decoder(nc, A, out)
    r = _run(nc, [{"in_" + k: v for k, v in arrays.items()}], core_ids=[0])
    y = r.results[0]["out_x"]
    return y.transpose(1, 0, 2).reshape(B, S, D)
```

```python
from contextlib import ExitStack

import concourse.bass as bass
from concourse import mybir

ALU = mybir.AluOpType
ACT = mybir.ActivationFunctionType
AX = mybir.AxisListType
F32 = mybir.dt.float32
BF16 = mybir.dt.bfloat16
I32 = mybir.dt.int32
U32 = mybir.dt.uint32

P = 128
B, S, D = 2, 512, 256
T = B * S
NT = T // P
TB = S // P
AREA = 17160
KD = D // P
BANK = 512


class Chain:

    def __init__(self, eng, sem):
        self.eng, self.sem, self.n = eng, sem, 0

    def link(self, ins):
        self.n += 1
        ins.then_inc(self.sem, 1)
        self.eng.wait_ge(self.sem, self.n)


def layernorm_vector(dve, link, src, dst, st6, mv, rstd, var_ready, rstd_ready, normed):
    for b in range(B):
        for i in range(b * TB, (b + 1) * TB):
            last = dve.bn_stats(st6[:, i, :], src[:, i, :])
        link(last)
        for i in range(b * TB, (b + 1) * TB):
            last = dve.bn_aggr(mv[:, i, :], st6[:, i, :])
        last.then_inc(var_ready, 1)
    dve.wait_ge(var_ready, B)
    normalise_vector(dve, src, dst, mv, rstd, rstd_ready, normed)


def normalise_vector(dve, src, dst, mv, rstd, rstd_ready, normed):
    for b in range(B):
        if rstd_ready is not None:
            dve.wait_ge(rstd_ready, b + 1)
        for i in range(b * TB, (b + 1) * TB):
            last = dve.tensor_scalar(dst[:, i, :], src[:, i, :], mv[:, i, 0:1], rstd[:, i:i + 1],
                                     ALU.subtract, ALU.mult)
        last.then_inc(normed, 1)


def inverse_deviations_gpsimd(pool, mhalf, mv, rstd, eps, var_ready, eps_added, rstd_ready):
    for b in range(B):
        tiles = slice(b * TB, (b + 1) * TB)
        pool.wait_ge(var_ready, b + 1)
        pool.tensor_scalar(rstd[:, tiles], mv[:, tiles, 1], eps, None, ALU.add).then_inc(eps_added, 1)
        pool.wait_ge(eps_added, b + 1)
        pool.tensor_tensor(rstd[:, tiles], rstd[:, tiles], mhalf[:, tiles], ALU.pow).then_inc(rstd_ready, 1)
    pool.wait_ge(rstd_ready, B)


class NextStatistics:

    LN_EPS = 1e-05

    def __init__(self, sh, sem):
        self.sh = sh
        self.st6_ready, self.var_ready, self.eps_added, self.rstd_ready = (
            sem("next_" + n) for n in ("st6_ready", "var_ready", "eps_added", "rstd_ready"))

    def tile(self, dve, i, written, value):
        dve.wait_ge(written, value)
        dve.bn_stats(self.sh.st6[:, i, :], self.sh.X[:, i, :]).then_inc(self.st6_ready, 1)
        if i % TB == TB - 1:
            dve.wait_ge(self.st6_ready, i + 1)
            for j in range(i + 1 - TB, i + 1):
                last = dve.bn_aggr(self.sh.mv[:, j, :], self.sh.st6[:, j, :])
            last.then_inc(self.var_ready, 1)

    def gpsimd(self, pool):
        inverse_deviations_gpsimd(pool, self.sh.mhalf, self.sh.mv, self.sh.rstd, self.LN_EPS,
                                  self.var_ready, self.eps_added, self.rstd_ready)


def transposes_tensor(pe, PS, XN, ident, ready, per_batch, done):
    for b in range(B):
        pe.wait_ge(ready, (b + 1) * per_batch)
        for k in range(KD):
            for i in range(TB):
                last = pe.transpose(PS[:, KD * b + k, i * P:(i + 1) * P],
                                    XN[:, b * TB + i, k * P:(k + 1) * P], ident[:, :])
            last.then_inc(done, 1)


class Shared:
    pass


class Area:

    def __init__(self, whole):
        self.whole, self.used = whole, 0

    def take(self, shape, dt=F32):
        words = 1
        for n in shape[1:]:
            words *= n
        words = words * mybir.dt.size(dt) // 4
        flat = self.whole[0:shape[0], self.used:self.used + words]
        self.used += words
        if dt != F32:
            flat = flat.bitcast(dt)
        names = "abcd"[:len(shape) - 1]
        return flat.rearrange(f"p ({' '.join(names)}) -> p {' '.join(names)}", **dict(zip(names, shape[1:])))


class ExpertWeights:

    EXP = 8

    def __init__(self, nc, ctx, sh, A, layer):
        self.first = layer == 0
        self.pre = "e_" if self.first else "g_"
        self.F = 512 if self.first else 1024
        self.KF = self.F // P
        area = Area(sh.area)
        self.W1 = area.take([P, KD, self.EXP * self.F])
        self.W2 = area.take([P, self.KF, self.EXP * D]) if self.first else None
        self.A = A
        self.loaded = ctx.enter_context(nc.semaphore(self.pre + "weights_loaded"))
        self.loads = (2 if self.first else 1) * self.EXP

    def load_expert(self, eng, e):
        def cut(name):
            return self.A[self.pre + name][bass.ds(e, 1), :, :, :].rearrange("e p k f -> p (e k) f")
        F = self.F
        eng.dma_start(self.W1[:, :, bass.ds(e * F, F)], cut("w1")).then_inc(self.loaded, 16)
        if self.first:
            eng.dma_start(self.W2[:, :, bass.ds(e * D, D)], cut("w2")).then_inc(self.loaded, 16)


SLOT_TILES = NT + ExpertWeights.EXP - 1
SLOTS = SLOT_TILES * P


class StageSemaphores:

    def __init__(self, nc):
        self.nc, self.held = nc, []

    def enter_context(self, semaphore):
        handle = semaphore.__enter__()
        self.held.append((semaphore, handle))
        return handle

    def clear(self):
        nums = sorted(h.num for _, h in self.held)
        starts = [n for n in nums if n - 1 not in nums]
        ends = [n + 1 for n in nums if n + 1 not in nums]
        for lo, hi in zip(starts, ends):
            self.nc.all_engine_barrier(sems_to_clear=range(lo, hi))
        for semaphore, _ in self.held:
            semaphore.__exit__(None, None, None)


def mamba_stage(nc, ctx, sh, A):
    HEADS, HD, DI, DS, TAPS = 8, 64, 512, 64, 4
    MX = DI // P
    PAD = TAPS - 1
    DT0, B0, C0, X0, Z0 = 2 * DI + 2 * DS, 2 * DI, 2 * DI + DS, DI, 0
    RMS_EPS, GN_EPS, LN_EPS = 1.1920929e-07, 1e-05, 1e-05
    PS, X, XN, XT, ident = sh.PS, sh.X, sh.XN, sh.XT, sh.ident

    stage = ExitStack()
    mhalf = sh.mhalf

    def sb(name, shape, dt=F32):
        return stage.enter_context(nc.sbuf_tensor("m_" + name, shape, dt))

    def sem(name):
        return ctx.enter_context(nc.semaphore("m_" + name))

    area = Area(sh.area)
    w_in = sb("w_in", [P, KD, 2 * DI + 2 * DS + HEADS])
    w_out = sb("w_out", [P, MX, D])
    rw1, rw2 = sb("rw1", [P, KD, 32]), sb("rw2", [32, 3])
    rb1, rb2 = sb("rb1", [32, 1]), sb("rb2", [P, 3])
    cwx, cbx = sb("cwx", [P, MX, TAPS]), sb("cbx", [P, MX])
    cwbc, cbbc = sb("cwbc", [DS, 2, TAPS]), sb("cbbc", [DS, 2])
    hp = sb("hp", [HEADS, 2])
    negA = sb("negA", [HEADS, 1])
    Dv, gw = sb("Dv", [P, MX]), sb("gw", [P, MX])
    tri = sb("tri", [P, P])
    sel = sb("sel", [HEADS, HEADS, P])
    XL = sb("XL", [P, NT, D])
    st6, mv, rstd = sh.st6, sh.mv, sh.rstd
    following = NextStatistics(sh, sem)
    ms = sb("ms", [P, NT])
    rr, rms = sb("rr", [P, NT]), sb("rms", [P, NT])
    xsum = sb("xsum", [P, KD, B])
    hid, hidB = sb("hid", [32, B]), sb("hidB", [32, B, P])
    lg, mxl, pr, psm = sb("lg", [P, B, 3]), sb("mxl", [P, B]), sb("pr", [P, B, 3]), sb("psm", [P, B])
    pmam = sb("pmam", [P, B])
    dtr, ab, sp, dt = (sb(n, [HEADS, T]) for n in ("dtr", "ab", "sp", "dt"))
    La = sb("La", [HEADS, T])
    TD = sb("TD", [P, 3, NT, HEADS])
    XC = [sb(f"XC{n}", [P, B, PAD + S]) for n in range(2)]
    CV = [sb(f"CV{n}", [P, B, S]) for n in range(2)]
    nw, ones = area.take([P, D]), area.take([P, S])
    XH = area.take([P, MX, T])
    BC = sb("BC", [DS, 2, T])
    SZ = area.take([P, MX, T])
    XD = area.take([P, NT, DI])
    GT = area.take([P, B, TB * BANK])
    Lm = [sb(f"Lm{n}", [P, TB, P]) for n in range(2)]
    E = [sb(f"E{n}", [P, 5 * BANK]) for n in range(2)]
    W = [sb(f"W{n}", [P, TB * BANK]) for n in range(2)]
    SQ, YG = XH, SZ
    base = XL
    gr = sb("gr", [P, NT])
    row = [XC[n][0:1, 1, 0:S] for n in range(2)]
    yt = [XC[n][:, 0, 0:S] for n in range(2)]

    small_in, w_in_in, w_out_in = sem("small_in"), sem("w_in_in"), sem("w_out_in")
    normed, squared, xn_ready = sem("normed"), sem("squared"), sem("xn_ready")
    xT_done, xT_ready = sem("xT_done"), sem("xT_ready")
    proj_done, proj_taken = sem("proj_done"), sem("proj_taken")
    hid_mm, hid_ready, hidB_ready, lg_mm, lg_ready, pr_ready = (
        sem(n) for n in ("hid_mm", "hid_ready", "hidB_ready", "lg_mm", "lg_ready", "pr_ready"))
    negA_ready, sp_ready, La_ready = sem("negA_ready"), sem("sp_ready"), sem("La_ready")
    td_mm, td_ready = sem("td_mm"), sem("td_ready")
    padded, conv_ready, silu_ready = sem("padded"), sem("conv_ready"), sem("silu_ready")
    xh_mm, xd_ready = sem("xh_mm"), sem("xd_ready")
    g_mm, g_copied, g_ready = sem("g_mm"), sem("g_copied"), sem("g_ready")
    decay_mm, diag_ready, e_ready, w_ready, y_mm, yt_ready, yg_ready = (
        sem(n) for n in ("decay_mm", "diag_ready", "e_ready", "w_ready", "y_mm", "yt_ready", "yg_ready"))
    sq_ready, w_out_scaled, ss_mm, out_mm, base_ready = (
        sem(n) for n in ("sq_ready", "w_out_scaled", "ss_mm", "out_mm", "base_ready"))
    var_ready, eps_added, rstd_ready, ms_ready, rms_ready = (
        sem(n) for n in ("var_ready", "eps_added", "rstd_ready", "ms_ready", "rms_ready"))
    own_v, own_a, own_p = sem("own_v"), sem("own_a"), sem("own_p")
    out_taken, row_mm, row_ready = sem("out_taken"), sem("row_mm"), sem("row_ready")

    def out_bank(i):
        return 4 + i % 2

    mtiles = [("dt", DT0, HEADS, 0), ("bc", B0, DS, 0), ("bc", C0, DS, 1)]
    for m in range(MX):
        mtiles += [("x", X0 + P * m, P, m), ("z", Z0 + P * m, P, m)]
    convs = [t for t in mtiles if t[0] in ("bc", "x")]
    NSMALL = 14

    with stage, nc.Block() as block:

        @block.sync
        def _(sp_):
            for dst, name in ((nw, "m_nw"), (rw1, "m_rw1"), (rw2, "m_rw2"), (rb1, "m_rb1"),
                              (rb2, "m_rb2"), (cwx, "m_cwx"), (cbx, "m_cbx"), (cwbc, "m_cwbc"),
                              (cbbc, "m_cbbc"), (hp, "m_hp"), (Dv, "m_D"), (gw, "m_gw"),
                              (tri, "tri"), (sel, "sel")):
                src = A[name]
                sp_.dma_start(dst[tuple(slice(None) for _ in dst.shape)], src).then_inc(small_in, 16)
            sp_.dma_start(w_in[:, :, :], A["m_win"]).then_inc(w_in_in, 16)
            sp_.dma_start(w_out[:, :, :], A["m_wout"]).then_inc(w_out_in, 16)
            zero_slots(sp_, sh)

        @block.gpsimd
        def _(pool):
            c = Chain(pool, own_p)
            for n in range(2):
                last = pool.memset(XC[n][:, :, 0:PAD], 0.0)
            pool.memset(ones[:, :], 1.0).then_inc(padded, 1)
            inverse_deviations_gpsimd(pool, mhalf, mv, rstd, LN_EPS, var_ready, eps_added, rstd_ready)
            for b in range(B):
                tiles = slice(b * TB, (b + 1) * TB)
                pool.wait_ge(ms_ready, b + 1)
                pool.tensor_tensor(rms[:, tiles], rr[:, tiles], mhalf[:, tiles], ALU.pow).then_inc(rms_ready, 1)
            pool.wait_ge(xn_ready, NT)
            c.link(pool.tensor_tensor(base[:, :, :], X[:, :, :], XL[:, :, :], ALU.add))
            pool.wait_ge(pr_ready, 1)
            pool.wait_ge(xT_done, KD * B)
            for i in range(NT):
                b = i // TB
                last = pool.tensor_scalar(XN[:, i, :], XN[:, i, :], pr[:, b, 0:1], None, ALU.mult)
            c.link(last)
            pool.wait_ge(w_out_in, 16)
            for m in range(MX):
                last = pool.tensor_scalar(w_out[:, m, :], w_out[:, m, :], gw[:, m:m + 1], None, ALU.mult)
            last.then_inc(w_out_scaled, 1)
            pool.tensor_tensor(base[:, :, :], base[:, :, :], XN[:, :, :], ALU.add).then_inc(base_ready, 1)
            def inverse_rms(b):
                tiles = slice(b * TB, (b + 1) * TB)
                pool.wait_ge(ms_ready, B + b + 1)
                pool.tensor_tensor(rr[:, tiles], gr[:, tiles], mhalf[:, tiles], ALU.pow).then_inc(rms_ready, 1)

            for n in range(B * MX):
                b, m = divmod(n, MX)
                cols = slice(b * S, (b + 1) * S)
                pool.wait_ge(yt_ready, n + 1)
                pool.tensor_tensor(YG[:, m, cols], yt[n % 2], SZ[:, m, cols], ALU.mult).then_inc(yg_ready, 1)
                if n == MX + 1:
                    inverse_rms(0)
            inverse_rms(1)
            following.gpsimd(pool)

        @block.vector
        def _(dve):
            c = Chain(dve, own_v)
            layernorm_vector(dve, c.link, X, XL, st6, mv, rstd, var_ready, rstd_ready, normed)
            for b in range(B):
                tiles = slice(b * TB, (b + 1) * TB)
                dve.wait_ge(squared, (b + 1) * TB)
                dve.tensor_scalar(rr[:, tiles], ms[:, tiles], 1.0 / D, RMS_EPS, ALU.mult, ALU.add).then_inc(ms_ready, 1)
            dve.wait_ge(small_in, 16 * NSMALL)
            for i in range(NT):
                dve.wait_ge(rms_ready, i // TB + 1)
                dve.scalar_tensor_tensor(out=XN[:, i, :], in0=XL[:, i, :], scalar=rms[:, i:i + 1],
                                         in1=nw[:, :], op0=ALU.mult, op1=ALU.mult).then_inc(xn_ready, 1)

            for n, (what, _, rows, m) in enumerate(convs):
                w = cwbc[:, m, :] if what == "bc" else cwx[:, m, :]
                xc, cv = XC[n % 2], CV[n % 2]
                dve.wait_ge(proj_taken, 2 * (mtiles.index(convs[n]) + 1))
                for tap in range(TAPS - 1):
                    last = dve.scalar_tensor_tensor(out=cv[0:rows, :, :], in0=xc[0:rows, :, tap:tap + S],
                                                    scalar=w[0:rows, tap:tap + 1], in1=cv[0:rows, :, :],
                                                    op0=ALU.mult, op1=ALU.add)
                    if tap < TAPS - 2:
                        c.link(last)
                last.then_inc(conv_ready, 1)
                if n == 0:
                    dve.wait_ge(hid_ready, 1)
                    dve.tensor_copy(hidB[:, :, :], hid[:, :].unsqueeze(2).to_broadcast([32, B, P])).then_inc(hidB_ready, 1)
                    dve.wait_ge(sp_ready, 1)
                    c.link(dve.tensor_scalar(ab[:, :], dtr[:, :], 0.0, None, ALU.max))
                    c.link(dve.tensor_tensor(dt[:, :], ab[:, :], sp[:, :], ALU.add))
                    dve.wait_ge(negA_ready, 1)
                    c.link(dve.tensor_scalar(ab[:, :], dt[:, :], negA[:, 0:1], -1.0, ALU.mult, ALU.mult))
                    dve.wait_ge(padded, 1)
                    for b in range(B):
                        cols = slice(b * S, (b + 1) * S)
                        last = dve.tensor_tensor_scan(La[:, cols], ones[0:HEADS, :], ab[:, cols], 0.0,
                                                      ALU.mult, ALU.add)
                    last.then_inc(La_ready, 1)
                if n == 1:
                    dve.wait_ge(td_mm, 1)
                    for slot in (0, 1):
                        src = PS[:, 2, slot * NT * HEADS:(slot + 1) * NT * HEADS]
                        last = dve.tensor_copy(TD[:, 2 * slot, :, :], src.rearrange("p (i h) -> p i h", i=NT))
                    c.link(last)
                    dve.tensor_scalar(TD[:, 1, :, :], src.rearrange("p (i h) -> p i h", i=NT),
                                      -1.0, None, ALU.mult).then_inc(td_ready, 1)
                    dve.wait_ge(lg_mm, 1)
                    c.link(dve.tensor_tensor(lg[:, :, :], PS[:, 1, 0:3 * B].rearrange("p (b e) -> p b e", b=B),
                                             rb2[:, :].unsqueeze(1).to_broadcast([P, B, 3]), ALU.add))
                    c.link(dve.tensor_reduce(mxl[:, :], lg[:, :, :], AX.X, ALU.max))
                    dve.tensor_tensor(lg[:, :, :], lg[:, :, :], mxl[:, :].unsqueeze(2).to_broadcast([P, B, 3]),
                                      ALU.subtract).then_inc(lg_ready, 1)

            dve.wait_ge(lg_ready, 2)
            c.link(dve.tensor_reduce(psm[:, :], pr[:, :, :], AX.X, ALU.add))
            c.link(dve.reciprocal(mxl[:, :], psm[:, :]))
            c.link(dve.tensor_tensor(pr[:, :, :], pr[:, :, :], mxl[:, :].unsqueeze(2).to_broadcast([P, B, 3]),
                                     ALU.mult))
            dve.tensor_tensor(pmam[:, :], pr[:, :, 1], pr[:, :, 2], ALU.add).then_inc(pr_ready, 1)

            for n in range(B * TB):
                b, s = divmod(n, TB)
                dve.wait_ge(g_copied, n + 1)
                o = s * (BANK + P)
                dve.tensor_tensor(GT[:, b, o:o + P], GT[:, b, o:o + P], tri[:, :], ALU.mult).then_inc(g_ready, 1)

            for i in range(NT):
                dve.wait_ge(xh_mm, i + 1)
                dve.tensor_tensor(XD[:, i, :].rearrange("p (h c) -> p h c", h=HEADS),
                                  PS[:, 6 + i % 2, :].rearrange("p (h c) -> p h c", h=HEADS),
                                  TD[:, 0, i, :].unsqueeze(2).to_broadcast([P, HEADS, HD]),
                                  ALU.mult).then_inc(xd_ready, 1)

            def diagonal(n):
                b, h = divmod(n, HEADS)
                dve.wait_ge(decay_mm, n + 1)
                if n >= 2:
                    dve.wait_ge(e_ready, n - 1)
                dve.tensor_tensor(Lm[n % 2][:, :, :], PS[:, n % 2, :].rearrange("p (s c) -> p s c", s=TB),
                                  TD[:, 2, b * TB:(b + 1) * TB, h].unsqueeze(2).to_broadcast([P, TB, P]),
                                  ALU.min).then_inc(diag_ready, 1)

            def weights(n):
                b = n // HEADS
                dve.wait_ge(e_ready, n + 1)
                if n >= 2:
                    dve.wait_ge(y_mm, n - 1)
                for s in range(TB):
                    o, m = s * BANK + s * P, S - s * P
                    last = dve.tensor_tensor(W[n % 2][:, o:o + m], E[n % 2][:, o:o + m], GT[:, b, o:o + m], ALU.mult)
                last.then_inc(w_ready, 1)

            def gate(n):
                b, h = divmod(n, HEADS)
                m = h // 2
                cols = slice(b * S, (b + 1) * S)
                dve.wait_ge(y_mm, n + 1)
                if n // 2 >= 2:
                    dve.wait_ge(yg_ready, n // 2 - 1)
                dve.scalar_tensor_tensor(out=yt[n // 2 % 2], in0=XH[:, m, cols], scalar=Dv[:, m:m + 1],
                                         in1=PS[:, 2 + (n // 2) % 2, :], op0=ALU.mult, op1=ALU.add).then_inc(yt_ready, 1)

            def mean_squares(b):
                tiles = slice(b * TB, (b + 1) * TB)
                dve.wait_ge(ss_mm, b + 1)
                dve.tensor_scalar(gr[:, tiles], PS[:, 7, tiles], 1.0 / DI, GN_EPS, ALU.mult, ALU.add).then_inc(ms_ready, 1)

            def take_output(b):
                tiles = slice(b * TB, (b + 1) * TB)
                dve.wait_ge(rms_ready, B + b + 1)
                c.link(dve.tensor_tensor(gr[:, tiles], rr[:, tiles], pmam[:, b:b + 1].to_broadcast([P, TB]), ALU.mult))
                dve.wait_ge(base_ready, 1)
                for i in range(b * TB, (b + 1) * TB):
                    dve.wait_ge(out_mm, i + 1)
                    dve.scalar_tensor_tensor(out=X[:, i, :], in0=PS[:, out_bank(i), 0:D], scalar=gr[:, i:i + 1],
                                             in1=base[:, i, :], op0=ALU.mult, op1=ALU.add).then_inc(out_taken, 1)
                    following.tile(dve, i, out_taken, i + 1)

            diagonal(0)
            for n in range(B * HEADS):
                if n + 1 < B * HEADS:
                    diagonal(n + 1)
                weights(n)
                if n >= 2 and n % 2 == 0:
                    gate(n - 1)
                if n == HEADS + 5:
                    mean_squares(0)
            gate(B * HEADS - 1)
            take_output(0)
            mean_squares(1)
            take_output(1)

        def silu_of(act, n):
            what, _, rows, m = convs[n]
            bias = cbbc[:, m:m + 1] if what == "bc" else cbx[:, m:m + 1]
            dst = BC if what == "bc" else XH
            act.wait_ge(conv_ready, n + 1)
            act.activation(dst[:, m, :], CV[n % 2][0:rows, :, :], ACT.Silu, bias=bias).then_inc(silu_ready, 1)

        @block.scalar
        def _(act):
            c = Chain(act, own_a)
            for i in range(NT):
                act.wait_ge(normed, i // TB + 1)
                act.activation(XN[:, i, :], XL[:, i, :], ACT.Square, accum_out=ms[:, i:i + 1]).then_inc(squared, 1)
            for g in range(KD * B):
                act.wait_ge(xT_done, g + 1)
                b, k = divmod(g, KD)
                act.activation(XT[:, k, b * S:(b + 1) * S], PS[:, g, :], ACT.Identity,
                               accum_out=xsum[:, k, b:b + 1]).then_inc(xT_ready, 1)
            act.wait_ge(small_in, 16 * NSMALL)
            act.activation(negA[:, :], hp[:, 1:2], ACT.Exp).then_inc(negA_ready, 1)
            for n, (what, _, rows, m) in enumerate(mtiles):
                for b in range(B):
                    j = 2 * n + b
                    act.wait_ge(proj_done, j + 1)
                    src = PS[0:rows, 4 + j % 4, :]
                    if what == "dt":
                        dst = dtr[:, b * S:(b + 1) * S]
                        act.activation(dst, src, ACT.Identity, bias=hp[:, 0:1]).then_inc(proj_taken, 1)
                    elif what == "z":
                        act.activation(SZ[:, m, b * S:(b + 1) * S], src, ACT.Silu).then_inc(proj_taken, 1)
                    else:
                        k = convs.index(mtiles[n])
                        w = cwbc[:, m, TAPS - 1:TAPS] if what == "bc" else cwx[:, m, TAPS - 1:TAPS]
                        if b == 0 and k >= 2:
                            act.wait_ge(conv_ready, k - 1)
                        if k == 0 and b == 0:
                            act.wait_ge(padded, 1)
                        act.activation(XC[k % 2][0:rows, b, PAD:PAD + S], src, ACT.Copy)
                        if k >= 2:
                            act.wait_ge(silu_ready, k - 1)
                        act.activation(CV[k % 2][0:rows, b, :], src, ACT.Identity, scale=w).then_inc(proj_taken, 1)
                if n == 1:
                    act.wait_ge(proj_taken, 2)
                    c.link(act.activation(ab[:, :], dtr[:, :], ACT.Abs))
                    c.link(act.activation(dt[:, :], ab[:, :], ACT.Exp, scale=-1.0))
                    act.activation(sp[:, :], dt[:, :], ACT.Ln, bias=1.0).then_inc(sp_ready, 1)
                    act.wait_ge(hid_mm, 1)
                    act.activation(hid[:, :], PS[0:32, 0, 0:B], ACT.Silu, bias=rb1[:, 0:1],
                                   scale=1.0 / S).then_inc(hid_ready, 1)
                if what == "z":
                    silu_of(act, m + 1)
                elif (what, m) == ("bc", 1):
                    silu_of(act, 0)
            silu_of(act, len(convs) - 1)
            act.wait_ge(lg_ready, 1)
            act.activation(pr[:, :, :], lg[:, :, :], ACT.Exp).then_inc(lg_ready, 1)

            for n in range(B * TB):
                b, s = divmod(n, TB)
                act.wait_ge(g_mm, n + 1)
                o, m = s * (BANK + P), S - s * P
                act.activation(GT[:, b, o:o + m], PS[:, 4 + n % 2, s * P:S], ACT.Copy).then_inc(g_copied, 1)

            def squares(n):
                b, m = divmod(n, MX)
                cols = slice(b * S, (b + 1) * S)
                act.wait_ge(yg_ready, n + 1)
                act.activation(SQ[:, m, cols], YG[:, m, cols], ACT.Square).then_inc(sq_ready, 1)

            def take_row(b):
                act.wait_ge(row_mm, b + 1)
                act.activation(row[b], PS[0:1, 6, :], ACT.Copy).then_inc(row_ready, 1)

            for n in range(B * HEADS):
                b, h = divmod(n, HEADS)
                e = E[n % 2]
                act.wait_ge(diag_ready, n + 1)
                if n >= 2:
                    act.wait_ge(w_ready, n - 1)
                for s in range(TB - 1):
                    o, m = s * BANK + (s + 1) * P, S - (s + 1) * P
                    act.activation(e[:, o:o + m], PS[:, n % 2, (s + 1) * P:S], ACT.Exp,
                                   bias=TD[:, 1, b * TB + s, h:h + 1])
                for s in range(TB):
                    last = act.activation(e[:, s * (BANK + P):s * (BANK + P) + P], Lm[n % 2][:, s, :], ACT.Exp,
                                          bias=TD[:, 1, b * TB + s, h:h + 1])
                last.then_inc(e_ready, 1)
                if n >= 3 and n % 2 == 1:
                    squares((n - 3) // 2)
                if n == HEADS + 3:
                    take_row(0)
            squares(B * MX - 1)
            take_row(1)

        @block.tensor
        def _(pe):
            pe.wait_ge(small_in, 16 * NSMALL)
            transposes_tensor(pe, PS, XN, ident, xn_ready, TB, xT_done)
            pe.wait_ge(w_in_in, 16)
            for n, (what, col, rows, m) in enumerate(mtiles):
                for b in range(B):
                    j = 2 * n + b
                    pe.wait_ge(xT_ready, KD * B)
                    if j >= 4:
                        pe.wait_ge(proj_taken, j - 3)
                    for k in range(KD):
                        last = pe.matmul(PS[0:rows, 4 + j % 4, :], w_in[:, k, col:col + rows],
                                         XT[:, k, b * S:(b + 1) * S], start=(k == 0), stop=(k == KD - 1))
                    last.then_inc(proj_done, 1)
                if n == 0:
                    for k in range(KD):
                        last = pe.matmul(PS[0:32, 0, 0:B], rw1[:, k, :], xsum[:, k, :], start=(k == 0),
                                         stop=(k == KD - 1))
                    last.then_inc(hid_mm, 1)
                if n == 3:
                    pe.wait_ge(hidB_ready, 1)
                    for b in range(B):
                        last = pe.matmul(PS[:, 1, 3 * b:3 * b + 3], hidB[:, b, :], rw2[:, :], start=True, stop=True)
                    last.then_inc(lg_mm, 1)
                if n == 4:
                    pe.wait_ge(La_ready, 1)
                    for a, src in enumerate((dt, La)):
                        for i in range(NT):
                            o = (a * NT + i) * HEADS
                            last = pe.transpose(PS[:, 2, o:o + HEADS], src[:, i * P:(i + 1) * P],
                                                ident[0:HEADS, 0:HEADS])
                    last.then_inc(td_mm, 1)
            pe.wait_ge(silu_ready, 2)
            pe.wait_ge(td_ready, 1)
            pe.wait_ge(lg_ready, 1)
            pe.wait_ge(proj_taken, 2 * len(mtiles))
            for n in range(B * TB):
                b, s = divmod(n, TB)
                if n >= 2:
                    pe.wait_ge(g_copied, n - 1)
                pe.matmul(PS[:, 4 + n % 2, s * P:S], BC[:, 0, b * S + s * P:b * S + (s + 1) * P],
                          BC[:, 1, b * S + s * P:(b + 1) * S], start=True, stop=True).then_inc(g_mm, 1)
            pe.wait_ge(silu_ready, len(convs))
            for i in range(NT):
                if i >= 2:
                    pe.wait_ge(xd_ready, i - 1)
                for m in range(MX):
                    last = pe.transpose(PS[:, 6 + i % 2, m * P:(m + 1) * P], XH[:, m, i * P:(i + 1) * P], ident[:, :])
                last.then_inc(xh_mm, 1)

            def decay(n):
                b, h = divmod(n, HEADS)
                if n >= 2:
                    pe.wait_ge(e_ready, n - 1)
                pe.matmul(PS[:, n % 2, :], sel[:, h, :], La[:, b * S:(b + 1) * S], start=True,
                          stop=True).then_inc(decay_mm, 1)

            def project(i):
                if i == 0:
                    pe.wait_ge(w_out_scaled, 1)
                if i % TB == 0:
                    pe.wait_ge(yg_ready, (i // TB + 1) * MX)
                if i >= 2:
                    pe.wait_ge(out_taken, i - 1)
                for m in range(MX):
                    last = pe.matmul(PS[:, out_bank(i), 0:D], YG[:, m, i * P:(i + 1) * P], w_out[:, m, :],
                                     start=(m == 0), stop=(m == MX - 1))
                last.then_inc(out_mm, 1)

            def sum_squares(n):
                b, m = divmod(n, MX)
                pe.wait_ge(sq_ready, n + 1)
                if b > 0 and m == 0:
                    pe.wait_ge(row_ready, b)
                last = pe.matmul(PS[0:1, 6, :], ones[:, 0:1], SQ[:, m, b * S:(b + 1) * S],
                                 start=(m == 0), stop=(m == MX - 1))
                if m == MX - 1:
                    last.then_inc(row_mm, 1)

            def sums_by_token(b):
                pe.wait_ge(row_ready, b + 1)
                if b > 0:
                    pe.wait_ge(ms_ready, B + b)
                for i in range(TB):
                    last = pe.matmul(PS[:, 7, b * TB + i:b * TB + i + 1], row[b][:, i * P:(i + 1) * P], ones[0:1, 0:1],
                                     start=True, stop=True)
                last.then_inc(ss_mm, 1)

            decay(0)
            decay(1)
            pe.wait_ge(xd_ready, NT)
            for n in range(B * HEADS):
                b, h = divmod(n, HEADS)
                half = slice((h % 2) * HD, (h % 2 + 1) * HD)
                if n + 2 < B * HEADS:
                    decay(n + 2)
                pe.wait_ge(w_ready, n + 1)
                if n >= 4 and n % 2 == 0:
                    pe.wait_ge(yt_ready, n // 2 - 1)
                for s in range(TB):
                    o, m = s * BANK + s * P, S - s * P
                    last = pe.matmul(PS[half, 2 + (n // 2) % 2, s * P:S], XD[:, b * TB + s, h * HD:(h + 1) * HD],
                                     W[n % 2][:, o:o + m], start=(s == 0), stop=(s == TB - 1),
                                     skip_group_check=True)
                last.then_inc(y_mm, 1)
                if n >= 4 and n % 2 == 0:
                    sum_squares(n // 2 - 2)
                if n == HEADS + 4:
                    sums_by_token(0)
                if n in (HEADS + 3, HEADS + 5):
                    project((n - HEADS - 3) // 2)
            for i in range(2, TB):
                project(i)
            for n in range(B * MX - 2, B * MX):
                sum_squares(n)
            project(TB)
            sums_by_token(1)
            for i in range(TB + 1, NT):
                project(i)


HEADS, HD = 16, 16
GH = 4
NG = HEADS // GH
UNITS = B * NG
VW = 32
NBLK = 6
K_ROWS = (2, 1, 0)
Q_ROWS = (0, 1, 2, 0)
K_RUNS = (0, HD, 2 * HD)
Q_RUNS = (0, 0, 3 * HD)
STACK_RUNS = (0, 3 * HD, 5 * HD, NBLK * HD + 3)
TAIL = NBLK * HD
TAIL_ROWS = 3
ROWS = TAIL + TAIL_ROWS
K_DRAM, Q_DRAM = len(K_ROWS) * HD + TAIL_ROWS, len(Q_ROWS) * HD + TAIL_ROWS
MASKED = 2.0 ** 32


class Attention:

    LOADS = 6

    def __init__(self, nc, ctx, stage, PS, name, NK, KH, ident, identb):
        def sb(n, shape, dt=F32):
            return stage.enter_context(nc.sbuf_tensor(name + n, shape, dt))

        def sem(n):
            return ctx.enter_context(nc.semaphore(name + n))

        self.PS, self.ident, self.identb = PS, ident, identb
        self.NK, self.KT, self.C, self.KH = NK, NK // P, TB * NK // BANK, KH
        self.Qs = [sb(f"Qs{n}", [ROWS, GH, S], BF16) for n in range(3)]
        self.Ks = [sb(f"Ks{n}", [ROWS, KH, NK], BF16) for n in range(3)]
        self.Vs = [sb(f"Vs{n}", [P, NK // P, KH, VW]) for n in range(3)]
        self.qtail = sb("qtail", [TAIL_ROWS, GH * S], BF16)
        self.E = [sb(f"E{n}", [P, GH, S]) for n in range(2)]
        self.mx = sb("mx", [P, TB, GH, 2])
        self.m = sb("m", [P, TB, GH])
        self.MT = sb("MT", [P, TB, GH, VW], BF16)
        self.Oraw = sb("Oraw", [P, S])
        self.rc = sb("rc", [P, TB, GH])
        self.Otok = sb("Otok", [P, UNITS, TB, GH * HD])
        self.loaded = [sem(f"loaded{n}") for n in range(3)]
        self.v_loaded = [sem(f"v_loaded{n}") for n in range(3)]
        (self.s_done, self.max_done, self.m_ready, self.mT_done, self.q_ready,
         self.st_done, self.exp_done, self.av_done, self.o_copied, self.oT_done, self.o_normed, self.rc_ready) = (
            sem(n) for n in ("s_done", "max_done", "m_ready", "mT_done", "q_ready",
                             "st_done", "exp_done", "av_done", "o_copied", "oT_done", "o_normed", "rc_ready"))
        self.m_final, self.mt_set = sem("m_final"), sem("mt_set")

    def steps(self, eng, step):
        step(0, 0, 0, 0, first=True)
        with eng.Fori(0, (UNITS - 2) // 3) as i:
            for n in range(1, 4):
                step(i * 3 + n, n % 3, i + n // 3, i + (n + 1) // 3)
        step(UNITS - 1, (UNITS - 1) % 3, (UNITS - 1) // 3, None, last=True)

    def sync(self, sp, load, between, also=None):
        for u in range(2):
            load(u, u)
        between()
        with sp.Fori(0, (UNITS - 2) // 3) as i:
            for n in range(2, 5):
                u = i * 3 + n
                sp.wait_ge(self.av_done, (u - 2) * (2 * self.KT))
                load(u, n % 3)
                if also:
                    also(u)

    def tensor(self, pe, between=None, meanwhile=None):
        PS, KT, C = self.PS, self.KT, self.C

        def scores(u, buf, rnd, c, j, first=False):
            qt, half = divmod(c, C // TB)
            if c == 0 and j == 0:
                pe.wait_ge(self.loaded[buf], (rnd + 1) * (16 * self.LOADS))
            if not (first and c == 0 and j < 2):
                pe.wait_ge(self.max_done, u * (GH * C) + (GH * c + j - 1))
            pe.matmul(PS[:, j % 2, :], self.Qs[buf][:, j, qt * P:(qt + 1) * P],
                      self.Ks[buf][:, j % self.KH, half * BANK:(half + 1) * BANK],
                      start=True, stop=True).then_inc(self.s_done, 1)

        def transposed_scores(u, buf, kt, p, first):
            if kt == 0 and p == 0:
                pe.wait_ge(self.q_ready, u * 2 + 2)
            if not (first and kt == 0):
                pe.wait_ge(self.exp_done, u * (2 * KT) + (2 * kt + p - 1))
            for j in (2 * p, 2 * p + 1):
                last = pe.matmul(PS[:, 2 + j, :], self.Ks[buf][:, j % self.KH, kt * P:(kt + 1) * P],
                                 self.Qs[buf][:, j, :], start=True, stop=True)
            last.then_inc(self.st_done, 1)

        def values(u, buf, kt, p, first=False):
            pe.wait_ge(self.exp_done, u * (2 * KT) + (2 * kt + p + 1))
            if kt == 0 and p == 0 and not first:
                pe.wait_ge(self.o_copied, u)
            for j in (2 * p, 2 * p + 1):
                last = pe.matmul(PS[32 * j:32 * j + 32, 6, :], self.Vs[buf][:, kt, j % self.KH, :],
                                 self.E[kt % 2][:, j, :], start=(kt == 0), stop=(kt == KT - 1),
                                 skip_group_check=True)
            last.then_inc(self.av_done, 1)

        def maxima_transposes(u):
            pe.wait_ge(self.m_ready, u + 1)
            for qt in range(TB):
                last = pe.transpose(PS[:, 7, :].bitcast(BF16)[:, qt * P:(qt + 1) * P],
                                    self.MT[:, qt, :, :].rearrange("p j c -> p (j c)"), self.identb[:, :])
            last.then_inc(self.mT_done, 1)

        def output_transposes(u):
            pe.wait_ge(self.o_copied, u + 1)
            for qt in range(TB):
                last = pe.transpose(PS[:, 7, qt * P:(qt + 1) * P], self.Oraw[:, qt * P:(qt + 1) * P],
                                    self.ident[:, :])
            last.then_inc(self.oT_done, 1)

        def step(u, buf, rnd, nxt, first=False, last=False):
            for p in range(2):
                if not last:
                    scores(u + 1, (buf + 1) % 3, nxt, 0, p)
            maxima_transposes(u)
            if not first:
                for p in range(2):
                    values(u - 1, (buf + 2) % 3, KT - 1, p)
            pe.wait_ge(self.v_loaded[buf], (rnd + 1) * 16)
            for kt in range(KT):
                for p in range(2):
                    if not last and kt > 0:
                        scores(u + 1, (buf + 1) % 3, nxt, kt, 2 * p)
                    transposed_scores(u, buf, kt, p, first)
                    if not last:
                        scores(u + 1, (buf + 1) % 3, nxt, kt, 2 + p if kt == 0 else 2 * p + 1)
                    if kt > 0:
                        values(u, buf, kt - 1, p, first)
                if kt == 1 and not first:
                    output_transposes(u - 1)
                if last:
                    meanwhile(pe, kt, KT)

        for c in range(C):
            for j in range(GH):
                scores(0, 0, 0, c, j, first=True)
        if between:
            between()
        self.steps(pe, step)
        for p in range(2):
            values(UNITS - 1, (UNITS - 1) % 3, KT - 1, p)
        pe.wait_ge(self.o_normed, UNITS - 1)
        output_transposes(UNITS - 1)

    def vector(self, dve, between=None, meanwhile=None):
        PS, C = self.PS, self.C

        def maxima(u, c, heads=range(GH)):
            qt, half = divmod(c, C // TB)
            for j in heads:
                dve.wait_ge(self.s_done, u * (GH * C) + (GH * c + j + 1))
                dve.tensor_reduce(self.mx[:, qt, j, half:half + 1], PS[:, j % 2, :], AX.X,
                                  ALU.max).then_inc(self.max_done, 1)

        def negated(u, first=False):
            dve.wait_ge(self.max_done, (u + 1) * (GH * C))
            if C > TB:
                dve.tensor_tensor(self.m[:, :, :], self.mx[:, :, :, 0], self.mx[:, :, :, 1],
                                  ALU.max).then_inc(self.m_final, 1)
            else:
                dve.tensor_copy(self.m[:, :, :], self.mx[:, :, :, 0]).then_inc(self.m_final, 1)
            dve.wait_ge(self.m_final, u * 2 + 1)
            if not first:
                dve.wait_ge(self.mT_done, u)
            dve.tensor_scalar(self.MT[:, :, :, 0], self.m[:, :, :], -1.0, None, ALU.mult).then_inc(self.m_final, 1)
            dve.wait_ge(self.m_final, u * 2 + 2)
            dve.scalar_tensor_tensor(out=self.MT[:, :, :, 1], in0=self.m[:, :, :], scalar=-1.0,
                                     in1=self.MT[:, :, :, 0], op0=ALU.mult,
                                     op1=ALU.subtract).then_inc(self.m_ready, 1)

        def tails(u, buf):
            dve.wait_ge(self.mT_done, u + 1)
            for j in (2, 3):
                last = dve.tensor_copy(self.Qs[buf][TAIL:ROWS, j, :],
                                       PS[32 * j:32 * j + TAIL_ROWS, 7, :].bitcast(BF16)[:, 0:S])
            last.then_inc(self.q_ready, 1)

        def normalise(u):
            src = PS[:, 7, :].rearrange("p (t j c) -> p t j c", t=TB, j=GH)
            dve.wait_ge(self.oT_done, u + 1)
            dve.reciprocal(self.rc[:, :, :], src[:, :, :, HD]).then_inc(self.rc_ready, 1)
            dve.wait_ge(self.rc_ready, u + 1)
            for qt in range(TB):
                last = dve.tensor_tensor(
                    self.Otok[:, bass.ds(u, 1), qt, :]
                    .rearrange("p u (j c) -> p (u j) c", j=GH),
                    src[:, qt, :, 0:HD], self.rc[:, qt, :].unsqueeze(2).to_broadcast([P, GH, HD]), ALU.mult)
            last.then_inc(self.o_normed, 1)

        def step(u, buf, rnd, nxt, first=False, last=False):
            if not last:
                maxima(u + 1, 0, (0, 1))
            tails(u, buf)
            if not last:
                maxima(u + 1, 0, (2, 3))
                maxima(u + 1, 1)
            if not first:
                normalise(u - 1)
            if not last:
                for c in range(2, C):
                    maxima(u + 1, c)
                negated(u + 1)

        dve.memset(self.MT[:, :, :, :], 0.0).then_inc(self.mt_set, 1)
        dve.wait_ge(self.mt_set, 1)
        dve.memset(self.MT[:, :, :, 2], 1.0).then_inc(self.mt_set, 1)
        dve.wait_ge(self.mt_set, 2)
        for c in range(C):
            maxima(0, c)
        negated(0, first=True)
        if between:
            between()
        self.steps(dve, step)
        meanwhile()
        normalise(UNITS - 1)

    def scalar(self, act):
        PS, KT = self.PS, self.KT

        def tails(u, buf):
            act.wait_ge(self.mT_done, u + 1)
            for j in (0, 1):
                last = act.activation(self.Qs[buf][TAIL:ROWS, j, :],
                                      PS[32 * j:32 * j + TAIL_ROWS, 7, :].bitcast(BF16)[:, 0:S], ACT.Copy)
            last.then_inc(self.q_ready, 1)

        def copy_output(u, last=False):
            act.wait_ge(self.av_done, (u + 1) * (2 * KT))
            if last:
                act.wait_ge(self.oT_done, u)
            else:
                act.wait_ge(self.mT_done, u + 2)
            act.activation(self.Oraw[:, :], PS[:, 6, :], ACT.Copy).then_inc(self.o_copied, 1)

        def step(u, buf, rnd, nxt, first=False, last=False):
            tails(u, buf)
            for kt in range(KT):
                for p in range(2):
                    act.wait_ge(self.st_done, u * (2 * KT) + (2 * kt + p + 1))
                    if not (first and kt < 2):
                        act.wait_ge(self.av_done, u * (2 * KT) + (2 * kt + p - 3))
                    act.activation(self.E[kt % 2][:, 2 * p:2 * p + 2, :], PS[:, 2 + 2 * p:4 + 2 * p, :],
                                   ACT.Exp, scale=0.25).then_inc(self.exp_done, 1)
                if kt == 0 and not first:
                    copy_output(u - 1)

        self.steps(act, step)
        copy_output(UNITS - 1, last=True)


class Splitter:

    def __init__(self, nc, ctx, space, name, dst, rows, n):
        self.F, self.R = [space[:, i, :] for i in range(2)], [space[:, 2 + i, :] for i in range(2)]
        self.dst, self.rows, self.n = dst, rows, n
        self.f_ready, self.p0_ready, self.r_ready, self.p1_ready, self.p2_ready = (
            ctx.enter_context(nc.semaphore(f"{name}{s}"))
            for s in ("f_ready", "p0_ready", "r_ready", "p1_ready", "p2_ready"))

    def buffer(self, dve, n):
        if n >= 2:
            dve.wait_ge(self.r_ready, n - 1)
        return self.F[n % 2][0:self.rows[n]]

    def scalar(self, act, lo, hi):
        for n in range(lo, hi + 1):
            if n < hi:
                act.wait_ge(self.f_ready, n + 1)
                act.activation(self.dst(n, 0), self.F[n % 2][0:self.rows[n]], ACT.Copy).then_inc(self.p0_ready, 1)
            if n > lo:
                act.wait_ge(self.r_ready, n)
                act.activation(self.dst(n - 1, 1), self.R[(n - 1) % 2][0:self.rows[n - 1]],
                               ACT.Copy).then_inc(self.p1_ready, 1)

    def rest(self, dve, n):
        f, r = self.F[n % 2][0:self.rows[n]], self.R[n % 2][0:self.rows[n]]
        dve.wait_ge(self.p0_ready, n + 1)
        if n >= 2:
            dve.wait_ge(self.p2_ready, n - 1)
        dve.tensor_tensor(r, f, self.dst(n, 0), ALU.subtract).then_inc(self.r_ready, 1)

    def gpsimd(self, pool, lo, hi):
        for n in range(lo, hi):
            r = self.R[n % 2][0:self.rows[n]]
            pool.wait_ge(self.p1_ready, n + 1)
            pool.tensor_tensor(self.dst(n, 2), r, self.dst(n, 1), ALU.subtract).then_inc(self.p2_ready, 1)


K_STORES, Q_STORES = 2 * len(K_ROWS), 2 * len(Q_ROWS)


def store_query_tails(sp, q_stack, qtail, done):
    sp.dma_start(q_stack[:, Q_DRAM - TAIL_ROWS:, :, :].rearrange("u r h n -> r u (h n)"),
                 qtail[:, :].unsqueeze(1).to_broadcast([TAIL_ROWS, UNITS, GH * S])).then_inc(done, 16)


def store_parts(sp, stack, order, parts, b, done):
    groups = NG // KD
    for slot, part in enumerate(order):
        for g in range(groups):
            dst = stack[b * NG:(b + 1) * NG, slot * HD:(slot + 1) * HD, :, :]
            dst = dst.rearrange("(m g) d h n -> g (d h) m n", m=KD)[g]
            src = parts(part)[g * GH * HD:(g + 1) * GH * HD, :, :]
            sp.dma_start(dst, src).then_inc(done, 16)


def load_unit(sp, at, q_stack, k_stack, values):
    def load(u, buf):
        for dst, src, runs in ((at.Ks[buf], k_stack, K_RUNS), (at.Qs[buf], q_stack, Q_RUNS)):
            for r, row in enumerate(runs):
                lo, hi = STACK_RUNS[r], STACK_RUNS[r + 1]
                sp.dma_start(dst[lo:hi, :, :], src[bass.ds(u, 1), row:row + hi - lo, :, :]
                             .rearrange("u r h n -> r (u h) n")).then_inc(at.loaded[buf], 16)
        sp.dma_start(at.Vs[buf][:, :, :, :],
                     values[:, bass.ds(u, 1), :, :, :].rearrange("p u t h c -> p (u t) h c")).then_inc(at.v_loaded[buf], 16)
    return load


class OutputProjection:

    def __init__(self, at, sh, sem, w, w_in, w_loads):
        self.following = NextStatistics(sh, sem)
        self.at, self.sh, self.w, self.w_in, self.w_loads = at, sh, w, w_in, w_loads
        self.o_placed, self.oT_done, self.oT_ready, self.out_mm, self.out_taken = (
            sem("po_" + n) for n in ("o_placed", "oT_done", "oT_ready", "out_mm", "out_taken"))

    @staticmethod
    def bank(i):
        return i % 2 if i < TB else 2 + i % 4

    def transposes(self, pe, b):
        pe.wait_ge(self.o_placed, b + 1)
        if b > 0:
            pe.wait_ge(self.out_taken, TB * b)
        for k in range(KD):
            for qt in range(TB):
                last = pe.transpose(self.sh.PS[:, k, qt * P:(qt + 1) * P],
                                    self.sh.XN[:, b * TB + qt, k * P:(k + 1) * P], self.sh.ident[:, :])
            last.then_inc(self.oT_done, 1)

    def project(self, pe, tiles):
        for i in tiles:
            pe.wait_ge(self.w_in, 16 * self.w_loads)
            pe.wait_ge(self.oT_ready, KD * (i // TB + 1))
            if 2 <= i < TB:
                pe.wait_ge(self.out_taken, i - 1)
            for k in range(KD):
                last = pe.matmul(self.sh.PS[:, self.bank(i), 0:D], self.sh.XT[:, k, i * P:(i + 1) * P],
                                 self.w[:, k, :], start=(k == 0), stop=(k == KD - 1))
            last.then_inc(self.out_mm, 1)

    def tensor_meanwhile(self, pe, kt, KT):
        if kt == KT // 4:
            self.transposes(pe, 0)
        for n in range(2):
            if kt == KT // 2 + n:
                self.project(pe, range(n * TB // 2, (n + 1) * TB // 2))

    def tensor(self, pe):
        self.transposes(pe, 1)
        self.project(pe, range(TB, NT))

    def vector(self, dve, b):
        sh = self.sh
        dve.wait_ge(self.at.o_normed, (b + 1) * NG)
        dve.tensor_copy(sh.XN[:, b * TB:(b + 1) * TB, :].rearrange("p t (g c) -> p g t c", g=NG),
                        self.at.Otok[:, b * NG:(b + 1) * NG, :, :]).then_inc(self.o_placed, 1)
        for k in range(KD):
            dve.wait_ge(self.oT_done, b * KD + k + 1)
            dve.tensor_copy(sh.XT[:, k, b * S:(b + 1) * S], sh.PS[:, k, :]).then_inc(self.oT_ready, 1)
        for i in range(b * TB, (b + 1) * TB):
            dve.wait_ge(self.out_mm, i + 1)
            dve.tensor_tensor(sh.X[:, i, :], sh.X[:, i, :], sh.PS[:, self.bank(i), 0:D],
                              ALU.add).then_inc(self.out_taken, 1)
            self.following.tile(dve, i, self.out_taken, i + 1)


class Norm:

    def __init__(self, nc, ctx, sh, name):
        self.sh = sh
        self.xn_ready, self.xT_done, self.xT_ready = (
            ctx.enter_context(nc.semaphore(name + n)) for n in ("xn_ready", "xT_done", "xT_ready"))

    def vector(self, dve):
        normalise_vector(dve, self.sh.X, self.sh.XN, self.sh.mv, self.sh.rstd, None, self.xn_ready)

    def tensor(self, pe):
        transposes_tensor(pe, self.sh.PS, self.sh.XN, self.sh.ident, self.xn_ready, 1, self.xT_done)

    def scalar(self, act):
        for g in range(KD * B):
            b, k = divmod(g, KD)
            act.wait_ge(self.xT_done, g + 1)
            act.activation(self.sh.XT[:, k, b * S:(b + 1) * S], self.sh.PS[:, g, :], ACT.Copy).then_inc(self.xT_ready, 1)


def cross_stage(nc, ctx, sh, A):
    NK = 1024
    PS, X, XN, XT = sh.PS, sh.X, sh.XN, sh.XT
    stage = ExitStack()

    def sb(name, shape, dt=F32):
        return stage.enter_context(nc.sbuf_tensor("c_" + name, shape, dt))

    def sem(name):
        return ctx.enter_context(nc.semaphore("c_" + name))

    area = Area(sh.area)

    nm = Norm(nc, ctx, sh, "c_n")
    wo, bo = sb("wo", [P, KD, D]), sb("bo", [P, D])
    VB = sb("VB", [P, UNITS, NK // P, GH, VW])
    at = Attention(nc, ctx, stage, PS, "c_a", NK, GH, sh.ident, sh.identb)
    ctxT = area.take([P, KD, B * NK])
    wq, wk, wv = (area.take([P, KD, D]) for _ in range(3))
    bq, bk = area.take([P, KD]), area.take([P, KD])
    bv = area.take([P, D])
    maski = at.E[0][:, :, :].rearrange("p j s -> p (j s)").bitcast(I32).rearrange("p (b n) -> p b n", b=B)
    ind = area.take([P, B, NK])
    ktc = area.take([TAIL_ROWS, 2])
    otok = at.Otok[0:TAIL_ROWS, :, :, :].rearrange("r u t c -> r (u t c)").bitcast(BF16)
    ktail = otok[:, 0:B * NK].rearrange("r (b n) -> r b n", b=B)
    KP = [area.take([P, B, KD, NK], BF16) for _ in range(3)]
    QP = [area.take([P, KD, T], BF16) for _ in range(3)]
    q_stack = nc.dram_tensor("c_q_stack", [UNITS, Q_DRAM, GH, S], BF16, kind="Internal").ap()
    k_stack = nc.dram_tensor("c_k_stack", [UNITS, K_DRAM, GH, NK], BF16, kind="Internal").ap()

    small_in, wv_in, wo_in, mask_in = (sem(n) for n in ("small_in", "wv_in", "wo_in", "mask_in"))
    ctx_in = [sem(f"ctx_in{b}") for b in range(B)]
    NSMALL = 6
    proj_done, proj_taken = sem("proj_done"), sem("proj_taken")
    ind_ready, tail_ready, tail_stored = sem("ind_ready"), sem("tail_ready"), sem("tail_stored")
    k_stored = [sem(f"k_stored{b}") for b in range(B)]
    q_stored = [sem(f"q_stored{b}") for b in range(B)]
    v_ones, xb_ready, qtail_set = sem("v_ones"), sem("xb_ready"), sem("qtail_set")
    NKC = B * KD * 2
    NV = B * NK // P
    NQC = B * KD

    def k_chunk(n):
        n -= NQC
        return n // 4, n // 2 % 2, n % 2

    outputs = [("split", n) for n in range(NQC)]
    for b in range(B):
        outputs += [("split", NQC + b * NKC // B + c) for c in range(NKC // B)]
        outputs += [("v", b * NV // B + t) for t in range(NV // B)]

    def dst(n, part):
        if n >= NQC:
            b, m, half = k_chunk(n)
            return KP[part][:, b, m, half * BANK:(half + 1) * BANK]
        b, m = divmod(n, KD)
        return QP[part][:, m, b * S:(b + 1) * S]

    sp_l = Splitter(nc, ctx, at.E[1][:, :, :], "c_s", dst, [P] * (NKC + NQC), NKC + NQC)
    projection = OutputProjection(at, sh, sem, wo, wo_in, 2)

    with stage, nc.Block() as block:

        @block.sync
        def _(sp):
            for d, name in ((wq, "c_wq"), (bq, "c_bq"), (wk, "c_wk"), (bk, "c_bk"), (ktc, "c_ktc"), (bv, "c_bv")):
                sp.dma_start(d[tuple(slice(None) for _ in d.shape)], A[name]).then_inc(small_in, 16)
            sp.dma_start(maski, A["mask"].unsqueeze(0).to_broadcast([P, B, NK])).then_inc(mask_in, 16)
            for b in range(B):
                sp.dma_start(ctxT[:, :, b * NK:(b + 1) * NK], A["ctxT"][:, :, b * NK:(b + 1) * NK]).then_inc(ctx_in[b], 16)
            sp.dma_start(wv[:, :, :], A["c_wv"]).then_inc(wv_in, 16)
            sp.dma_start(wo[:, :, :], A["c_wo"]).then_inc(wo_in, 16)
            sp.dma_start(bo[:, :], A["c_bo"]).then_inc(wo_in, 16)
            sp.wait_ge(qtail_set, 2)
            store_query_tails(sp, q_stack, at.qtail, tail_stored)
            sp.wait_ge(tail_ready, B)
            for b in range(B):
                for h in range(GH):
                    sp.dma_start(k_stack[b * NG:(b + 1) * NG, K_DRAM - TAIL_ROWS:, h, :].rearrange("u r n -> r u n"),
                                 ktail[:, b, :].unsqueeze(1).to_broadcast([TAIL_ROWS, NG, NK])).then_inc(tail_stored, 16)

            for b in range(B):
                sp.wait_ge(sp_l.p2_ready, (b + 1) * KD)
                store_parts(sp, q_stack, Q_ROWS, lambda part: QP[part][:, :, b * S:(b + 1) * S], b, q_stored[b])

            def store_k(b):
                sp.wait_ge(sp_l.p2_ready, NQC + (b + 1) * NKC // B)
                store_parts(sp, k_stack, K_ROWS, lambda part: KP[part][:, b, :, :], b, k_stored[b])

            def rest():
                store_k(1)
                sp.wait_ge(proj_taken, NV)
                sp.wait_ge(k_stored[1], 16 * K_STORES)
                sp.wait_ge(q_stored[1], 16 * Q_STORES)

            store_k(0)
            sp.wait_ge(tail_stored, 16 * (1 + B * GH))
            sp.wait_ge(k_stored[0], 16 * K_STORES)
            sp.wait_ge(q_stored[0], 16 * Q_STORES)
            sp.wait_ge(proj_taken, NV // B)
            weights = sh.weights[0]
            at.sync(sp, load_unit(sp, at, q_stack, k_stack, VB), rest, also=lambda u: weights.load_expert(sp, u))
            for e in range(2):
                weights.load_expert(sp, e)

        @block.gpsimd
        def _(pool):
            pool.memset(at.qtail[:, :], 0.0).then_inc(qtail_set, 1)
            pool.wait_ge(qtail_set, 1)
            pool.tensor_scalar(at.qtail[:, :], at.qtail[:, :], sh.query_tail[:, 0:1], None,
                               ALU.add).then_inc(qtail_set, 1)
            pool.wait_ge(qtail_set, 2)
            for g in range(UNITS):
                last = pool.memset(VB[:, g, :, :, HD:VW], 1.0)
            last.then_inc(v_ones, 1)
            sp_l.gpsimd(pool, 0, NKC + NQC)
            pool.wait_ge(wo_in, 32)
            pool.wait_ge(nm.xn_ready, B)
            for i in range(NT):
                last = pool.tensor_tensor(X[:, i, :], X[:, i, :], bo[:, :], ALU.add)
            last.then_inc(xb_ready, 1)
            projection.following.gpsimd(pool)

        @block.vector
        def _(dve):
            nm.vector(dve)
            dve.wait_ge(small_in, 16 * NSMALL)

            def masks():
                dve.wait_ge(mask_in, 16)
                dve.tensor_scalar(ind[:, :, :], maski, 0.0, None, ALU.not_equal).then_inc(ind_ready, 1)
                dve.wait_ge(ind_ready, 1)
                for b in range(B):
                    dve.tensor_scalar(ktail[:, b, :], ind[0:TAIL_ROWS, b, :], ktc[:, 0:1], ktc[:, 1:2], ALU.mult,
                                      ALU.add).then_inc(tail_ready, 1)

            for j, (what, n) in enumerate(outputs):
                dve.wait_ge(proj_done, j + 1)
                bank = PS[:, 4 + j % 4, :]
                if what == "v":
                    if n == 0:
                        dve.wait_ge(v_ones, 1)
                    b, kt = divmod(n, NK // P)
                    dve.tensor_tensor(VB[:, b * NG:(b + 1) * NG, kt, :, 0:HD],
                                      bank[:, 0:D].rearrange("p (g h c) -> p g h c", g=NG, h=GH),
                                      bv[:, :].rearrange("p (g h c) -> p g h c", g=NG, h=GH),
                                      ALU.add).then_inc(proj_taken, 1)
                    continue
                f = sp_l.buffer(dve, n)
                if n < NQC:
                    m = n % KD
                    dve.tensor_scalar(f, bank, bq[:, m:m + 1], None, ALU.add).then_inc(sp_l.f_ready, 1)
                else:
                    if n == NQC:
                        masks()
                    b, m, half = k_chunk(n)
                    dve.scalar_tensor_tensor(out=f, in0=bank, scalar=bk[:, m:m + 1],
                                             in1=ind[:, b, half * BANK:(half + 1) * BANK], op0=ALU.add,
                                             op1=ALU.mult).then_inc(sp_l.f_ready, 1)
                if j > 0 and outputs[j - 1][0] == "split":
                    sp_l.rest(dve, n - 1)
                if outputs[j + 1][0] == "v":
                    sp_l.rest(dve, n)
            dve.wait_ge(xb_ready, 1)
            at.vector(dve, meanwhile=lambda: projection.vector(dve, 0))
            projection.vector(dve, 1)

        @block.scalar
        def _(act):
            nm.scalar(act)
            sp_l.scalar(act, 0, NQC + NKC)
            act.wait_ge(sp_l.p2_ready, NQC + NKC)
            at.scalar(act)

        @block.tensor
        def _(pe):
            nm.tensor(pe)
            pe.wait_ge(small_in, 16 * NSMALL)

            for j, (what, n) in enumerate(outputs):
                bank = PS[:, 4 + j % 4, :]
                if j >= 4:
                    before, o = outputs[j - 4]
                    pe.wait_ge(proj_taken if before == "v" else sp_l.f_ready, o + 1)
                if what == "v":
                    if n == 0:
                        pe.wait_ge(wv_in, 16)
                    for k in range(KD):
                        last = pe.matmul(bank[:, 0:D], ctxT[:, k, n * P:(n + 1) * P], wv[:, k, :],
                                         start=(k == 0), stop=(k == KD - 1))
                elif n < NQC:
                    b, m = divmod(n, KD)
                    pe.wait_ge(nm.xT_ready, KD * (b + 1))
                    for k in range(KD):
                        last = pe.matmul(bank, wq[:, k, m * P:(m + 1) * P], XT[:, k, b * S:(b + 1) * S],
                                         start=(k == 0), stop=(k == KD - 1))
                else:
                    b, m, half = k_chunk(n)
                    pe.wait_ge(ctx_in[b], 16)
                    c0 = b * NK + half * BANK
                    for k in range(KD):
                        last = pe.matmul(bank, wk[:, k, m * P:(m + 1) * P], ctxT[:, k, c0:c0 + BANK],
                                         start=(k == 0), stop=(k == KD - 1))
                last.then_inc(proj_done, 1)
            pe.wait_ge(proj_taken, NV)
            at.tensor(pe, meanwhile=projection.tensor_meanwhile)
            projection.tensor(pe)


def shared_kv_stage(nc, ctx, sh, A):
    H, DK = 8, 128
    UN = B * H
    G = UN * TB
    LAG = 3
    STEPS = G + 2 * TB + LAG + 1

    def output_part(g):
        v, m = divmod(g - LAG, TB)
        return v - 1, m

    def projection_part(g):
        v, i = divmod(g - LAG - 1, TB)
        return v - 2, i

    PS, X, XN, XT = sh.PS, sh.X, sh.XN, sh.XT
    stage = ExitStack()

    def sb(name, shape, dt=F32):
        return stage.enter_context(nc.sbuf_tensor("s_" + name, shape, dt))

    def sem(name):
        return ctx.enter_context(nc.semaphore("s_" + name))

    nm = Norm(nc, ctx, sh, "s_n")
    following = NextStatistics(sh, sem)
    wq, wo = sb("wq", [P, H, KD, DK]), sb("wo", [P, H, D])
    wk, wv = sb("wk", [P, KD, DK]), sb("wv", [P, KD, DK])
    KTr, V = sb("KT", [P, T]), sb("V", [P, NT, DK])
    QT = [sb(f"QT{n}", [P, S]) for n in range(2)]
    NPB = LAG + 2
    Pr = [sb(f"Pr{n}", [P, S]) for n in range(NPB)]
    Pn = [sb(f"Pn{n}", [P, S]) for n in range(NPB)]
    mx, nmx, sm, rs = (sb(n, [P, NPB]) for n in ("mx", "nmx", "sm", "rs"))
    PT = [sb(f"PT{n}", [P, TB, S]) for n in range(2)]
    OT = [sb(f"OT{n}", [P, S]) for n in range(2)]

    wkv_in, wq_in, wo_in = sem("wkv_in"), sem("wq_in"), sem("wo_in")
    kv_mm, k_ready, v_ready = sem("kv_mm"), sem("k_ready"), sem("v_ready")
    q_mm, q_ready = sem("q_mm"), sem("q_ready")
    s_mm, mx_ready, nmx_ready, p_ready, rs_ready, pn_ready, t_mm, pt_ready = (
        sem(n) for n in ("s_mm", "mx_ready", "nmx_ready", "p_ready", "rs_ready", "pn_ready", "t_mm", "pt_ready"))
    o_mm, o_ready, y_mm, y_taken = sem("o_mm"), sem("o_ready"), sem("y_mm"), sem("y_taken")

    with stage, nc.Block() as block:

        @block.sync
        def _(sp):
            sp.dma_start(wk[:, :, :], A["s_wk"]).then_inc(wkv_in, 16)
            sp.dma_start(wv[:, :, :], A["s_wv"]).then_inc(wkv_in, 16)
            sp.dma_start(wq[:, :, :, :], A["s_wq"]).then_inc(wq_in, 16)
            sp.dma_start(wo[:, :, :], A["s_wo"]).then_inc(wo_in, 16)
            for e in range(ExpertWeights.EXP):
                sh.weights[1].load_expert(sp, e)

        @block.gpsimd
        def _(pool):
            for g in range(G):
                pool.wait_ge(rs_ready, g + 1)
                if g >= NPB:
                    pool.wait_ge(t_mm, g - NPB + 1)
                pool.tensor_scalar(Pn[g % NPB][:, :], Pr[g % NPB][:, :], rs[:, g % NPB:g % NPB + 1], None,
                                   ALU.mult).then_inc(pn_ready, 1)
            following.gpsimd(pool)

        @block.vector
        def _(dve):
            nm.vector(dve)
            for b in range(B):
                for i in range(0, TB, 2):
                    n = B + (b * TB + i) // 2
                    dve.wait_ge(kv_mm, n + 1)
                    dve.tensor_copy(V[:, b * TB + i:b * TB + i + 2, :],
                                    PS[:, 4 + n % 4, 0:2 * DK].rearrange("p (i c) -> p i c", i=2)).then_inc(v_ready, 1)

            def maximum(g):
                dve.wait_ge(s_mm, g + 1)
                if g >= NPB:
                    dve.wait_ge(p_ready, g - NPB + 1)
                dve.tensor_reduce(mx[:, g % NPB:g % NPB + 1], PS[:, g % 2, :], AX.X, ALU.max).then_inc(mx_ready, 1)
                dve.wait_ge(mx_ready, g + 1)
                dve.tensor_scalar(nmx[:, g % NPB:g % NPB + 1], mx[:, g % NPB:g % NPB + 1], -1.0, None,
                                  ALU.mult).then_inc(nmx_ready, 1)

            def inverse_sum(g):
                dve.wait_ge(p_ready, g + 1)
                if g >= NPB:
                    dve.wait_ge(pn_ready, g - NPB + 1)
                dve.reciprocal(rs[:, g % NPB:g % NPB + 1], sm[:, g % NPB:g % NPB + 1]).then_inc(rs_ready, 1)

            def take_transposes(g):
                n, qt = divmod(g, TB)
                dve.wait_ge(t_mm, g + 1)
                if n >= 2:
                    dve.wait_ge(o_mm, n - 1)
                dve.tensor_copy(PT[n % 2][:, :, qt * P:(qt + 1) * P],
                                PS[:, 2 + g % 2, :].rearrange("p (m q) -> p m q", m=TB)).then_inc(pt_ready, 1)

            def take_output(b):
                for bank in range(2):
                    dve.wait_ge(y_mm, (b + 1) * H)
                    i = b * TB + 2 * bank
                    dve.tensor_tensor(X[:, i:i + 2, :], X[:, i:i + 2, :],
                                      PS[:, 6 + bank, :].rearrange("p (i d) -> p i d", i=2),
                                      ALU.add).then_inc(y_taken, 1)
                for i in range(b * TB, (b + 1) * TB):
                    following.tile(dve, i, y_taken, 2 * b + 2)

            for g in range(G + LAG + 1):
                if g < G:
                    maximum(g)
                if 1 <= g <= G:
                    inverse_sum(g - 1)
                if g > LAG:
                    take_transposes(g - LAG - 1)
                if (g - LAG - 1) % TB == TB - 1 and (g - LAG - 1) // TB - 2 == H - 1:
                    take_output(0)
            take_output(1)

        @block.scalar
        def _(act):
            nm.scalar(act)
            for b in range(B):
                act.wait_ge(kv_mm, b + 1)
                act.activation(KTr[:, b * S:(b + 1) * S], PS[:, 4 + b, :], ACT.Copy).then_inc(k_ready, 1)

            def take_q(n):
                act.wait_ge(q_mm, n + 1)
                if n >= 2:
                    act.wait_ge(s_mm, (n - 1) * TB)
                act.activation(QT[n % 2][:, :], PS[:, 4, :], ACT.Copy).then_inc(q_ready, 1)

            def take_o(n):
                act.wait_ge(o_mm, n + 1)
                if n >= 2:
                    act.wait_ge(y_mm, n - 1)
                act.activation(OT[n % 2][:, :], PS[:, 5, :], ACT.Copy).then_inc(o_ready, 1)

            take_q(0)
            for g in range(STEPS):
                n, qt = divmod(g, TB)
                if g < G:
                    act.wait_ge(nmx_ready, g + 1)
                    if g >= NPB:
                        act.wait_ge(pn_ready, g - NPB + 1)
                    act.activation(Pr[g % NPB][:, :], PS[:, g % 2, :], ACT.Exp, bias=nmx[:, g % NPB:g % NPB + 1],
                                   accum_out=sm[:, g % NPB:g % NPB + 1]).then_inc(p_ready, 1)
                if qt == 1 and n + 1 < UN:
                    take_q(n + 1)
                v, m = output_part(g)
                if 0 <= v < UN and m == TB - 1:
                    take_o(v)

        @block.tensor
        def _(pe):
            nm.tensor(pe)
            pe.wait_ge(nm.xT_ready, KD * B)
            pe.wait_ge(wkv_in, 32)
            for b in range(B):
                for k in range(KD):
                    last = pe.matmul(PS[:, 4 + b, :], wk[:, k, :], XT[:, k, b * S:(b + 1) * S],
                                     start=(k == 0), stop=(k == KD - 1))
                last.then_inc(kv_mm, 1)
            for i in range(0, NT, 2):
                n = B + i // 2
                if n >= 4:
                    pe.wait_ge(k_ready, n - 3)
                for j in range(2):
                    for k in range(KD):
                        last = pe.matmul(PS[:, 4 + n % 4, j * DK:(j + 1) * DK], XT[:, k, (i + j) * P:(i + j + 1) * P],
                                         wv[:, k, :], start=(k == 0), stop=(k == KD - 1))
                last.then_inc(kv_mm, 1)
            pe.wait_ge(k_ready, B)
            pe.wait_ge(v_ready, NT // 2)
            pe.wait_ge(wq_in, 16)
            pe.wait_ge(wo_in, 16)

            def query_part(n, k):
                b, h = divmod(n, H)
                if n >= 1 and k == 0:
                    pe.wait_ge(q_ready, n)
                last = pe.matmul(PS[:, 4, :], wq[:, h, k, :], XT[:, k, b * S:(b + 1) * S],
                                 start=(k == 0), stop=(k == KD - 1))
                if k == KD - 1:
                    last.then_inc(q_mm, 1)

            def scores(g):
                n, qt = divmod(g, TB)
                b = n // H
                pe.wait_ge(q_ready, n + 1)
                if g >= 2:
                    pe.wait_ge(p_ready, g - 1)
                pe.matmul(PS[:, g % 2, :], QT[n % 2][:, qt * P:(qt + 1) * P], KTr[:, b * S:(b + 1) * S],
                          start=True, stop=True).then_inc(s_mm, 1)

            def transposes(g):
                pe.wait_ge(pn_ready, g + 1)
                if g >= 2:
                    pe.wait_ge(pt_ready, g - 1)
                for m in range(TB):
                    last = pe.transpose(PS[:, 2 + g % 2, m * P:(m + 1) * P], Pn[g % NPB][:, m * P:(m + 1) * P],
                                        sh.ident[:, :])
                last.then_inc(t_mm, 1)

            def output(n, m):
                if m == 0:
                    pe.wait_ge(pt_ready, (n + 1) * TB)
                    if n >= 1:
                        pe.wait_ge(o_ready, n)
                last = pe.matmul(PS[:, 5, :], V[:, n // H * TB + m, :], PT[n % 2][:, m, :], start=(m == 0),
                                 stop=(m == TB - 1))
                if m == TB - 1:
                    last.then_inc(o_mm, 1)

            def project(n, i):
                b, h = divmod(n, H)
                if i == 0:
                    pe.wait_ge(o_ready, n + 1)
                    if h == 0 and b > 0:
                        pe.wait_ge(y_taken, 2 * b)
                last = pe.matmul(PS[:, 6 + i // 2, (i % 2) * D:(i % 2 + 1) * D], OT[n % 2][:, i * P:(i + 1) * P],
                                 wo[:, h, :], start=(h == 0 and i % 2 == 0), stop=(h == H - 1 and i % 2 == 1),
                                 skip_group_check=True)
                if i == TB - 1:
                    last.then_inc(y_mm, 1)

            for k in range(KD):
                query_part(0, k)
            for g in range(STEPS):
                n, qt = divmod(g, TB)
                if g < G:
                    scores(g)
                if qt < KD and n + 1 < UN:
                    query_part(n + 1, qt)
                if LAG <= g < G + LAG:
                    transposes(g - LAG)
                v, m = output_part(g)
                if 0 <= v < UN:
                    output(v, m)
                v, i = projection_part(g)
                if 0 <= v < UN:
                    project(v, i)


class Context:

    def __init__(self, nc, ctx, A):
        def sb(n, shape):
            return ctx.enter_context(nc.sbuf_tensor("ctx_" + n, shape, F32))

        NK = A["h_ctxT"].shape[2]
        self.NKT = NK // P
        self.ctxT = sb("T", [P, KD, NK])
        self.w = sb("w", [P, KD, 2 * HD])
        self.kv = sb("kv", [P, self.NKT, 2 * HD])
        self.rows = nc.dram_tensor("ctx_rows", [NK, 2 * HD], F32, kind="Internal").ap()
        self.loaded, self.mm, self.ready, self.stored = (
            ctx.enter_context(nc.semaphore("ctx_" + n)) for n in ("loaded", "mm", "ready", "stored"))
        self.A = A

    def load(self, sp):
        sp.dma_start(self.w[:, :, :], self.A["h_wkv"]).then_inc(self.loaded, 16)
        sp.dma_start(self.ctxT[:, :, :], self.A["h_ctxT"]).then_inc(self.loaded, 16)

    def tensor(self, pe, bank):
        pe.wait_ge(self.loaded, 32)
        for t in range(self.NKT):
            for k in range(KD):
                last = pe.matmul(bank[:, t * 2 * HD:(t + 1) * 2 * HD], self.ctxT[:, k, t * P:(t + 1) * P],
                                 self.w[:, k, :], start=(k == 0), stop=(k == KD - 1), skip_group_check=True)
        last.then_inc(self.mm, 1)

    def vector(self, dve, bank):
        dve.wait_ge(self.mm, 1)
        dve.tensor_copy(self.kv[:, :, :], bank.rearrange("p (t c) -> p t c", t=self.NKT)).then_inc(self.ready, 1)

    def store(self, sp):
        sp.wait_ge(self.ready, 1)
        sp.dma_start(self.rows.rearrange("(t p) c -> p t c", p=P), self.kv[:, :, :]).then_inc(self.stored, 16)


def hard_cross_stage(nc, ctx, sh, A):
    NK = 1024
    PS, X, XN, XT = sh.PS, sh.X, sh.XN, sh.XT
    stage = ExitStack()

    def sb(name, shape, dt=F32):
        return stage.enter_context(nc.sbuf_tensor("h_" + name, shape, dt))

    def sem(name):
        return ctx.enter_context(nc.semaphore("h_" + name))

    nm = Norm(nc, ctx, sh, "h_n")
    wc = sb("wc", [P, KD, D])
    VB = sb("VB", [P, UNITS, TB, 1, VW])
    at = Attention(nc, ctx, stage, PS, "h_a", S, 1, sh.ident, sh.identb)
    ctxT = sh.context.ctxT
    wq = sb("wq", [P, KD, D])
    QF = sb("QF", [P, KD, T])
    QP = [sb(f"QP{n}", [P, KD, T], BF16) for n in range(3)]
    KP = [sb(f"KP{n}", [HD, B, S], BF16) for n in range(3)]
    ktail = sb("ktail", [TAIL_ROWS, S], BF16)
    ktc = sb("ktc", [TAIL_ROWS, 1])
    top = sb("top", [P, NT, 8])
    idx = sb("idx", [P, NT, 8], U32)
    row = sb("row", [P, NT], U32)
    GM = sb("GM", [P, NT, 2 * HD])
    q_stack = nc.dram_tensor("h_q_stack", [UNITS, Q_DRAM, GH, S], BF16, kind="Internal").ap()
    k_stack = nc.dram_tensor("h_k_stack", [UNITS, K_DRAM, 1, S], BF16, kind="Internal").ap()

    small_in, w_in, wc_in = sem("small_in"), sem("w_in"), sem("wc_in")
    qf_mm, qf_ready = sem("qf_mm"), sem("qf_ready")
    sc_mm, top_ready, idx_ready, row_ready = (sem(n) for n in ("sc_mm", "top_ready", "idx_ready", "row_ready"))
    kT_mm, v_ones, v_ready, qtail_set = (sem(n) for n in ("kT_mm", "v_ones", "v_ready", "qtail_set"))
    tail_zero, tail_ready, tail_stored = (sem(n) for n in ("tail_zero", "tail_ready", "tail_stored"))
    k_stored = [sem(f"k_stored{b}") for b in range(B)]
    q_stored = [sem(f"q_stored{b}") for b in range(B)]
    found = [sem(f"found{b}") for b in range(B)]
    NQC = B * KD

    def dst(n, part):
        if n < NQC:
            b, m = divmod(n, KD)
            return QP[part][:, m, b * S:(b + 1) * S]
        return KP[part][:, n - NQC, :]

    LATER = 2
    spl = Splitter(nc, ctx, at.E[1][:, :, :], "h_s", dst, [P] * NQC + [HD] * B, NQC + B)
    projection = OutputProjection(at, sh, sem, wc, wc_in, 1)

    with stage, nc.Block() as block:

        @block.sync
        def _(sp):
            sp.dma_start(ktc[:, :], A["h_ktc"]).then_inc(small_in, 16)
            sp.dma_start(wq[:, :, :], A["h_wq"]).then_inc(w_in, 16)
            sp.dma_start(wc[:, :, :], A["h_wc"]).then_inc(wc_in, 16)
            sp.wait_ge(qtail_set, 2)
            store_query_tails(sp, q_stack, at.qtail, tail_stored)

            def spread(rows, src):
                units = rows[:, :, 0, :].rearrange("u r n -> r u n")
                return units, src.unsqueeze(1).to_broadcast([src.shape[0], rows.shape[0], S])

            sp.wait_ge(tail_ready, 1)
            d, src = spread(k_stack[:, K_DRAM - TAIL_ROWS:, :, :], ktail[:, :])
            sp.dma_start(d, src).then_inc(tail_stored, 16)
            for b in range(B):
                sp.wait_ge(spl.p2_ready, (b + 1) * KD)
                store_parts(sp, q_stack, Q_ROWS, lambda part: QP[part][:, :, b * S:(b + 1) * S], b, q_stored[b])

            def store_k(b):
                sp.wait_ge(spl.p2_ready, NQC + b + 1)
                for slot, part in enumerate(K_ROWS):
                    d, src = spread(k_stack[b * NG:(b + 1) * NG, slot * HD:(slot + 1) * HD, :, :], KP[part][:, b, :])
                    sp.dma_start(d, src).then_inc(k_stored[b], 16)

            def rest():
                store_k(1)
                sp.wait_ge(k_stored[1], 16 * len(K_ROWS))
                sp.wait_ge(q_stored[1], 16 * Q_STORES)
                sp.wait_ge(v_ready, B)

            store_k(0)
            sp.wait_ge(tail_stored, 16 * 2)
            sp.wait_ge(k_stored[0], 16 * len(K_ROWS))
            sp.wait_ge(q_stored[0], 16 * Q_STORES)
            sp.wait_ge(v_ready, 1)
            at.sync(sp, load_unit(sp, at, q_stack, k_stack, VB), rest)

        @block.gpsimd
        def _(pool):
            pool.memset(VB[:, :, :, :, :], 1.0).then_inc(v_ones, 1)
            pool.memset(at.qtail[:, :], 0.0).then_inc(qtail_set, 1)
            pool.wait_ge(qtail_set, 1)
            pool.wait_ge(v_ones, 1)
            pool.tensor_scalar(at.qtail[:, :], at.qtail[:, :], sh.query_tail[:, 0:1], None,
                               ALU.add).then_inc(qtail_set, 1)
            pool.memset(ktail[:, :], 0.0).then_inc(tail_zero, 1)
            pool.wait_ge(small_in, 16)
            pool.wait_ge(tail_zero, 1)
            pool.wait_ge(qtail_set, 2)
            pool.tensor_scalar(ktail[:, :], ktail[:, :], ktc[:, 0:1], None, ALU.add).then_inc(tail_ready, 1)
            pool.wait_ge(tail_ready, 1)
            spl.gpsimd(pool, 0, NQC)
            pool.wait_ge(sh.context.stored, 16)

            def find(b):
                for i in range(b * TB, (b + 1) * TB):
                    pool.wait_ge(row_ready, i + 1)
                    pool.indirect_dma_start(out=GM[:, i, :], out_offset=None, in_=sh.context.rows,
                                            in_offset=bass.IndirectOffsetOnAxis(ap=row[:, i:i + 1], axis=0),
                                            ).then_inc(found[b], 16)

            find(0)
            spl.gpsimd(pool, NQC, NQC + 1)
            find(1)
            spl.gpsimd(pool, NQC + 1, NQC + 2)
            projection.following.gpsimd(pool)

        @block.vector
        def _(dve):
            nm.vector(dve)
            for n in range(NQC):
                dve.wait_ge(qf_mm, n + 1)
                dve.tensor_copy(spl.buffer(dve, n), PS[:, 4 + n, :]).then_inc(spl.f_ready, 1)
                if n > 0:
                    spl.rest(dve, n - 1)
            spl.rest(dve, NQC - 1)

            def best(i):
                b = i // TB
                bank = 2 * (i % 2)
                dve.wait_ge(sc_mm, i + 1)
                dve.max(top[:, i, :], PS[:, bank:bank + 2, :]).then_inc(top_ready, 1)
                dve.wait_ge(top_ready, i + 1)
                dve.max_index(idx[:, i, :], top[:, i, :],
                              PS[:, bank:bank + 2, :].rearrange("p h n -> p (h n)")).then_inc(idx_ready, 1)
                dve.wait_ge(idx_ready, i + 1)
                dve.tensor_scalar(row[:, i:i + 1], idx[:, i, 0:1], float(b * NK), None, ALU.add).then_inc(row_ready, 1)

            def take_found(b):
                dve.wait_ge(kT_mm, b + 1)
                dve.tensor_copy(spl.buffer(dve, NQC + b), PS[0:HD, 7, :]).then_inc(spl.f_ready, 1)
                for g in range(NG):
                    last = dve.tensor_copy(VB[:, b * NG + g, :, 0, 0:HD], GM[:, b * TB:(b + 1) * TB, HD:2 * HD])
                last.then_inc(v_ready, 1)
                spl.rest(dve, NQC + b)

            for i in range(TB + LATER):
                best(i)
            dve.wait_ge(v_ones, 1)
            take_found(0)
            for i in range(TB + LATER, NT):
                best(i)
            at.vector(dve, between=lambda: take_found(1), meanwhile=lambda: projection.vector(dve, 0))
            projection.vector(dve, 1)

        @block.scalar
        def _(act):
            nm.scalar(act)
            for n in range(NQC):
                b, m = divmod(n, KD)
                act.wait_ge(spl.f_ready, n + 1)
                act.activation(QF[:, m, b * S:(b + 1) * S], spl.F[n % 2], ACT.Copy).then_inc(qf_ready, 1)
                spl.scalar(act, n, n + 1)
            spl.scalar(act, NQC, NQC + 1)
            spl.scalar(act, NQC + 1, NQC + 2)
            act.wait_ge(spl.p2_ready, NQC + B)
            at.scalar(act)

        @block.tensor
        def _(pe):
            nm.tensor(pe)
            pe.wait_ge(w_in, 16)
            pe.wait_ge(nm.xT_ready, KD * B)
            for n in range(NQC):
                b, m = divmod(n, KD)
                for k in range(KD):
                    last = pe.matmul(PS[:, 4 + n, :], wq[:, k, m * P:(m + 1) * P], XT[:, k, b * S:(b + 1) * S],
                                     start=(k == 0), stop=(k == KD - 1))
                last.then_inc(qf_mm, 1)

            def context_scores(i):
                b = i // TB
                pe.wait_ge(qf_ready, KD * (b + 1))
                if i >= 2:
                    pe.wait_ge(idx_ready, i - 1)
                for half in range(2):
                    for k in range(KD):
                        c0 = b * NK + half * BANK
                        last = pe.matmul(PS[:, 2 * (i % 2) + half, :], QF[:, k, i * P:(i + 1) * P],
                                         ctxT[:, k, c0:c0 + BANK], start=(k == 0), stop=(k == KD - 1))
                last.then_inc(sc_mm, 1)

            def found_keys(b):
                pe.wait_ge(found[b], 16 * TB)
                pe.wait_ge(spl.f_ready, NQC + b)
                for i in range(TB):
                    last = pe.transpose(PS[0:HD, 7, i * P:(i + 1) * P], GM[:, b * TB + i, 0:HD], sh.ident[:, :])
                last.then_inc(kT_mm, 1)

            for i in range(TB + LATER):
                context_scores(i)
            found_keys(0)
            for i in range(TB + LATER, NT):
                context_scores(i)
            pe.wait_ge(idx_ready, NT)

            def between():
                found_keys(1)
                pe.wait_ge(spl.f_ready, NQC + B)

            at.tensor(pe, between=between, meanwhile=projection.tensor_meanwhile)
            projection.tensor(pe)


def experts_stage(nc, ctx, sh, A, layer):
    first = layer == 0
    weights = sh.weights[layer]
    EXP, F, KF, pre = weights.EXP, weights.F, weights.KF, weights.pre
    NB1 = F // BANK
    PS, X, XN, XT = sh.PS, sh.X, sh.XN, sh.XT
    stage = ExitStack()

    def sb(name, shape, dt=F32):
        return stage.enter_context(nc.sbuf_tensor(pre + name, shape, dt))

    def sem(name):
        return ctx.enter_context(nc.semaphore(pre + name))

    nm = Norm(nc, ctx, sh, pre + "n")
    wr, br = sb("wr", [P, KD, EXP]), sb("br", [P, EXP])
    following = NextStatistics(sh, sem) if first else None
    W1 = weights.W1
    W2 = weights.W2 if first else sb("W2", [P, KF, D])
    B1 = sb("B1", [P, EXP * F])
    B2 = sb("B2", [P, (EXP if first else 1) * D])
    tri, ones = sb("tri", [P, P]), sb("ones", [P, P])
    iota = sb("iota", [P, 16])
    iotaP = sb("iotaP", [P, EXP])
    lg, ex = sb("lg", [P, NT, EXP]), sb("ex", [P, NT, EXP])
    prob, den = sb("prob", [P, NT]), sb("den", [P, NT])
    top, idx = sb("top", [P, NT, 8]), sb("idx", [P, NT, 8], U32)
    idxf = sb("idxf", [P, NT])
    OH = sb("OH", [P, NT, EXP])
    before = sb("before", [P, NT + 1, EXP])
    cmp_ = sb("cmp", [P, EXP, EXP])
    tiles, upto, base = sb("tiles", [P, EXP]), sb("upto", [P, EXP]), sb("base", [P, EXP])
    pos = sb("pos", [P, NT, EXP])
    slotf, slot = sb("slotf", [P, NT]), sb("slot", [P, NT], U32)
    cmps = sb("cmps", [P, 16, EXP])
    exf, ext = sb("exf", [P, 16]), sb("ext", [P, 16], I32)
    gb = None if first else sb("gb", [P, 2, D])
    Xs = [sb(f"Xs{n}", [P, D]) for n in range(2)]
    XsT = [sb(f"XsT{n}", [P, KD, P]) for n in range(2)]
    Hs = [sb(f"H{n}", [P, F]) for n in range(2)]
    HT = [sb(f"HT{n}", [P, KF, P]) for n in range(2)]
    Ys = [sb(f"Y{n}", [P, D]) for n in range(2)]
    YG = sb("YG", [P, NT, D])
    xs = sh.xs[layer]
    ys = nc.dram_tensor(pre + "ys", [SLOTS, D], F32, kind="Internal").ap()

    small_in, b_in, w2_in, ones_set = (sem(n) for n in ("small_in", "b_in", "w2_in", "ones_set"))
    own, lg_mm, lg_ready, ex_ready, oh_ready, rank_mm, slot_ready, ext_ready = (
        sem(n) for n in ("own", "lg_mm", "lg_ready", "ex_ready", "oh_ready", "rank_mm", "slot_ready", "ext_ready"))
    scattered = sem("scattered")
    xs_in = [sem(f"xs_in{n}") for n in range(2)]
    xsT_mm, xsT_ready, w1_mm, h_sum, h_ready, hT_mm, hT_ready, w2_mm, y_ready = (
        sem(n) for n in ("xsT_mm", "xsT_ready", "w1_mm", "h_sum", "h_ready", "hT_mm", "hT_ready", "w2_mm",
                         "y_ready"))
    gathered = [sem(f"gathered{b}") for b in range(B)]
    stored = [sem(f"stored{n}") for n in range(2)]
    xb_ready, var2_ready, rstd2_ready, eps2_ready, out_ready = (
        sem(n) for n in ("xb_ready", "var2_ready", "rstd2_ready", "eps2_ready", "out_ready"))
    NSMALL = 5

    def tiles_loop(eng, step):
        for t in range(2):
            step(t, t)
        with eng.Fori(0, (SLOT_TILES - 5) // 2) as i:
            step(i * 2 + 2, 0)
            step(i * 2 + 3, 1)
        for t in range(SLOT_TILES - 3, SLOT_TILES):
            step(t, t % 2)

    def known_below(t, n):
        return isinstance(t, int) and t < n

    def rows(t):
        return bass.ds(t * P, P)

    with stage, nc.Block() as block:

        @block.sync
        def _(sp):
            small = [(wr, pre + "wr"), (tri, "tris"), (iota, "iota"), (iotaP, "iotaP")]
            small += [(br, pre + "br")] if first else []
            for d, s in small:
                sp.dma_start(d[tuple(slice(None) for _ in d.shape)], A[s]).then_inc(small_in, 16)
            sp.dma_start(B1[:, :], A[pre + "b1"].to_broadcast([P, EXP * F])).then_inc(b_in, 16)
            sp.dma_start(B2[:, :], A[pre + "b2"]).then_inc(b_in, 16)
            if not first:
                sp.dma_start(W2[:, :, :], A["g_w2"]).then_inc(w2_in, 16)
            if first:
                sh.context.load(sp)
            sp.wait_ge(scattered, 16 * NT)

            def load(t, p):
                if not known_below(t, 2):
                    sp.wait_ge(xsT_mm, t - 1)
                sp.dma_start(Xs[p][:, :], xs[rows(t), :]).then_inc(xs_in[p], 16)

            def step(t, p):
                if not (isinstance(t, int) and t + 2 >= SLOT_TILES):
                    load(t + 2, p)
                sp.wait_ge(y_ready, t + 1)
                sp.dma_start(ys[rows(t), :], Ys[p][:, :]).then_inc(stored[p], 16)

            load(0, 0)
            load(1, 1)
            tiles_loop(sp, step)
            if first:
                sh.context.store(sp)
            for p in range(2):
                sp.wait_ge(stored[p], 16 * ((SLOT_TILES + 1 - p) // 2))
            if not first:
                for b in range(B):
                    tiles = slice(b * TB, (b + 1) * TB)
                    sp.wait_ge(out_ready, b + 1)
                    sp.dma_start(sh.out[:, tiles, :], X[:, tiles, :]).then_inc(sh.out_stored, 16)
                sp.wait_ge(sh.out_stored, 16 * B)

        @block.gpsimd
        def _(pool):
            pool.memset(ones[:, :], 1.0).then_inc(ones_set, 1)
            pool.wait_ge(nm.xn_ready, B)
            pool.wait_ge(sh.zeroed, 16 * len(sh.xs))
            pool.wait_ge(slot_ready, 1)
            for i in range(NT):
                pool.indirect_dma_start(out=xs, out_offset=bass.IndirectOffsetOnAxis(ap=slot[:, i:i + 1], axis=0),
                                        in_=XN[:, i, :], in_offset=None).then_inc(scattered, 16)
            if not first:
                pool.wait_ge(scattered, 16 * NT)
                pool.wait_ge(nm.xT_done, KD * B)
                pool.wait_ge(b_in, 32)
                for i in range(NT):
                    last = pool.tensor_tensor(XN[:, i, :], XN[:, i, :], B2[:, :], ALU.add)
                last.then_inc(xb_ready, 1)
                pool.wait_ge(small_in, 16 * NSMALL)
                pool.wait_ge(nm.xn_ready, B)
                for i in range(NT):
                    last = pool.tensor_tensor(X[:, i, :], X[:, i, :], gb[:, 1, :], ALU.add)
                last.then_inc(xb_ready, 1)
            for p in range(2):
                pool.wait_ge(stored[p], 16 * ((SLOT_TILES + 1 - p) // 2))
            for i in range(NT):
                pool.indirect_dma_start(out=YG[:, i, :], out_offset=None, in_=ys,
                                        in_offset=bass.IndirectOffsetOnAxis(ap=slot[:, i:i + 1], axis=0),
                                        ).then_inc(gathered[i // TB], 16)
            if not first:
                inverse_deviations_gpsimd(pool, sh.mhalf, sh.mv, sh.rstd, 1e-12, var2_ready, eps2_ready, rstd2_ready)
            else:
                following.gpsimd(pool)

        @block.vector
        def _(dve):
            nm.vector(dve)
            c = Chain(dve, own)
            dve.wait_ge(small_in, 16 * NSMALL)
            dve.wait_ge(lg_mm, 1)
            src = PS[:, 4, 0:NT * EXP].rearrange("p (i e) -> p i e", i=NT)
            if first:
                c.link(dve.tensor_tensor(lg[:, :, :], src, br[:, :].unsqueeze(1).to_broadcast([P, NT, EXP]), ALU.add))
            else:
                c.link(dve.tensor_copy(lg[:, :, :], src))
            for i in range(NT):
                last = dve.max(top[:, i, :], lg[:, i, :])
            c.link(last)
            for i in range(NT):
                last = dve.max_index(idx[:, i, :], top[:, i, :], lg[:, i, :])
            c.link(last)
            c.link(dve.tensor_copy(idxf[:, :], idx[:, :, 0]))
            dve.tensor_tensor(OH[:, :, :], iota[:, 0:EXP].unsqueeze(1).to_broadcast([P, NT, EXP]),
                              idxf[:, :].unsqueeze(2).to_broadcast([P, NT, EXP]), ALU.is_equal).then_inc(oh_ready, 1)
            if first:
                dve.tensor_tensor(lg[:, :, :], lg[:, :, :], top[:, :, 0:1].to_broadcast([P, NT, EXP]),
                                  ALU.subtract).then_inc(lg_ready, 1)
            c.link(dve.memset(before[:, 0, :], 0.0))
            dve.wait_ge(rank_mm, 1)
            NE = NT * EXP
            for i in range(NT):
                c.link(dve.tensor_tensor(before[:, i + 1, :], before[:, i, :],
                                         PS[:, 5, NE + i * EXP:NE + (i + 1) * EXP], ALU.add))
            c.link(dve.tensor_tensor(cmp_[:, :, :], before[:, NT, :].unsqueeze(2).to_broadcast([P, EXP, EXP]),
                                     iotaP[:, :].unsqueeze(1).to_broadcast([P, EXP, EXP]), ALU.is_gt))
            c.link(dve.tensor_reduce(tiles[:, :], cmp_[:, :, :], AX.X, ALU.add))
            dve.wait_ge(ones_set, 1)
            c.link(dve.tensor_tensor_scan(upto[:, :], ones[:, 0:EXP], tiles[:, :], 0.0, ALU.mult, ALU.add))
            c.link(dve.tensor_tensor(base[:, :], upto[:, :], tiles[:, :], ALU.subtract))
            c.link(dve.tensor_tensor(pos[:, :, :], before[:, 0:NT, :],
                                     PS[:, 5, 0:NE].rearrange("p (i e) -> p i e", i=NT), ALU.add))
            c.link(dve.scalar_tensor_tensor(out=pos[:, :, :], in0=base[:, :].unsqueeze(1).to_broadcast([P, NT, EXP]),
                                            scalar=float(P), in1=pos[:, :, :], op0=ALU.mult, op1=ALU.add))
            c.link(dve.tensor_tensor(pos[:, :, :], pos[:, :, :], OH[:, :, :], ALU.mult))
            c.link(dve.tensor_reduce(slotf[:, :], pos[:, :, :], AX.X, ALU.add))
            dve.tensor_copy(slot[:, :], slotf[:, :]).then_inc(slot_ready, 1)
            c.link(dve.tensor_tensor(cmps[:, :, :], upto[:, :].unsqueeze(1).to_broadcast([P, 16, EXP]),
                                     iota[:, :].unsqueeze(2).to_broadcast([P, 16, EXP]), ALU.is_le))
            c.link(dve.tensor_reduce(exf[:, :], cmps[:, :, :], AX.X, ALU.add))
            c.link(dve.tensor_scalar(exf[:, :], exf[:, :], EXP - 1.0, None, ALU.min))
            dve.tensor_copy(ext[:, :], exf[:, :]).then_inc(ext_ready, 1)
            if first:
                dve.wait_ge(ex_ready, 1)
                c.link(dve.tensor_reduce(den[:, :], ex[:, :, :], AX.X, ALU.add))
                c.link(dve.reciprocal(prob[:, :], den[:, :]))

            dve.wait_ge(ext_ready, 1)
            if first:
                sh.context.vector(dve, PS[:, 7, :])
            dve.wait_ge(b_in, 32)

            def hidden(t, p):
                e = dve.value_load(ext[0:1, bass.ds(t, 1)], min_val=0, max_val=EXP - 1)
                dve.wait_ge(w1_mm, t + 1)
                if not known_below(t, 2):
                    dve.wait_ge(hT_mm, t - 1)
                b0 = 1 + p * NB1
                dve.tensor_tensor(Hs[p][:, :], PS[:, b0:b0 + NB1, :].rearrange("p h n -> p (h n)"),
                                  B1[:, bass.ds(e * F, F)], ALU.add).then_inc(h_sum, 1)

            def result(t, p):
                if first:
                    e = dve.value_load(ext[0:1, bass.ds(t, 1)], min_val=0, max_val=EXP - 1)
                dve.wait_ge(w2_mm, t + 1)
                if not known_below(t, 2):
                    dve.wait_ge(stored[p], (t - p) * 8)
                if first:
                    last = dve.tensor_tensor(Ys[p][:, :], PS[:, 7, 0:D], B2[:, bass.ds(e * D, D)], ALU.add)
                else:
                    last = dve.tensor_copy(Ys[p][:, :], PS[:, 7, 0:D])
                last.then_inc(y_ready, 1)

            def step(t, p):
                if not (isinstance(t, int) and t + 1 >= SLOT_TILES):
                    hidden(t + 1, 1 - p)
                result(t, p)

            hidden(0, 0)
            tiles_loop(dve, step)
            if first:
                for i in range(NT):
                    dve.wait_ge(gathered[i // TB], 16 * TB)
                    dve.scalar_tensor_tensor(out=X[:, i, :], in0=YG[:, i, :], scalar=prob[:, i:i + 1],
                                             in1=X[:, i, :], op0=ALU.mult, op1=ALU.add).then_inc(xb_ready, 1)
                    following.tile(dve, i, xb_ready, i + 1)
            else:
                dve.wait_ge(xb_ready, 2)
                for b in range(B):
                    batch = range(b * TB, (b + 1) * TB)
                    dve.wait_ge(gathered[b], 16 * TB)
                    for i in batch:
                        last = dve.tensor_tensor(XN[:, i, :], XN[:, i, :], YG[:, i, :], ALU.add)
                    c.link(last)
                    for i in batch:
                        last = dve.bn_stats(sh.st6[:, i, :], XN[:, i, :])
                    c.link(last)
                    for i in batch:
                        last = dve.bn_aggr(sh.mv[:, i, :], sh.st6[:, i, :])
                    last.then_inc(var2_ready, 1)
                dve.wait_ge(var2_ready, B)
                for b in range(B):
                    batch = range(b * TB, (b + 1) * TB)
                    for i in batch:
                        last = dve.scalar_tensor_tensor(out=YG[:, i, :], in0=XN[:, i, :], scalar=sh.mv[:, i, 0:1],
                                                        in1=gb[:, 0, :], op0=ALU.subtract, op1=ALU.mult)
                    c.link(last)
                    dve.wait_ge(rstd2_ready, b + 1)
                    for i in batch:
                        last = dve.scalar_tensor_tensor(out=X[:, i, :], in0=YG[:, i, :], scalar=sh.rstd[:, i:i + 1],
                                                        in1=X[:, i, :], op0=ALU.mult, op1=ALU.add)
                    last.then_inc(out_ready, 1)

        @block.scalar
        def _(act):
            if not first:
                act.dma_start(gb[:, :, :], A["g_gb"]).then_inc(small_in, 16)
            nm.scalar(act)
            if first:
                act.wait_ge(lg_ready, 1)
                act.activation(ex[:, :, :], lg[:, :, :], ACT.Exp).then_inc(ex_ready, 1)

            def take_x(t, p):
                act.wait_ge(xsT_mm, t + 1)
                if not known_below(t, 2):
                    act.wait_ge(w1_mm, t - 1)
                act.activation(XsT[p][:, :, :], PS[:, 0, 0:D].rearrange("p (k n) -> p k n", k=KD),
                               ACT.Copy).then_inc(xsT_ready, 1)

            def gelu(t, p):
                act.wait_ge(h_sum, t + 1)
                act.activation(Hs[p][:, :], Hs[p][:, :], ACT.Gelu).then_inc(h_ready, 1)

            def take_h(t, p):
                act.wait_ge(hT_mm, t + 1)
                if not known_below(t, 2):
                    act.wait_ge(w2_mm, t - 1)
                b0, n = (5 + p, 1) if first else (5, 2)
                act.activation(HT[p][:, :, :].rearrange("p k n -> p (k n)"),
                               PS[:, b0:b0 + n, :].rearrange("p h n -> p (h n)"),
                               ACT.Relu if first else ACT.Copy).then_inc(hT_ready, 1)

            def step(t, p):
                take_h(t, p)
                if not first and not (isinstance(t, int) and t + 1 >= SLOT_TILES):
                    gelu(t + 1, 1 - p)
                if not (isinstance(t, int) and t + 2 >= SLOT_TILES):
                    take_x(t + 2, p)

            take_x(0, 0)
            take_x(1, 1)
            if not first:
                gelu(0, 0)
            tiles_loop(act, step)

        @block.tensor
        def _(pe):
            nm.tensor(pe)
            pe.wait_ge(small_in, 16 * NSMALL)
            pe.wait_ge(nm.xT_ready, KD * B)
            for i in range(NT):
                for k in range(KD):
                    last = pe.matmul(PS[:, 4, i * EXP:(i + 1) * EXP], XT[:, k, i * P:(i + 1) * P], wr[:, k, :],
                                     start=(k == 0), stop=(k == KD - 1), skip_group_check=True)
            last.then_inc(lg_mm, 1)
            pe.wait_ge(oh_ready, 1)
            pe.wait_ge(ones_set, 1)
            hot = OH[:, :, :].rearrange("p i e -> p (i e)")
            pe.matmul(PS[:, 5, 0:NT * EXP], tri[:, :], hot, start=True, stop=True)
            pe.matmul(PS[:, 5, NT * EXP:2 * NT * EXP], ones[:, :], hot, start=True, stop=True).then_inc(rank_mm, 1)
            pe.wait_ge(ext_ready, 1)
            if first:
                sh.context.tensor(pe, PS[:, 7, :])
            pe.wait_ge(weights.loaded, 16 * weights.loads)
            if not first:
                pe.wait_ge(w2_in, 16)

            def transpose_x(t, p):
                pe.wait_ge(xs_in[p], (t - p) * 8 + 16)
                if not known_below(t, 1):
                    pe.wait_ge(xsT_ready, t)
                for k in range(KD):
                    last = pe.transpose(PS[:, 0, k * P:(k + 1) * P], Xs[p][:, k * P:(k + 1) * P], sh.ident[:, :])
                last.then_inc(xsT_mm, 1)

            def up(t, p):
                e = pe.value_load(ext[0:1, bass.ds(t, 1)], min_val=0, max_val=EXP - 1)
                pe.wait_ge(xsT_ready, t + 1)
                if not known_below(t, 2):
                    pe.wait_ge(h_sum, t - 1)
                for half in range(NB1):
                    for k in range(KD):
                        last = pe.matmul(PS[:, 1 + p * NB1 + half, :], XsT[p][:, k, :],
                                         W1[:, k, bass.ds(e * F + half * BANK, BANK)],
                                         start=(k == 0), stop=(k == KD - 1))
                last.then_inc(w1_mm, 1)

            def transpose_h(t, p):
                pe.wait_ge(h_sum if first else h_ready, t + 1)
                if first:
                    if not known_below(t, 2):
                        pe.wait_ge(hT_ready, t - 1)
                elif not known_below(t, 1):
                    pe.wait_ge(hT_ready, t)
                for k in range(KF):
                    bank = 5 + p if first else 5 + k // TB
                    last = pe.transpose(PS[:, bank, k % TB * P:(k % TB + 1) * P], Hs[p][:, k * P:(k + 1) * P],
                                        sh.ident[:, :])
                last.then_inc(hT_mm, 1)

            def down(t, p):
                e = pe.value_load(ext[0:1, bass.ds(t, 1)], min_val=0, max_val=EXP - 1) if first else 0
                pe.wait_ge(hT_ready, t + 1)
                if not known_below(t, 1):
                    pe.wait_ge(y_ready, t)
                elif first:
                    pe.wait_ge(sh.context.ready, 1)
                for k in range(KF):
                    last = pe.matmul(PS[:, 7, 0:D], HT[p][:, k, :], W2[:, k, bass.ds(e * D, D)],
                                     start=(k == 0), stop=(k == KF - 1))
                last.then_inc(w2_mm, 1)

            def step(t, p):
                transpose_h(t, p)
                if not (isinstance(t, int) and t + 1 >= SLOT_TILES):
                    up(t + 1, 1 - p)
                down(t, p)
                if not (isinstance(t, int) and t + 2 >= SLOT_TILES):
                    transpose_x(t + 2, p)

            transpose_x(0, 0)
            transpose_x(1, 1)
            up(0, 0)
            tiles_loop(pe, step)


def experts0_stage(nc, ctx, sh, A):
    sh.context = Context(nc, sh.held, A)
    experts_stage(nc, ctx, sh, A, 0)


def experts1_stage(nc, ctx, sh, A):
    sh.held.close()
    experts_stage(nc, ctx, sh, A, 1)


def layouts(np, I):
    def ktile(w):
        return w.reshape(-1, P, w.shape[-1]).transpose(1, 0, 2)

    def cols(v):
        return v.reshape(-1, P).T

    def dim_major(w):
        return w.reshape(*w.shape[:-1], NG, GH, HD).swapaxes(-1, -2).reshape(w.shape)

    def rows(v):
        return np.broadcast_to(v, (P, v.shape[-1]))

    A = {}
    A["x"] = I["x"].reshape(NT, P, D).transpose(1, 0, 2)
    A["ident"] = np.eye(P, dtype=np.float32)
    A["tri"] = np.triu(np.ones((P, P), np.float32))
    A["sel"] = np.broadcast_to(np.eye(8, dtype=np.float32)[:, :, None], (8, 8, P))
    A["m_nw"] = rows(I["L0_attn_norm_w"])
    A["m_rw1"] = ktile(I["L0_attn_r_w1"].T)
    A["m_rw2"] = I["L0_attn_r_w2"].T
    A["m_rb1"] = I["L0_attn_r_b1"][:, None]
    A["m_rb2"] = rows(I["L0_attn_r_b2"])
    cw, cb = I["L0_attn_conv_w"], I["L0_attn_conv_b"]
    A["m_cwx"] = ktile(cw[0:512])
    A["m_cbx"] = cols(cb[0:512])
    A["m_cwbc"] = cw[512:].reshape(2, 64, 4).transpose(1, 0, 2)
    A["m_cbbc"] = cb[512:].reshape(2, 64).T
    A["m_hp"] = np.stack([I["L0_attn_dt_bias"], I["L0_attn_A_log"]], 1)
    A["m_D"] = cols(np.repeat(I["L0_attn_D_param"], 64))
    A["m_gw"] = cols(I["L0_attn_gnorm_w"])
    A["m_win"] = ktile(I["L0_attn_in_proj_w"].T)
    A["m_wout"] = ktile(I["L0_attn_out_proj_w"].T)
    A["query_tail"] = np.array([[0], [0], [1]], np.float32)
    A["ctxT"] = I["ctx_1024"].transpose(2, 0, 1).reshape(KD, P, -1).transpose(1, 0, 2)
    A["mask"] = I["mask_Bx1x1xS2_if1"].reshape(B, -1)
    for n in ("q", "k", "v", "o"):
        A["c_w" + n] = ktile(I["L0_xattn_w" + n].T)
    for n in ("c_wq", "c_wk"):
        A[n] = dim_major(A[n])
    A["c_bq"], A["c_bk"] = cols(dim_major(I["L0_xattn_bq"])), cols(dim_major(I["L0_xattn_bk"]))
    A["c_bv"], A["c_bo"] = rows(I["L0_xattn_bv"]), rows(I["L0_xattn_bo"])
    A["tris"] = np.triu(np.ones((P, P), np.float32), 1)
    A["iota"] = rows(np.arange(16, dtype=np.float32))
    A["iotaP"] = rows(P * np.arange(8, dtype=np.float32))
    A["e_wr"], A["e_br"] = ktile(I["L0_ffn_w_router"]), rows(I["L0_ffn_b_router"])
    A["e_w1"] = I["L0_ffn_w1"].reshape(8, KD, P, -1).transpose(0, 2, 1, 3)
    A["e_b1"] = I["L0_ffn_b1"].reshape(1, -1)
    A["e_w2"] = I["L0_ffn_w2"].reshape(8, 4, P, D).transpose(0, 2, 1, 3)
    A["e_b2"] = rows(I["L0_ffn_b2"].reshape(-1))
    A["g_wr"] = ktile(I["L1_ffn_Wr"].T)
    A["g_w1"] = I["L1_ffn_W1"].reshape(8, KD, P, -1).transpose(0, 2, 1, 3)
    A["g_b1"] = I["L1_ffn_b1"].reshape(1, -1)
    A["g_w2"] = ktile(I["L1_ffn_Wo"])
    A["g_b2"] = rows(I["L1_ffn_bo"])
    A["g_gb"] = np.broadcast_to(np.stack([I["L1_ffn_gamma"], I["L1_ffn_beta"]]), (P, 2, D))
    A["s_wq"] = I["L1_attn_proj_q"].reshape(8, KD, P, P).transpose(2, 0, 1, 3)
    A["s_wk"], A["s_wv"] = ktile(I["L1_attn_proj_k"]), ktile(I["L1_attn_proj_v"])
    A["s_wo"] = I["L1_attn_proj_o"].transpose(2, 0, 1)
    A["h_wq"], A["h_wc"] = ktile(I["L1_xattn_Wq"].T), ktile(I["L1_xattn_Wc"].T)
    A["h_wq"] = dim_major(A["h_wq"])
    A["h_ctxT"] = dim_major(I["ctx_1024"]).transpose(2, 0, 1).reshape(KD, P, -1).transpose(1, 0, 2)
    A["h_wkv"] = ktile(dim_major(I["L1_xattn_Wkv"]).T)
    A["h_ktc"] = np.array([[1], [1], [0]], np.float32)
    A["c_ktc"] = np.array([[0, 1], [0, 1], [MASKED, -MASKED]], np.float32)
    return {k: np.ascontiguousarray(v) for k, v in A.items()}


STAGES = [mamba_stage, cross_stage, experts0_stage, shared_kv_stage, hard_cross_stage, experts1_stage]


def zero_slots(sp, sh):
    for xs in sh.xs:
        sp.dma_start(xs.rearrange("(t p) c -> p t c", p=P),
                     sh.zero[:, :].unsqueeze(1).to_broadcast([P, SLOT_TILES, D])).then_inc(sh.zeroed, 16)


def constants(nc, ctx, sh, A):
    zero_set = ctx.enter_context(nc.semaphore("zero_set"))
    const_in, identb_made = ctx.enter_context(nc.semaphore("const_in")), ctx.enter_context(nc.semaphore("identb_made"))
    with nc.Block() as block:
        @block.sync
        def _(sp):
            sp.dma_start(sh.X[:, :, :], A["x"]).then_inc(const_in, 16)
            sp.dma_start(sh.ident[:, :], A["ident"]).then_inc(const_in, 16)
            sp.dma_start(sh.query_tail[:, :], A["query_tail"]).then_inc(const_in, 16)
            sp.wait_ge(const_in, 48)


        @block.gpsimd
        def _(pool):
            pool.memset(sh.mhalf[:, :], -0.5)
            pool.memset(sh.zero[:, :], 0.0).then_inc(zero_set, 1)
            pool.wait_ge(zero_set, 1)

        @block.vector
        def _(dve):
            dve.wait_ge(const_in, 48)
            dve.tensor_copy(sh.identb[:, :], sh.ident[:, :]).then_inc(identb_made, 1)
            dve.wait_ge(identb_made, 1)


def decoder(nc, A, out, stages=None):
    ctx = ExitStack()
    with ctx:
        sh = Shared()
        sh.PS = ctx.enter_context(nc.psum_tensor("PS", [P, 8, BANK], F32))
        sh.X = ctx.enter_context(nc.sbuf_tensor("X", [P, NT, D], F32))
        sh.XN = ctx.enter_context(nc.sbuf_tensor("XN", [P, NT, D], F32))
        sh.XT = ctx.enter_context(nc.sbuf_tensor("XT", [P, KD, T], F32))
        sh.mhalf = ctx.enter_context(nc.sbuf_tensor("mhalf", [P, NT], F32))
        sh.st6, sh.mv, sh.rstd = (ctx.enter_context(nc.sbuf_tensor(n, [P, NT] + more, F32))
                                  for n, more in (("st6", [6]), ("mv", [2]), ("rstd", [])))
        sh.zero = ctx.enter_context(nc.sbuf_tensor("zero", [P, D], F32))
        sh.ident = ctx.enter_context(nc.sbuf_tensor("ident", [P, P], F32))
        sh.identb = ctx.enter_context(nc.sbuf_tensor("identb", [P, P], BF16))
        sh.query_tail = ctx.enter_context(nc.sbuf_tensor("query_tail", [TAIL_ROWS, 1], F32))
        sh.area = ctx.enter_context(nc.sbuf_tensor("area", [P, AREA], F32))
        sh.weights = [ExpertWeights(nc, ctx, sh, A, layer) for layer in range(2)]
        sh.xs = [nc.dram_tensor(f"xs{layer}", [SLOTS, D], F32, kind="Internal").ap() for layer in range(2)]
        sh.zeroed, sh.out_stored = (ctx.enter_context(nc.semaphore(n)) for n in ("zeroed", "out_stored"))
        sh.out = out
        sh.held = ctx.enter_context(ExitStack())
        constants(nc, ctx, sh, A)
        for s in (STAGES if stages is None else stages):
            s(nc, own := StageSemaphores(nc), sh, A)
            own.clear()


def kernel(**inputs):
    import numpy as _np
    import concourse.bacc as _bacc
    from concourse import mybir as _mybir
    from concourse.bass_utils import run_bass_kernel_spmd as _run

    nc = _bacc.Bacc("TRN2", target_bir_lowering=False, num_devices=1)
    arrays = layouts(_np, {k: _np.asarray(v) for k, v in inputs.items()})
    A = {k: nc.dram_tensor("in_" + k, v.shape, _mybir.dt.from_np(v.dtype), kind="ExternalInput").ap()
         for k, v in arrays.items()}
    out = nc.dram_tensor("out_x", (P, NT, D), F32, kind="ExternalOutput").ap()
    decoder(nc, A, out)
    r = _run(nc, [{"in_" + k: v for k, v in arrays.items()}], core_ids=[0])
    y = r.results[0]["out_x"]
    return y.transpose(1, 0, 2).reshape(B, S, D)
```
